# Optimizing a Trainium2 kernel written in Bass

```python
import numpy as np
import jax
import jax.numpy as jnp

def _softmax(x, axis=-1):
    return jax.nn.softmax(x, axis=axis)

def _gelu(x):
    return jax.nn.gelu(x, approximate=True)

def _silu(x):
    return jax.nn.silu(x)

def _sigmoid(x):
    return jax.nn.sigmoid(x)

def _layernorm(x, axis=-1, eps=1e-05):
    m = jnp.mean(x, axis=axis, keepdims=True)
    v = jnp.var(x, axis=axis, keepdims=True)
    return (x - m) / jnp.sqrt(v + eps)

def _scatter_add(tgt, idx, src, axis=0):
    return tgt.at[idx].add(src)

def _segment_sum(src, seg, n):
    return jax.ops.segment_sum(src, seg, n)
kernel_name = 'mk_xattn_seq_d2_seqx_r4_0e3ea5'

def setup_inputs(seed: int=0):
    np.random.seed(seed)
    _w = jnp.asarray

    def _rec_inputs():
        import jax
        import jax.numpy as jnp
        _rk = jax.random.key(seed)
        x = 7.22e-05 + 1 * jax.random.normal(jax.random.fold_in(_rk, 1), (8, 256, 512), jnp.float32)
        _lenS = 256 - jax.random.randint(jax.random.fold_in(_rk, 7), (8,), 0, max(1, 256 // 4) + 1, jnp.int32)
        _lenS2 = 256 - jax.random.randint(jax.random.fold_in(_rk, 8), (8,), 0, max(1, 256 // 4) + 1, jnp.int32)
        _ctx_2048P = jax.random.normal(jax.random.fold_in(_rk, 11), (8, 16, 512), jnp.float32)
        _ctx_2048c = jax.random.dirichlet(jax.random.fold_in(_rk, 511), 0.3 * jnp.ones((16,), jnp.float32), (8, 256))
        _ctx_2048t = jnp.einsum('bsk,bkd->bsd', _ctx_2048c, _ctx_2048P)
        _ctx_2048t = _ctx_2048t * jax.lax.rsqrt(jnp.mean(jnp.square(_ctx_2048t)) + 1e-12) * 0.953939
        ctx_2048 = 3.03215e-05 + 0.0999827 * (_ctx_2048t + 0.3 * jax.random.normal(jax.random.fold_in(_rk, 611), (8, 256, 512), jnp.float32))
        _validS = jnp.arange(256)[None, :] < _lenS[:, None]
        _validS2 = jnp.arange(256)[None, :] < _lenS2[:, None]
        _causal = jnp.tril(jnp.ones((256, 256), dtype=bool))
        mask_1x1xSxS2_fc1 = jnp.where(jnp.broadcast_to(_validS2[0:1, None, None, :], (1, 1, 256, 256)), 1.0, 0.0).astype(jnp.float32)
        mask_Bx1xSxS2_ff1 = jnp.where(jnp.ones((8, 1, 256, 256), dtype=bool), 1.0, 0.0).astype(jnp.float32)
        return (x, ctx_2048, mask_1x1xSxS2_fc1, mask_Bx1xSxS2_ff1)
    x, ctx_2048, mask_1x1xSxS2_fc1, mask_Bx1xSxS2_ff1 = _rec_inputs()

    def _L0_xattn_setup():
        import jax, jax.numpy as jnp
        import numpy as np
        N_HEAD = 32
        EPS = 1e-05

        def _ln(x, w, b):
            m = jnp.mean(x, axis=-1, keepdims=True)
            v = jnp.mean((x - m) ** 2, axis=-1, keepdims=True)
            return (x - m) * jax.lax.rsqrt(v + EPS) * w + b

        def _forward(x, state, i, ln1_w, ln1_b, ln2_w, ln2_b, maa_x, maa_w, maa_k, maa_v, maa_r, maa_g, maa_w1, maa_w2, time_decay, decay_w1, decay_w2, faaaa, Wr, Wk, Wv, Wg, Wo, gn_w, gn_b, fmaa_k, fmaa_r, fWk, fWr, fWv):
            B, L, C = x.shape
            H = N_HEAD
            S = C // H
            i0 = (2 + S) * i
            xa = _ln(x, ln1_w, ln1_b)
            sx = jnp.concatenate([state[:, i0 + 1][:, None], xa[:, :-1]], axis=1) - xa
            xxx = xa + sx * maa_x
            t = jnp.tanh(xxx @ maa_w1).reshape(B, L, 5, -1)
            m = jnp.einsum('blfd,fdc->blfc', t, maa_w2)
            mw, mk, mv, mr, mg = (m[:, :, j] for j in range(5))
            xw = xa + sx * (maa_w + mw)
            xk = xa + sx * (maa_k + mk)
            xv = xa + sx * (maa_v + mv)
            xr = xa + sx * (maa_r + mr)
            xg = xa + sx * (maa_g + mg)
            w = time_decay + jnp.tanh(xw @ decay_w1) @ decay_w2
            w = jnp.exp(-jnp.exp(w)).reshape(B, L, H, S)
            r = (xr @ Wr.T).reshape(B, L, H, S)
            k = (xk @ Wk.T).reshape(B, L, H, S)
            v = (xv @ Wv.T).reshape(B, L, H, S)
            g = jax.nn.silu(xg @ Wg.T)
            s0 = state[:, i0 + 2:i0 + 2 + S].reshape(B, H, S, S)

            def step(s, inp):
                k_l, v_l, w_l, r_l = inp
                a = k_l[..., :, None] * v_l[..., None, :]
                out = jnp.einsum('bhs,bhst->bht', r_l, faaaa * a + s)
                s_new = a + w_l[..., None] * s
                return (s_new, out)
            seq = tuple((z.transpose(1, 0, 2, 3) for z in (k, v, w, r)))
            _, outs = jax.lax.scan(step, s0, seq)
            y = outs.transpose(1, 0, 2, 3)
            gm = jnp.mean(y, axis=-1, keepdims=True)
            gv = jnp.mean((y - gm) ** 2, axis=-1, keepdims=True)
            y = ((y - gm) * jax.lax.rsqrt(gv + EPS)).reshape(B, L, C) * gn_w + gn_b
            x = x + y * g @ Wo.T
            xc = _ln(x, ln2_w, ln2_b)
            sxc = jnp.concatenate([state[:, i0][:, None], xc[:, :-1]], axis=1) - xc
            xk2 = xc + sxc * fmaa_k
            xr2 = xc + sxc * fmaa_r
            rr = jax.nn.sigmoid(xr2 @ fWr.T)
            kk = jnp.square(jax.nn.relu(xk2 @ fWk.T))
            x = x + rr * (kk @ fWv.T)
            return x
        key = jax.random.key(seed)
        B, L, C, H = (8, 128, 512, N_HEAD)
        S = C // H
        DM, DD = (32, 64)
        ks = jax.random.split(key, 32)
        n = lambda k, shp, s=1.0: jax.random.normal(k, shp, dtype=jnp.float32) * s
        u = lambda k, shp: jax.random.uniform(k, shp, dtype=jnp.float32)
        inp = {'x': n(ks[0], (B, L, C)), 'state': n(ks[1], (B, 2 + S, C), 0.1), 'i': 0, 'ln1_w': jnp.ones((C,), jnp.float32), 'ln1_b': jnp.zeros((C,), jnp.float32), 'ln2_w': jnp.ones((C,), jnp.float32), 'ln2_b': jnp.zeros((C,), jnp.float32), 'maa_x': u(ks[2], (C,)), 'maa_w': u(ks[3], (C,)), 'maa_k': u(ks[4], (C,)), 'maa_v': u(ks[5], (C,)), 'maa_r': u(ks[6], (C,)), 'maa_g': u(ks[7], (C,)), 'maa_w1': n(ks[8], (C, 5 * DM), 0.02), 'maa_w2': n(ks[9], (5, DM, C), 0.02), 'time_decay': n(ks[10], (C,), 0.5), 'decay_w1': n(ks[11], (C, DD), 0.02), 'decay_w2': n(ks[12], (DD, C), 0.02), 'faaaa': n(ks[13], (H, S, 1), 0.1), 'Wr': n(ks[14], (C, C), 0.02), 'Wk': n(ks[15], (C, C), 0.02), 'Wv': n(ks[16], (C, C), 0.02), 'Wg': n(ks[17], (C, C), 0.02), 'Wo': n(ks[18], (C, C), 0.02), 'gn_w': jnp.ones((C,), jnp.float32), 'gn_b': jnp.zeros((C,), jnp.float32), 'fmaa_k': u(ks[19], (C,)), 'fmaa_r': u(ks[20], (C,)), 'fWk': n(ks[21], (C, C), 0.02), 'fWr': n(ks[22], (C, C), 0.02), 'fWv': n(ks[23], (C, C), 0.02)}
        return inp
    _L0_xattn_all = _L0_xattn_setup()
    _L0_xattn_in = {k: v for k, v in _L0_xattn_all.items() if k in ('ln1_w', 'ln1_b', 'ln2_w', 'ln2_b', 'maa_x', 'maa_w', 'maa_k', 'maa_v', 'maa_r', 'maa_g', 'maa_w1', 'maa_w2', 'time_decay', 'decay_w1', 'decay_w2', 'faaaa', 'Wr', 'Wk', 'Wv', 'Wg', 'Wo', 'gn_w', 'gn_b', 'fmaa_k', 'fmaa_r', 'fWk', 'fWr', 'fWv')}
    del _L0_xattn_all

    def _L1_xattn_setup():
        import jax, jax.numpy as jnp
        import numpy as np
        H = 512
        NH = 16
        HD = H // NH
        EPS = 1e-05

        def gelu(x):
            return 0.5 * x * (1.0 + jnp.tanh(0.7978845608028654 * x * (1.0 + 0.044715 * x * x)))

        def layernorm(x, scale, bias):
            m = jnp.mean(x, axis=-1, keepdims=True)
            v = jnp.mean(jnp.square(x - m), axis=-1, keepdims=True)
            return (x - m) * jax.lax.rsqrt(v + EPS) * scale + bias

        def split_heads(x):
            b, s, _ = x.shape
            return x.reshape(b, s, NH, HD).transpose(0, 2, 1, 3)

        def merge_heads(x):
            b, nh, s, hd = x.shape
            return x.transpose(0, 2, 1, 3).reshape(b, s, nh * hd)

        def attention(q, k, v, mask):
            scores = jnp.einsum('bhqd,bhkd->bhqk', q, k) / jnp.sqrt(jnp.float32(HD))
            scores = scores * mask - 10000.0 * (1.0 - mask)
            probs = jax.nn.softmax(scores, axis=-1)
            return jnp.einsum('bhqk,bhkd->bhqd', probs, v)
        key = jax.random.key(seed)
        ks = jax.random.split(key, 16)
        b, s, t = (2, 256, 256)
        w = lambda k, i, o: jax.random.normal(k, (i, o), jnp.float32) * 0.02
        inp = {'hidden_states': jax.random.normal(ks[0], (b, s, H), jnp.float32), 'encoder_states': jax.random.normal(ks[1], (b, t, H), jnp.float32), 'ltor_mask': jnp.tril(jnp.ones((1, 1, s, s), jnp.float32)), 'cross_mask': jnp.ones((b, 1, s, t), jnp.float32), 'ln1_s': jnp.ones((H,), jnp.float32), 'ln1_b': jnp.zeros((H,), jnp.float32), 'w_qkv': w(ks[2], H, 3 * H), 'b_qkv': jnp.zeros((3 * H,), jnp.float32), 'w_ao': w(ks[3], H, H), 'b_ao': jnp.zeros((H,), jnp.float32), 'ln2_s': jnp.ones((H,), jnp.float32), 'ln2_b': jnp.zeros((H,), jnp.float32), 'w_q': w(ks[4], H, H), 'b_q': jnp.zeros((H,), jnp.float32), 'w_kv': w(ks[5], H, 2 * H), 'b_kv': jnp.zeros((2 * H,), jnp.float32), 'w_co': w(ks[6], H, H), 'b_co': jnp.zeros((H,), jnp.float32), 'ln3_s': jnp.ones((H,), jnp.float32), 'ln3_b': jnp.zeros((H,), jnp.float32), 'w1': w(ks[7], H, 4 * H), 'b1': jnp.zeros((4 * H,), jnp.float32), 'w2': w(ks[8], 4 * H, H), 'b2': jnp.zeros((H,), jnp.float32)}
        return inp
    _L1_xattn_all = _L1_xattn_setup()
    _L1_xattn_in = {k: v for k, v in _L1_xattn_all.items() if k in ('ln1_s', 'ln1_b', 'w_qkv', 'b_qkv', 'w_ao', 'b_ao', 'ln2_s', 'ln2_b', 'w_q', 'b_q', 'w_kv', 'b_kv', 'w_co', 'b_co', 'ln3_s', 'ln3_b', 'w1', 'b1', 'w2', 'b2')}
    del _L1_xattn_all
    return {'x': x, 'ctx_2048': ctx_2048, 'mask_1x1xSxS2_fc1': mask_1x1xSxS2_fc1, 'mask_Bx1xSxS2_ff1': mask_Bx1xSxS2_ff1, 'L0_xattn_ln1_w': _L0_xattn_in['ln1_w'], 'L0_xattn_ln1_b': _L0_xattn_in['ln1_b'], 'L0_xattn_ln2_w': _L0_xattn_in['ln2_w'], 'L0_xattn_ln2_b': _L0_xattn_in['ln2_b'], 'L0_xattn_maa_x': _L0_xattn_in['maa_x'], 'L0_xattn_maa_w': _L0_xattn_in['maa_w'], 'L0_xattn_maa_k': _L0_xattn_in['maa_k'], 'L0_xattn_maa_v': _L0_xattn_in['maa_v'], 'L0_xattn_maa_r': _L0_xattn_in['maa_r'], 'L0_xattn_maa_g': _L0_xattn_in['maa_g'], 'L0_xattn_maa_w1': _L0_xattn_in['maa_w1'], 'L0_xattn_maa_w2': _L0_xattn_in['maa_w2'], 'L0_xattn_time_decay': _L0_xattn_in['time_decay'], 'L0_xattn_decay_w1': _L0_xattn_in['decay_w1'], 'L0_xattn_decay_w2': _L0_xattn_in['decay_w2'], 'L0_xattn_faaaa': _L0_xattn_in['faaaa'], 'L0_xattn_Wr': _L0_xattn_in['Wr'], 'L0_xattn_Wk': _L0_xattn_in['Wk'], 'L0_xattn_Wv': _L0_xattn_in['Wv'], 'L0_xattn_Wg': _L0_xattn_in['Wg'], 'L0_xattn_Wo': _L0_xattn_in['Wo'], 'L0_xattn_gn_w': _L0_xattn_in['gn_w'], 'L0_xattn_gn_b': _L0_xattn_in['gn_b'], 'L0_xattn_fmaa_k': _L0_xattn_in['fmaa_k'], 'L0_xattn_fmaa_r': _L0_xattn_in['fmaa_r'], 'L0_xattn_fWk': _L0_xattn_in['fWk'], 'L0_xattn_fWr': _L0_xattn_in['fWr'], 'L0_xattn_fWv': _L0_xattn_in['fWv'], 'L1_xattn_ln1_s': _L1_xattn_in['ln1_s'], 'L1_xattn_ln1_b': _L1_xattn_in['ln1_b'], 'L1_xattn_w_qkv': _L1_xattn_in['w_qkv'], 'L1_xattn_b_qkv': _L1_xattn_in['b_qkv'], 'L1_xattn_w_ao': _L1_xattn_in['w_ao'], 'L1_xattn_b_ao': _L1_xattn_in['b_ao'], 'L1_xattn_ln2_s': _L1_xattn_in['ln2_s'], 'L1_xattn_ln2_b': _L1_xattn_in['ln2_b'], 'L1_xattn_w_q': _L1_xattn_in['w_q'], 'L1_xattn_b_q': _L1_xattn_in['b_q'], 'L1_xattn_w_kv': _L1_xattn_in['w_kv'], 'L1_xattn_b_kv': _L1_xattn_in['b_kv'], 'L1_xattn_w_co': _L1_xattn_in['w_co'], 'L1_xattn_b_co': _L1_xattn_in['b_co'], 'L1_xattn_ln3_s': _L1_xattn_in['ln3_s'], 'L1_xattn_ln3_b': _L1_xattn_in['ln3_b'], 'L1_xattn_w1': _L1_xattn_in['w1'], 'L1_xattn_b1': _L1_xattn_in['b1'], 'L1_xattn_w2': _L1_xattn_in['w2'], 'L1_xattn_b2': _L1_xattn_in['b2']}

def reference(x, ctx_2048, mask_1x1xSxS2_fc1, mask_Bx1xSxS2_ff1, L0_xattn_ln1_w, L0_xattn_ln1_b, L0_xattn_ln2_w, L0_xattn_ln2_b, L0_xattn_maa_x, L0_xattn_maa_w, L0_xattn_maa_k, L0_xattn_maa_v, L0_xattn_maa_r, L0_xattn_maa_g, L0_xattn_maa_w1, L0_xattn_maa_w2, L0_xattn_time_decay, L0_xattn_decay_w1, L0_xattn_decay_w2, L0_xattn_faaaa, L0_xattn_Wr, L0_xattn_Wk, L0_xattn_Wv, L0_xattn_Wg, L0_xattn_Wo, L0_xattn_gn_w, L0_xattn_gn_b, L0_xattn_fmaa_k, L0_xattn_fmaa_r, L0_xattn_fWk, L0_xattn_fWr, L0_xattn_fWv, L1_xattn_ln1_s, L1_xattn_ln1_b, L1_xattn_w_qkv, L1_xattn_b_qkv, L1_xattn_w_ao, L1_xattn_b_ao, L1_xattn_ln2_s, L1_xattn_ln2_b, L1_xattn_w_q, L1_xattn_b_q, L1_xattn_w_kv, L1_xattn_b_kv, L1_xattn_w_co, L1_xattn_b_co, L1_xattn_ln3_s, L1_xattn_ln3_b, L1_xattn_w1, L1_xattn_b1, L1_xattn_w2, L1_xattn_b2):
    import jax
    import jax.numpy as jnp

    def _L0_xattn_ref(x, state, i, ln1_w, ln1_b, ln2_w, ln2_b, maa_x, maa_w, maa_k, maa_v, maa_r, maa_g, maa_w1, maa_w2, time_decay, decay_w1, decay_w2, faaaa, Wr, Wk, Wv, Wg, Wo, gn_w, gn_b, fmaa_k, fmaa_r, fWk, fWr, fWv):
        import jax, jax.numpy as jnp
        import numpy as np
        N_HEAD = 32
        EPS = 1e-05

        def _ln(x, w, b):
            m = jnp.mean(x, axis=-1, keepdims=True)
            v = jnp.mean((x - m) ** 2, axis=-1, keepdims=True)
            return (x - m) * jax.lax.rsqrt(v + EPS) * w + b

        def _forward(x, state, i, ln1_w, ln1_b, ln2_w, ln2_b, maa_x, maa_w, maa_k, maa_v, maa_r, maa_g, maa_w1, maa_w2, time_decay, decay_w1, decay_w2, faaaa, Wr, Wk, Wv, Wg, Wo, gn_w, gn_b, fmaa_k, fmaa_r, fWk, fWr, fWv):
            B, L, C = x.shape
            H = N_HEAD
            S = C // H
            i0 = (2 + S) * i
            xa = _ln(x, ln1_w, ln1_b)
            sx = jnp.concatenate([state[:, i0 + 1][:, None], xa[:, :-1]], axis=1) - xa
            xxx = xa + sx * maa_x
            t = jnp.tanh(xxx @ maa_w1).reshape(B, L, 5, -1)
            m = jnp.einsum('blfd,fdc->blfc', t, maa_w2)
            mw, mk, mv, mr, mg = (m[:, :, j] for j in range(5))
            xw = xa + sx * (maa_w + mw)
            xk = xa + sx * (maa_k + mk)
            xv = xa + sx * (maa_v + mv)
            xr = xa + sx * (maa_r + mr)
            xg = xa + sx * (maa_g + mg)
            w = time_decay + jnp.tanh(xw @ decay_w1) @ decay_w2
            w = jnp.exp(-jnp.exp(w)).reshape(B, L, H, S)
            r = (xr @ Wr.T).reshape(B, L, H, S)
            k = (xk @ Wk.T).reshape(B, L, H, S)
            v = (xv @ Wv.T).reshape(B, L, H, S)
            g = jax.nn.silu(xg @ Wg.T)
            s0 = state[:, i0 + 2:i0 + 2 + S].reshape(B, H, S, S)

            def step(s, inp):
                k_l, v_l, w_l, r_l = inp
                a = k_l[..., :, None] * v_l[..., None, :]
                out = jnp.einsum('bhs,bhst->bht', r_l, faaaa * a + s)
                s_new = a + w_l[..., None] * s
                return (s_new, out)
            seq = tuple((z.transpose(1, 0, 2, 3) for z in (k, v, w, r)))
            _, outs = jax.lax.scan(step, s0, seq)
            y = outs.transpose(1, 0, 2, 3)
            gm = jnp.mean(y, axis=-1, keepdims=True)
            gv = jnp.mean((y - gm) ** 2, axis=-1, keepdims=True)
            y = ((y - gm) * jax.lax.rsqrt(gv + EPS)).reshape(B, L, C) * gn_w + gn_b
            x = x + y * g @ Wo.T
            xc = _ln(x, ln2_w, ln2_b)
            sxc = jnp.concatenate([state[:, i0][:, None], xc[:, :-1]], axis=1) - xc
            xk2 = xc + sxc * fmaa_k
            xr2 = xc + sxc * fmaa_r
            rr = jax.nn.sigmoid(xr2 @ fWr.T)
            kk = jnp.square(jax.nn.relu(xk2 @ fWk.T))
            x = x + rr * (kk @ fWv.T)
            return x
        return _forward(x, state, i, ln1_w, ln1_b, ln2_w, ln2_b, maa_x, maa_w, maa_k, maa_v, maa_r, maa_g, maa_w1, maa_w2, time_decay, decay_w1, decay_w2, faaaa, Wr, Wk, Wv, Wg, Wo, gn_w, gn_b, fmaa_k, fmaa_r, fWk, fWr, fWv)

    def _L1_xattn_ref(hidden_states, encoder_states, ltor_mask, cross_mask, ln1_s, ln1_b, w_qkv, b_qkv, w_ao, b_ao, ln2_s, ln2_b, w_q, b_q, w_kv, b_kv, w_co, b_co, ln3_s, ln3_b, w1, b1, w2, b2):
        import jax, jax.numpy as jnp
        import numpy as np
        H = 512
        NH = 16
        HD = H // NH
        EPS = 1e-05

        def gelu(x):
            return 0.5 * x * (1.0 + jnp.tanh(0.7978845608028654 * x * (1.0 + 0.044715 * x * x)))

        def layernorm(x, scale, bias):
            m = jnp.mean(x, axis=-1, keepdims=True)
            v = jnp.mean(jnp.square(x - m), axis=-1, keepdims=True)
            return (x - m) * jax.lax.rsqrt(v + EPS) * scale + bias

        def split_heads(x):
            b, s, _ = x.shape
            return x.reshape(b, s, NH, HD).transpose(0, 2, 1, 3)

        def merge_heads(x):
            b, nh, s, hd = x.shape
            return x.transpose(0, 2, 1, 3).reshape(b, s, nh * hd)

        def attention(q, k, v, mask):
            scores = jnp.einsum('bhqd,bhkd->bhqk', q, k) / jnp.sqrt(jnp.float32(HD))
            scores = scores * mask - 10000.0 * (1.0 - mask)
            probs = jax.nn.softmax(scores, axis=-1)
            return jnp.einsum('bhqk,bhkd->bhqd', probs, v)
        ln_out = layernorm(hidden_states, ln1_s, ln1_b)
        qkv = ln_out @ w_qkv + b_qkv
        q, k, v = jnp.split(qkv, 3, axis=-1)
        ctx = merge_heads(attention(split_heads(q), split_heads(k), split_heads(v), ltor_mask))
        attn_out = ctx @ w_ao + b_ao
        x = hidden_states + attn_out
        ln_out = layernorm(x, ln2_s, ln2_b)
        q = ln_out @ w_q + b_q
        kv = encoder_states @ w_kv + b_kv
        k, v = jnp.split(kv, 2, axis=-1)
        ctx = merge_heads(attention(split_heads(q), split_heads(k), split_heads(v), cross_mask))
        cross_out = ctx @ w_co + b_co
        x = x + cross_out
        ln_out = layernorm(x, ln3_s, ln3_b)
        mlp_out = gelu(ln_out @ w1 + b1) @ w2 + b2
        return x + mlp_out
    x = _L0_xattn_ref(x, ctx_2048, 0, L0_xattn_ln1_w, L0_xattn_ln1_b, L0_xattn_ln2_w, L0_xattn_ln2_b, L0_xattn_maa_x, L0_xattn_maa_w, L0_xattn_maa_k, L0_xattn_maa_v, L0_xattn_maa_r, L0_xattn_maa_g, L0_xattn_maa_w1, L0_xattn_maa_w2, L0_xattn_time_decay, L0_xattn_decay_w1, L0_xattn_decay_w2, L0_xattn_faaaa, L0_xattn_Wr, L0_xattn_Wk, L0_xattn_Wv, L0_xattn_Wg, L0_xattn_Wo, L0_xattn_gn_w, L0_xattn_gn_b, L0_xattn_fmaa_k, L0_xattn_fmaa_r, L0_xattn_fWk, L0_xattn_fWr, L0_xattn_fWv)
    x = _L1_xattn_ref(x, ctx_2048, mask_1x1xSxS2_fc1, mask_Bx1xSxS2_ff1, L1_xattn_ln1_s, L1_xattn_ln1_b, L1_xattn_w_qkv, L1_xattn_b_qkv, L1_xattn_w_ao, L1_xattn_b_ao, L1_xattn_ln2_s, L1_xattn_ln2_b, L1_xattn_w_q, L1_xattn_b_q, L1_xattn_w_kv, L1_xattn_b_kv, L1_xattn_w_co, L1_xattn_b_co, L1_xattn_ln3_s, L1_xattn_ln3_b, L1_xattn_w1, L1_xattn_b1, L1_xattn_w2, L1_xattn_b2)
    return x

_drawn_inputs = setup_inputs


def setup_inputs(seed=0):
    import zlib

    import numpy as np

    out = dict(_drawn_inputs(seed))
    spreads = {'L0_xattn_ln1_w': (1.0, 0.2),
     'L0_xattn_ln1_b': (0.0, 0.269),
     'L0_xattn_ln2_w': (1.0, 0.6),
     'L0_xattn_ln2_b': (0.0, 0.8),
     'L0_xattn_gn_w': (1.0, 0.6),
     'L0_xattn_gn_b': (0.0, 0.8),
     'L1_xattn_ln1_s': (1.0, 0.6),
     'L1_xattn_ln1_b': (0.0, 0.392),
     'L1_xattn_b_qkv': (0.0, 0.1),
     'L1_xattn_b_ao': (0.0, 0.1),
     'L1_xattn_ln2_s': (1.0, 0.6),
     'L1_xattn_ln2_b': (0.0, 0.8),
     'L1_xattn_b_q': (0.0, 0.8),
     'L1_xattn_b_kv': (0.0, 0.1),
     'L1_xattn_b_co': (0.0, 0.1),
     'L1_xattn_ln3_s': (1.0, 0.2),
     'L1_xattn_ln3_b': (0.0, 0.348),
     'L1_xattn_b1': (0.0, 0.1),
     'L1_xattn_b2': (0.0, 0.1)}
    factors = {'ctx_2048': 5.283,
     'L0_xattn_maa_x': 6.693,
     'L0_xattn_maa_w': 8.0,
     'L0_xattn_maa_w1': 3.475,
     'L0_xattn_maa_w2': 3.487,
     'L0_xattn_decay_w1': 8.0,
     'L0_xattn_decay_w2': 8.0,
     'L0_xattn_faaaa': 3.796,
     'L0_xattn_fmaa_r': 8.0,
     'L0_xattn_fWr': 7.638,
     'L1_xattn_w_q': 8.0,
     'L1_xattn_w_kv': 5.686}
    for name, (base, spread) in spreads.items():
        noise = np.random.default_rng([zlib.crc32(name.encode()), seed]).standard_normal(out[name].shape)
        drawn = base * np.exp(spread * noise) if base else spread * noise
        out[name] = jnp.asarray(drawn.astype(out[name].dtype))
    for name, factor in factors.items():
        out[name] = (out[name] * factor).astype(out[name].dtype)
    return out
```

```python
from contextlib import ExitStack

import concourse.bass as bass
from concourse import mybir

F32 = mybir.dt.float32
ALU = mybir.AluOpType
ACT = mybir.ActivationFunctionType
AX = mybir.AxisListType

P = 128
B = 8
L = 256
C = 512
CT = C // P
TT = L // P
S = 16
HT = P // S
NH = 16
HD = C // NH
HC = P // HD
DM = 32
DD = 64
FF = 4 * C
EPS = 1e-5
UNITS = 8
UW = S // 2
RING = 4

TIME_VECS = ["ln1_w", "ln1_b", "maa_x", "maa_w", "maa_k", "maa_v", "maa_r", "maa_g",
             "time_decay", "faaaa", "gn_w", "gn_b"]
CHAN_VECS = ["ln2_w", "ln2_b", "fmaa_k", "fmaa_r"]


class Count:

    def __init__(self, sem, per, ahead=0):
        self.sem, self.per, self.ahead = sem, per, ahead

    def at(self, n, k):
        return (n + self.ahead) * self.per + k

    def all(self, n):
        return (n + self.ahead + 1) * self.per


def counter(held, nc, phase):
    def make(name, per, ahead=0):
        held.append(nc.alloc_semaphore(name=f"{phase}_{name}"))
        return Count(held[-1], per, ahead)
    return make


def end_phase(nc, held):
    nc.clear_and_free_semaphores(held)
    nc.all_engine_barrier()
    held.clear()


def grant(eng, counts):
    for c in counts:
        if c.ahead:
            eng.sem_inc(c.sem, c.ahead * c.per)


def over_batches(eng, first, step, last):
    first()
    with eng.Fori(0, B // 2 - 1) as i:
        for par in range(2):
            step(i * 2 + par, par)
    step(B - 2, 0)
    last(B - 1, 1)


class LayerNorm:

    def __init__(self, ctx, nc, name, sem, x, x_loaded, turned, turned_free, out, out_free, scale, shift, ident, half,
                 passed):
        sb = lambda tile, shape: ctx.enter_context(nc.sbuf_tensor(f"{name}_ln_{tile}", shape, F32))
        self.nc, self.x, self.x_loaded, self.passed = nc, x, x_loaded, passed
        self.turned, self.turned_free, self.out, self.out_free = turned, turned_free, out, out_free
        self.scale, self.shift, self.ident, self.half = scale, shift, ident, half
        self.stats = sb("stats", [P, TT, 6])
        self.moments = sb("moments", [P, TT, 2])
        self.var = sb("var", [P, TT])
        self.rstd = sb("rstd", [P, TT])
        self.normed = sb("normed", [P, TT, C])
        self.stats_done = sem("ln_stats_done", 1, 1)
        self.moments_done = sem("ln_moments_done", 1)
        self.var_done = sem("ln_var_done", 1)
        self.rstd_done = sem("ln_rstd_done", 1)
        self.normed_done = sem("ln_normed_done", 1)
        self.turned_done = sem("ln_turned_done", 1, 1)
        self.out_done = sem("ln_out_done", 1)

    def vector_moments(self, dve, n, par):
        dve.wait_ge(self.x_loaded.sem, self.x_loaded.all(n))
        for t in range(TT):
            r = dve.bn_stats(self.stats[:, t, :], self.x[par][:, t, :])
        r.then_inc(self.stats_done.sem, 1)
        dve.wait_ge(self.stats_done.sem, self.stats_done.all(n))
        dve.sem_inc(self.passed.sem, 1)
        for t in range(TT):
            r = dve.bn_aggr(self.moments[:, t, :], self.stats[:, t, :])
        r.then_inc(self.moments_done.sem, 1)
        dve.wait_ge(self.moments_done.sem, self.moments_done.all(n))
        dve.tensor_scalar(self.var[:, :], self.moments[:, :, 1], EPS, None, ALU.add).then_inc(self.var_done.sem, 1)

    def gpsimd_rstd(self, pool, n):
        pool.wait_ge(self.var_done.sem, self.var_done.all(n))
        pool.tensor_tensor(self.rstd[:, :], self.var[:, :], self.half[:, 0:TT], ALU.pow).then_inc(self.rstd_done.sem, 1)

    def vector_normalise(self, dve, n, par):
        dve.wait_ge(self.rstd_done.sem, self.rstd_done.all(n))
        dve.wait_ge(self.turned_done.sem, self.turned_done.all(n - 1))
        for t in range(TT):
            r = dve.tensor_scalar(self.normed[:, t, :], self.x[par][:, t, :], self.moments[:, t, 0:1],
                                  self.rstd[:, t:t + 1], ALU.subtract, ALU.mult)
        r.then_inc(self.normed_done.sem, 1)

    def tensor_turn(self, pe, n):
        pe.wait_ge(self.normed_done.sem, self.normed_done.all(n))
        self.turned_free(pe, n)
        for t in range(TT):
            for c in range(CT):
                r = pe.transpose(self.turned[:, c, t * P:(t + 1) * P], self.normed[:, t, c * P:(c + 1) * P],
                                 self.ident)
        r.then_inc(self.turned_done.sem, 1)

    def scalar_out(self, act, n, before=None):
        act.wait_ge(self.turned_done.sem, self.turned_done.all(n))
        self.out_free(act, n)
        if before:
            tile, prev = before
            act.activation(tile[:, :, 0], prev[:, n, :], ACT.Copy)
        for c in range(CT):
            r = act.activation(self.out(c), self.turned[:, c, :], ACT.Identity,
                               bias=self.shift[:, c:c + 1], scale=self.scale[:, c:c + 1])
        r.then_inc(self.out_done.sem, 1)


def time_mix(nc, held, x_in, x_out, first_state, v_rows, weights):
    with ExitStack() as ctx:
        def sb(name, shape):
            return ctx.enter_context(nc.sbuf_tensor(f"tm_{name}", shape, F32))

        sem = counter(held, nc, "tm")

        w_proj = {f: sb(f"w_{f}", [P, CT, C]) for f in "vkrgo"}
        w_mix1 = sb("w_mix1", [P, CT, 5 * DM])
        w_mix2 = sb("w_mix2", [P, C])
        w_mix2g = sb("w_mix2g", [DM, C])
        w_dec1 = sb("w_dec1", [P, CT, DD])
        w_dec2 = sb("w_dec2", [DD, C])
        vecs = sb("vecs", [P, len(TIME_VECS), CT])
        pick = sb("pick", [P, S, P])
        fixed = sb("fixed", [P, 3, P])
        head_sum = sb("head_sum", [P, CT, C // S])
        head_out = sb("head_out", [C // S, CT, P])
        prev = sb("prev", [P, B, CT])
        half = sb("half", [P, TT])
        eps = sb("eps", [P, 1])
        vec = {name: vecs[:, i, :] for i, name in enumerate(TIME_VECS)}
        ident, head_ones, centre = fixed[:, 0, :], fixed[:, 1, :], fixed[:, 2, :]

        x = [sb(f"x{i}", [P, TT, C]) for i in range(2)]
        xa = sb("xa", [P, CT, L + 1])
        shift = sb("shift", [P, CT, L])
        mixed = [sb(f"mixed{i}", [P, CT, L]) for i in range(2)]
        mix_act = sb("mix_act", [P, L])
        mix_actg = sb("mix_actg", [DM, L])
        dec_act = sb("dec_act", [DD, L])
        decay_e = sb("decay_e", [P, CT, L])
        wT = [sb(f"wT{i}", [P, CT, L]) for i in range(2)]
        kT = [sb(f"kT{i}", [P, CT, L + 1]) for i in range(2)]
        vT = sb("vT", [P, CT, L + 1])
        rT = [sb(f"rT{i}", [P, CT, L]) for i in range(2)]
        gT = [sb(f"gT{i}", [P, CT, L]) for i in range(2)]
        g_half = sb("g_half", [P, CT, L])
        rkf = sb("rkf", [P, CT, L])
        now = sb("now", [P, CT, L])
        s0 = [sb(f"s0_{i}", [P, CT, S]) for i in range(2)]
        unit = [sb(f"unit{i}", [P, UW, L]) for i in range(RING)]
        y_sb = sb("y_sb", [P, CT, L])
        y_sq = decay_e
        head_rstd = sb("head_rstd", [C // S, L])
        yg = sb("yg", [P, CT, L])
        bank = [ctx.enter_context(nc.psum_tensor(f"tm_ps{i}", [P, CT, L], F32)) for i in range(4)]
        ps_turn, ps_mix, ps_proj, ps_y = bank

        weights_in = sem("weights_in", 0)
        passed = sem("passed", 0)
        x_loaded = sem("x_loaded", 16)
        s0_loaded = sem("s0_loaded", 16)
        v_stored = sem("v_stored", 16, 1)
        unit_loaded = [sem(f"unit{r}_loaded", 16 * UNITS // RING) for r in range(RING)]
        x_stored = sem("x_stored", 16, 2)
        consts_done = sem("consts_done", 0)
        shift_done = sem("shift_done", 1)
        mix_in_done = sem("mix_in_done", 1)
        mix_hidden = sem("mix_hidden", 1)
        mix_acted = sem("mix_acted", 1)
        mix_ps = sem("mix_ps", 5)
        mix_scaled = sem("mix_scaled", 5, 1)
        mix_added = sem("mix_added", 5, 1)
        dec_hidden = sem("dec_hidden", 1)
        dec_acted = sem("dec_acted", 1)
        proj_ps = sem("proj_ps", 5, 1)
        proj_out = sem("proj_out", 5, 1)
        decay_exp = sem("decay_exp", 1)
        g_done = sem("g_done", 1, 1)
        rkf_done = sem("rkf_done", 1)
        now_ps = sem("now_ps", 1, 1)
        now_done = sem("now_done", 1, 1)
        kv_done = sem("kv_done", UNITS, 2)
        scanned = sem("scanned", UNITS)
        read_out = sem("read_out", UNITS, 2)
        unit_summed = sem("unit_summed", UNITS, 1)
        y_copied = sem("y_copied", 1, 1)
        y_squared = sem("y_squared", 1)
        var_ps = sem("var_ps", 1)
        std_done = sem("std_done", 1)
        rstd_done = sem("rstd_done", 1)
        rstd_ps = sem("rstd_ps", 1)
        y_normed = sem("y_normed", 1)
        y_scaled = sem("y_scaled", 1)
        yg_done = sem("yg_done", 1, 2)
        out_ps = sem("out_ps", 1)
        x_added = sem("x_added", 1, 2)

        def turn_free(eng, n):
            eng.wait_ge(now_done.sem, now_done.all(n - 1))

        def xa_free(eng, n):
            eng.wait_ge(mix_added.sem, mix_added.all(n - 1))

        ln = LayerNorm(ctx, nc, "tm", sem, x, x_loaded, ps_turn, turn_free, lambda c: xa[:, c, 1:L + 1], xa_free,
                       vec["ln1_w"], vec["ln1_b"], ident, half, passed)

        ORDER = ["maa_v", "maa_k", "maa_w", "maa_r", "maa_g"]
        ROW = {"maa_w": 0, "maa_k": 1, "maa_v": 2, "maa_r": 3, "maa_g": 4}

        block = ctx.enter_context(nc.Block())

        @block.sync
        def _(sp):
            grant(sp, [x_stored, v_stored])
            loads = [(w_mix1, "maa_w1"), (vecs, "time_vecs"), (fixed, "fixed"), (w_dec1, "decay_w1"),
                     (w_proj["v"], "Wv"), (w_proj["k"], "Wk"), (w_proj["r"], "Wr"), (w_proj["g"], "Wg"),
                     (pick, "pick"), (prev, "prev1"), (head_sum, "head_sum"), (w_proj["o"], "Wo")]
            for tile, name in loads:
                sp.dma_start(tile[:, :, :], weights[name]).then_inc(weights_in.sem, 16)
            sp.dma_start(head_out[:, :, :], weights["head_out"]).then_inc(weights_in.sem, 16)
            sp.dma_start(w_mix2[:, :], weights["maa_w2"][0:P, :]).then_inc(weights_in.sem, 16)
            sp.dma_start(w_mix2g[:, :], weights["maa_w2"][P:P + DM, :]).then_inc(weights_in.sem, 16)
            sp.dma_start(w_dec2[:, :], weights["decay_w2"]).then_inc(weights_in.sem, 16)

            def load(n, par):
                sp.wait_ge(ln.stats_done.sem, ln.stats_done.all(n - 1))
                sp.sem_inc(passed.sem, 1)
                sp.wait_ge(x_stored.sem, x_stored.all(n - 2))
                sp.sem_inc(passed.sem, 1)
                sp.dma_start(x[par][:, :, :], x_in[n, :, :].rearrange("(t p) c -> p t c", p=P))\
                  .then_inc(x_loaded.sem, 16)
                sp.wait_ge(kv_done.sem, kv_done.all(n - 2))
                sp.sem_inc(passed.sem, 1)
                sp.dma_start(s0[par][:, :, :], first_state[n, :, :].rearrange("(c p) s -> p c s", p=P))\
                  .then_inc(s0_loaded.sem, 16)

            def store_v(n, par):
                sp.wait_ge(proj_out.sem, proj_out.at(n, 1))
                sp.dma_start(v_rows[par].rearrange("(c p) l -> p c l", p=P), vT[:, :, 0:L])\
                  .then_inc(v_stored.sem, 16)
                sp.wait_ge(v_stored.sem, v_stored.all(n))
                sp.sem_inc(passed.sem, 1)

            def load_unit(n, par, u):
                sp.wait_ge(unit_summed.sem, unit_summed.at(n - 1, u + 1 + UNITS - RING))
                c, h = u // 2, u % 2
                rows = v_rows[par].rearrange("(h s) l -> h (s l)", s=S)
                src = rows[c * HT:(c + 1) * HT, h * UW * L:(h + 1) * UW * L]
                sp.dma_start(unit[u % RING][:, :, :].rearrange("p s l -> p (s l)"),
                             src.unsqueeze(1).broadcast_to([HT, S, UW * L])).then_inc(unit_loaded[u % RING].sem, 16)

            def store(n, par):
                sp.wait_ge(x_added.sem, x_added.all(n))
                sp.sem_inc(passed.sem, 1)
                sp.dma_start(x_out[n, :, :].rearrange("(t p) c -> p t c", p=P), x[par][:, :, :])\
                  .then_inc(x_stored.sem, 16)

            def first():
                load(0, 0)
                store_v(0, 0)
                for u in range(RING):
                    load_unit(0, 0, u)

            def step(n, par):
                load(n + 1, 1 - par)
                for u in range(RING, UNITS):
                    load_unit(n, par, u)
                store_v(n + 1, 1 - par)
                for u in range(RING):
                    load_unit(n + 1, 1 - par, u)
                store(n, par)

            def last(n, par):
                for u in range(RING, UNITS):
                    load_unit(n, par, u)
                store(n, par)
                sp.wait_ge(x_stored.sem, x_stored.all(n))

            over_batches(sp, first, step, last)

        @block.vector
        def _(dve):
            dve.memset(eps[:, :], EPS).then_inc(consts_done.sem, 1)
            dve.memset(half[:, :], -0.5).then_inc(consts_done.sem, 1)
            dve.memset(kT[0][:, :, 0:1], 0.0).then_inc(consts_done.sem, 1)
            dve.memset(kT[1][:, :, 0:1], 0.0).then_inc(consts_done.sem, 1)
            dve.memset(vT[:, :, 0:1], 0.0).then_inc(consts_done.sem, 1)
            grant(dve, [ln.stats_done, mix_scaled, read_out, now_done, g_done, yg_done, x_added])
            dve.wait_ge(weights_in.sem, 16 * 16)

            def shifts(n, par):
                dve.wait_ge(ln.out_done.sem, ln.out_done.all(n))
                dve.tensor_tensor(shift[:, :, :], xa[:, :, 0:L], xa[:, :, 1:L + 1], ALU.subtract)\
                   .then_inc(shift_done.sem, 1)
                dve.wait_ge(shift_done.sem, shift_done.all(n))
                dve.wait_ge(proj_ps.sem, proj_ps.all(n - 1))
                for c in range(CT):
                    r = dve.scalar_tensor_tensor(mixed[1][:, c, :], shift[:, c, :], vec["maa_x"][:, c:c + 1],
                                                 xa[:, c, 1:L + 1], ALU.mult, ALU.add)
                r.then_inc(mix_in_done.sem, 1)

            def mix(n, j):
                dve.wait_ge(mix_ps.sem, mix_ps.at(n, j + 1))
                if j >= 2:
                    dve.wait_ge(proj_ps.sem, proj_ps.at(n, j - 1))
                for c in range(CT):
                    r = dve.scalar_tensor_tensor(mixed[j % 2][:, c, :], ps_mix[:, c, :], vec[ORDER[j]][:, c:c + 1],
                                                 shift[:, c, :], ALU.add, ALU.mult)
                r.then_inc(mix_scaled.sem, 1)

            def silu(n, par):
                dve.wait_ge(proj_out.sem, proj_out.at(n, 5))
                dve.scalar_tensor_tensor(gT[par][:, :, :], gT[par][:, :, :], 1.0, g_half[:, :, :], ALU.add, ALU.mult)\
                   .then_inc(g_done.sem, 1)

            def rkf_part(n, par):
                dve.wait_ge(proj_out.sem, proj_out.at(n, 4))
                dve.wait_ge(now_ps.sem, now_ps.all(n - 1))
                for c in range(CT):
                    r = dve.scalar_tensor_tensor(rkf[:, c, :], kT[par][:, c, 1:L + 1], vec["faaaa"][:, c:c + 1],
                                                 rT[par][:, c, :], ALU.mult, ALU.mult)
                r.then_inc(rkf_done.sem, 1)

            def now_part(n, par):
                dve.wait_ge(now_ps.sem, now_ps.all(n))
                dve.wait_ge(unit_summed.sem, unit_summed.at(n - 1, UNITS - 1))
                dve.tensor_tensor(now[:, :, :], ps_turn[:, :, :], vT[:, :, 1:L + 1], ALU.mult)\
                   .then_inc(now_done.sem, 1)

            def unit_part(n, par, u):
                c = u // 2
                dve.wait_ge(kv_done.sem, kv_done.at(n, u + 1))
                if u == 0:
                    dve.wait_ge(decay_exp.sem, decay_exp.all(n))
                buf = unit[u % RING]
                for s in range(UW):
                    r = dve.tensor_tensor_scan(buf[:, s, 1:L], wT[par][:, c, 0:L - 1], buf[:, s, 1:L],
                                               buf[:, s, 0:1], ALU.mult, ALU.add)
                r.then_inc(scanned.sem, 1)
                dve.wait_ge(scanned.sem, scanned.at(n, u + 1))
                dve.tensor_tensor(buf[:, :, :], buf[:, :, :],
                                  rT[par][:, c, :].unsqueeze(1).broadcast_to([P, UW, L]), ALU.mult)\
                   .then_inc(read_out.sem, 1)

            def back(n, par):
                dve.wait_ge(std_done.sem, std_done.all(n))
                dve.reciprocal(head_rstd[:, :], head_rstd[:, :]).then_inc(rstd_done.sem, 1)
                dve.wait_ge(rstd_ps.sem, rstd_ps.all(n))
                dve.tensor_tensor(y_sb[:, :, :], y_sb[:, :, :], ps_proj[:, :, :], ALU.mult).then_inc(y_normed.sem, 1)
                dve.wait_ge(y_scaled.sem, y_scaled.all(n))
                dve.tensor_tensor(yg[:, :, :], y_sb[:, :, :], gT[par][:, :, :], ALU.mult).then_inc(yg_done.sem, 1)
                dve.wait_ge(out_ps.sem, out_ps.all(n))
                dve.tensor_tensor(x[par][:, :, :], x[par][:, :, :],
                                  ps_proj[:, :, :].rearrange("p (t a) l -> p t (a l)", t=TT), ALU.add)\
                   .then_inc(x_added.sem, 1)

            def front(n, par, u):
                if u == 0:
                    ln.vector_moments(dve, n, par)
                if u == 1:
                    ln.vector_normalise(dve, n, par)
                if u == 2:
                    shifts(n, par)
                if u == 3:
                    mix(n, 0)
                if u == 4:
                    mix(n, 1)
                    mix(n, 2)
                if u == 5:
                    mix(n, 3)
                if u == 6:
                    mix(n, 4)
                if u == 7:
                    rkf_part(n, par)
                    now_part(n, par)
                    silu(n, par)

            def first():
                for u in range(UNITS):
                    front(0, 0, u)

            def step(n, par):
                for u in range(UNITS):
                    unit_part(n, par, u)
                    front(n + 1, 1 - par, u)
                back(n, par)

            def last(n, par):
                for u in range(UNITS):
                    unit_part(n, par, u)
                back(n, par)

            over_batches(dve, first, step, last)

        @block.gpsimd
        def _(pool):
            grant(pool, [mix_added, kv_done])
            pool.wait_ge(consts_done.sem, 5)

            def add(n, j):
                pool.wait_ge(mix_scaled.sem, mix_scaled.at(n, j + 1))
                pool.tensor_tensor(mixed[j % 2][:, :, :], mixed[j % 2][:, :, :], xa[:, :, 1:L + 1], ALU.add)\
                    .then_inc(mix_added.sem, 1)

            def unit_part(n, par, u):
                c, h = u // 2, u % 2
                buf = unit[u % RING]
                pool.wait_ge(unit_loaded[u % RING].sem, unit_loaded[u % RING].at(n, 16 * (u // RING + 1)))
                if u == 0:
                    pool.wait_ge(proj_out.sem, proj_out.at(n, 2))
                    pool.wait_ge(s0_loaded.sem, s0_loaded.all(n))
                pool.tensor_tensor(buf[:, :, 1:L], buf[:, :, 1:L],
                                   kT[par][:, c, 1:L].unsqueeze(1).broadcast_to([P, UW, L - 1]), ALU.mult)
                pool.tensor_copy(buf[:, :, 0:1], s0[par][:, c, h * UW:(h + 1) * UW].unsqueeze(2))\
                    .then_inc(kv_done.sem, 1)

            def first():
                ln.gpsimd_rstd(pool, 0)
                for j in range(5):
                    add(0, j)

            def step(n, par):
                unit_part(n, par, 0)
                ln.gpsimd_rstd(pool, n + 1)
                for u in range(1, UNITS):
                    unit_part(n, par, u)
                    if u == 3:
                        add(n + 1, 0)
                    if u == 4:
                        add(n + 1, 1)
                        add(n + 1, 2)
                    if u == 5:
                        add(n + 1, 3)
                    if u == 6:
                        add(n + 1, 4)

            def last(n, par):
                for u in range(UNITS):
                    unit_part(n, par, u)

            over_batches(pool, first, step, last)

        @block.scalar
        def _(act):
            grant(act, [proj_out, y_copied])
            act.wait_ge(weights_in.sem, 16 * 16)
            act.wait_ge(consts_done.sem, 5)

            def mix_tanh(n):
                act.wait_ge(mix_hidden.sem, mix_hidden.all(n))
                act.activation(mix_act[:, :], ps_turn[:, 0, :], ACT.Tanh)
                act.activation(mix_actg[:, :], ps_turn[0:DM, 1, :], ACT.Tanh).then_inc(mix_acted.sem, 1)

            def v_out(n, par):
                act.wait_ge(proj_ps.sem, proj_ps.at(n, 1))
                act.wait_ge(now_done.sem, now_done.all(n - 1))
                act.wait_ge(v_stored.sem, v_stored.all(n - 1))
                act.wait_ge(read_out.sem, read_out.all(n - 2))
                act.activation(vT[:, :, 1:L + 1], ps_proj[:, :, :], ACT.Copy).then_inc(proj_out.sem, 1)

            def k_out(n, par):
                act.wait_ge(proj_ps.sem, proj_ps.at(n, 2))
                act.activation(kT[par][:, :, 1:L + 1], ps_proj[:, :, :], ACT.Copy).then_inc(proj_out.sem, 1)

            def decay(n, par):
                act.wait_ge(dec_hidden.sem, dec_hidden.all(n))
                act.activation(dec_act[:, :], ps_proj[0:DD, 0, :], ACT.Tanh).then_inc(dec_acted.sem, 1)
                act.wait_ge(proj_ps.sem, proj_ps.at(n, 3))
                for c in range(CT):
                    r = act.activation(decay_e[:, c, :], ps_proj[:, c, :], ACT.Exp, bias=vec["time_decay"][:, c:c + 1])
                r.then_inc(proj_out.sem, 1)
                act.wait_ge(proj_out.sem, proj_out.at(n, 3))
                act.activation(wT[par][:, :, :], decay_e[:, :, :], ACT.Exp, scale=-1.0).then_inc(decay_exp.sem, 1)

            def r_out(n, par):
                act.wait_ge(proj_ps.sem, proj_ps.at(n, 4))
                act.activation(rT[par][:, :, :], ps_proj[:, :, :], ACT.Copy).then_inc(proj_out.sem, 1)

            def g_out(n, par):
                act.wait_ge(proj_ps.sem, proj_ps.at(n, 5))
                act.wait_ge(yg_done.sem, yg_done.all(n - 2))
                act.wait_ge(g_done.sem, g_done.all(n - 1))
                act.activation(gT[par][:, :, :], ps_proj[:, :, :], ACT.Tanh, scale=0.5)
                act.activation(g_half[:, :, :], ps_proj[:, :, :], ACT.Copy, scale=0.5).then_inc(proj_out.sem, 1)

            def back(n, par, ahead):
                act.wait_ge(decay_exp.sem, decay_exp.all(n + ahead))
                act.wait_ge(unit_summed.sem, unit_summed.all(n))
                act.wait_ge(yg_done.sem, yg_done.all(n - 1))
                act.activation(y_sb[:, :, :], ps_y[:, :, :], ACT.Copy)
                act.activation(y_sq[:, :, :], ps_y[:, :, :], ACT.Square).then_inc(y_copied.sem, 1)
                act.wait_ge(var_ps.sem, var_ps.all(n))
                act.activation(head_rstd[:, :], ps_proj[0:C // S, 0, :], ACT.Sqrt, bias=eps[0:C // S, 0:1])\
                   .then_inc(std_done.sem, 1)
                act.wait_ge(y_normed.sem, y_normed.all(n))
                for c in range(CT):
                    r = act.activation(y_sb[:, c, :], y_sb[:, c, :], ACT.Identity,
                                       bias=vec["gn_b"][:, c:c + 1], scale=vec["gn_w"][:, c:c + 1])
                r.then_inc(y_scaled.sem, 1)

            def front(n, par):
                ln.scalar_out(act, n, (xa, prev))
                mix_tanh(n)
                v_out(n, par)
                k_out(n, par)
                decay(n, par)
                r_out(n, par)
                g_out(n, par)

            def first():
                front(0, 0)

            def step(n, par):
                front(n + 1, 1 - par)
                back(n, par, 1)

            def last(n, par):
                back(n, par, 0)

            over_batches(act, first, step, last)

        @block.tensor
        def _(pe):
            grant(pe, [ln.turned_done, proj_ps, now_ps, unit_summed])
            pe.wait_ge(weights_in.sem, 16 * 16)

            def hidden(n):
                pe.wait_ge(mix_in_done.sem, mix_in_done.all(n))
                pe.wait_ge(ln.out_done.sem, ln.out_done.all(n))
                for c in range(CT):
                    pe.matmul(ps_turn[:, 0, :], w_mix1[:, c, 0:P], mixed[1][:, c, :], start=c == 0, stop=c == CT - 1)
                for c in range(CT):
                    r = pe.matmul(ps_turn[0:DM, 1, :], w_mix1[:, c, P:P + DM], mixed[1][:, c, :],
                                  start=c == 0, stop=c == CT - 1)
                r.then_inc(mix_hidden.sem, 1)

            def mixer(n, j):
                if j == 0:
                    pe.wait_ge(mix_acted.sem, mix_acted.all(n))
                    pe.wait_ge(mix_scaled.sem, mix_scaled.all(n - 1))
                else:
                    pe.wait_ge(mix_scaled.sem, mix_scaled.at(n, j))
                row = ROW[ORDER[j]] * DM
                for c in range(CT):
                    if row < P:
                        w, a = w_mix2[row:row + DM, c * P:(c + 1) * P], mix_act[row:row + DM, :]
                    else:
                        w, a = w_mix2g[:, c * P:(c + 1) * P], mix_actg[:, :]
                    r = pe.matmul(ps_mix[:, c, :], w, a, start=True, stop=True)
                r.then_inc(mix_ps.sem, 1)

            def project(n, j, f):
                pe.wait_ge(mix_added.sem, mix_added.at(n, j + 1))
                if f == "dec":
                    pe.wait_ge(proj_out.sem, proj_out.at(n, 2))
                    for c in range(CT):
                        r = pe.matmul(ps_proj[0:DD, 0, :], w_dec1[:, c, :], mixed[j % 2][:, c, :],
                                      start=c == 0, stop=c == CT - 1)
                    r.then_inc(dec_hidden.sem, 1)
                    pe.wait_ge(dec_acted.sem, dec_acted.all(n))
                    for c in range(CT):
                        r = pe.matmul(ps_proj[:, c, :], w_dec2[:, c * P:(c + 1) * P], dec_act[:, :],
                                      start=True, stop=True)
                else:
                    if j == 0:
                        pe.wait_ge(proj_out.sem, proj_out.all(n - 1))
                        pe.wait_ge(x_added.sem, x_added.all(n - 2))
                    else:
                        pe.wait_ge(proj_out.sem, proj_out.at(n, j))
                    for m in range(CT):
                        for c in range(CT):
                            r = pe.matmul(ps_proj[:, m, :], w_proj[f][:, c, m * P:(m + 1) * P], mixed[j % 2][:, c, :],
                                          start=c == 0, stop=c == CT - 1)
                r.then_inc(proj_ps.sem, 1)

            def now_part(n):
                pe.wait_ge(rkf_done.sem, rkf_done.all(n))
                pe.wait_ge(mix_acted.sem, mix_acted.all(n))
                for c in range(CT):
                    r = pe.matmul(ps_turn[:, c, :], head_ones, rkf[:, c, :], start=True, stop=True)
                r.then_inc(now_ps.sem, 1)

            def unit_part(n, u):
                c, h = u // 2, u % 2
                if u == 0:
                    pe.wait_ge(y_copied.sem, y_copied.all(n - 1))
                    pe.wait_ge(now_done.sem, now_done.all(n))
                if h == 0:
                    pe.matmul(ps_y[:, c, :], centre, now[:, c, :], start=True, stop=False)
                pe.wait_ge(read_out.sem, read_out.at(n, u + 1))
                for s in range(UW):
                    r = pe.matmul(ps_y[:, c, :], pick[:, h * UW + s, :], unit[u % RING][:, s, :],
                                  start=False, stop=h == 1 and s == UW - 1)
                r.then_inc(unit_summed.sem, 1)

            def back(n, ahead):
                pe.wait_ge(y_copied.sem, y_copied.all(n))
                pe.wait_ge(proj_out.sem, proj_out.all(n + ahead))
                for c in range(CT):
                    r = pe.matmul(ps_proj[0:C // S, 0, :], head_sum[:, c, :], y_sq[:, c, :],
                                  start=c == 0, stop=c == CT - 1)
                r.then_inc(var_ps.sem, 1)
                pe.wait_ge(rstd_done.sem, rstd_done.all(n))
                for c in range(CT):
                    r = pe.matmul(ps_proj[:, c, :], head_out[:, c, :], head_rstd[:, :], start=True, stop=True)
                r.then_inc(rstd_ps.sem, 1)
                pe.wait_ge(yg_done.sem, yg_done.all(n))
                out = ps_proj[:, :, :].rearrange("p (t a) l -> p t (a l)", t=TT)
                for t in range(TT):
                    for c in range(CT):
                        r = pe.matmul(out[:, t, :], yg[:, c, t * P:(t + 1) * P], w_proj["o"][:, c, :],
                                      start=c == 0, stop=c == CT - 1)
                r.then_inc(out_ps.sem, 1)

            def front(n, u):
                if u == 1:
                    ln.tensor_turn(pe, n)
                if u == 2:
                    hidden(n)
                    mixer(n, 0)
                if u == 3:
                    mixer(n, 1)
                    project(n, 0, "v")
                if u == 4:
                    mixer(n, 2)
                    project(n, 1, "k")
                if u == 5:
                    mixer(n, 3)
                    project(n, 2, "dec")
                if u == 6:
                    mixer(n, 4)
                    project(n, 3, "r")
                    project(n, 4, "g")
                if u == 7:
                    now_part(n)

            def first():
                for u in range(UNITS):
                    front(0, u)

            def step(n, par):
                for u in range(UNITS):
                    front(n + 1, u)
                    unit_part(n, u)
                back(n, 1)

            def last(n, par):
                for u in range(UNITS):
                    unit_part(n, u)
                back(n, 0)

            over_batches(pe, first, step, last)


def channel_mix(nc, held, x_in, x_out, weights):
    with ExitStack() as ctx:
        def sb(name, shape):
            return ctx.enter_context(nc.sbuf_tensor(f"cm_{name}", shape, F32))

        sem = counter(held, nc, "cm")

        wk, wr, wv = (sb(f"w{f}", [P, CT, C]) for f in "krv")
        vecs = sb("vecs", [P, len(CHAN_VECS), CT])
        vec = {name: vecs[:, i, :] for i, name in enumerate(CHAN_VECS)}
        fixed = sb("fixed", [P, 3, P])
        prev = sb("prev", [P, B, CT])
        half = sb("half", [P, TT])
        x = [sb(f"x{i}", [P, TT, C]) for i in range(2)]
        xc = sb("xc", [P, CT, L + 1])
        shift = sb("shift", [P, CT, L])
        xk = [sb(f"xk{i}", [P, CT, L]) for i in range(2)]
        xr = [sb(f"xr{i}", [P, CT, L]) for i in range(2)]
        relu = sb("relu", [P, CT, L])
        kk = sb("kk", [P, CT, L])
        gate = sb("gate", [P, TT, C])
        gated = sb("gated", [P, TT, C])
        ps_turn = ctx.enter_context(nc.psum_tensor("cm_ps_turn", [P, CT, L], F32))
        ps_k = ctx.enter_context(nc.psum_tensor("cm_ps_k", [P, CT, L], F32))
        ps_r = ctx.enter_context(nc.psum_tensor("cm_ps_r", [P, TT, C], F32))
        ps_v = ctx.enter_context(nc.psum_tensor("cm_ps_v", [P, TT, C], F32))

        weights_in = sem("weights_in", 0)
        passed = sem("passed", 0)
        consts_done = sem("consts_done", 0)
        x_loaded = sem("x_loaded", 16)
        x_stored = sem("x_stored", 16, 2)
        shift_done = sem("shift_done", 1)
        mixed_done = sem("mixed_done", 1, 1)
        k_ps = sem("k_ps", 1)
        r_ps = sem("r_ps", 1, 2)
        v_ps = sem("v_ps", 1, 1)
        relu_done = sem("relu_done", 1, 1)
        kk_done = sem("kk_done", 1, 1)
        gate_done = sem("gate_done", 1, 1)
        gated_done = sem("gated_done", 1, 1)
        x_added = sem("x_added", 1, 1)

        ln = LayerNorm(ctx, nc, "cm", sem, x, x_loaded, ps_turn,
                       lambda eng, n: eng.wait_ge(mixed_done.sem, mixed_done.all(n - 1)),
                       lambda c: xc[:, c, 1:L + 1],
                       lambda eng, n: eng.wait_ge(mixed_done.sem, mixed_done.all(n - 1)),
                       vec["ln2_w"], vec["ln2_b"], fixed[:, 0, :], half, passed)

        block = ctx.enter_context(nc.Block())

        @block.sync
        def _(sp):
            grant(sp, [x_stored])
            for tile, name in [(vecs, "chan_vecs"), (fixed, "fixed"), (prev, "prev0"), (wk, "fWk"), (wr, "fWr"), (wv, "fWv")]:
                sp.dma_start(tile[:, :, :], weights[name]).then_inc(weights_in.sem, 16)

            def load(n, par):
                sp.wait_ge(ln.stats_done.sem, ln.stats_done.all(n - 1))
                sp.sem_inc(passed.sem, 1)
                sp.wait_ge(x_stored.sem, x_stored.all(n - 2))
                sp.sem_inc(passed.sem, 1)
                sp.dma_start(x[par][:, :, :], x_in[n, :, :].rearrange("(t p) c -> p t c", p=P))\
                  .then_inc(x_loaded.sem, 16)

            def store(n, par):
                sp.wait_ge(x_added.sem, x_added.all(n))
                sp.sem_inc(passed.sem, 1)
                sp.dma_start(x_out[n, :, :].rearrange("(t p) c -> p t c", p=P), x[par][:, :, :])\
                  .then_inc(x_stored.sem, 16)

            def step(n, par):
                load(n + 1, 1 - par)
                store(n, par)

            def last(n, par):
                store(n, par)
                sp.wait_ge(x_stored.sem, x_stored.all(n))

            over_batches(sp, lambda: load(0, 0), step, last)

        @block.vector
        def _(dve):
            dve.memset(half[:, :], -0.5).then_inc(consts_done.sem, 1)
            grant(dve, [ln.stats_done, mixed_done, gated_done, x_added])
            dve.wait_ge(weights_in.sem, 16 * 6)

            def front(n, par):
                ln.vector_moments(dve, n, par)
                ln.vector_normalise(dve, n, par)
                dve.wait_ge(ln.out_done.sem, ln.out_done.all(n))
                dve.tensor_tensor(shift[:, :, :], xc[:, :, 0:L], xc[:, :, 1:L + 1], ALU.subtract)\
                   .then_inc(shift_done.sem, 1)
                dve.wait_ge(shift_done.sem, shift_done.all(n))
                dve.wait_ge(r_ps.sem, r_ps.all(n - 2))
                for tile, f in ((xk[par], "fmaa_k"), (xr[par], "fmaa_r")):
                    for c in range(CT):
                        r = dve.scalar_tensor_tensor(tile[:, c, :], shift[:, c, :], vec[f][:, c:c + 1],
                                                     xc[:, c, 1:L + 1], ALU.mult, ALU.add)
                r.then_inc(mixed_done.sem, 1)

            def back(n, par):
                dve.wait_ge(v_ps.sem, v_ps.all(n))
                dve.wait_ge(gate_done.sem, gate_done.all(n))
                dve.wait_ge(x_added.sem, x_added.all(n - 1))
                dve.scalar_tensor_tensor(gated[:, :, :], gate[:, :, :], 1.0, ps_v[:, :, :], ALU.add, ALU.mult)\
                   .then_inc(gated_done.sem, 1)
                dve.wait_ge(gated_done.sem, gated_done.all(n))
                dve.scalar_tensor_tensor(x[par][:, :, :], gated[:, :, :], 0.5, x[par][:, :, :], ALU.mult, ALU.add)\
                   .then_inc(x_added.sem, 1)

            def step(n, par):
                front(n + 1, 1 - par)
                back(n, par)

            over_batches(dve, lambda: front(0, 0), step, back)

        @block.gpsimd
        def _(pool):
            grant(pool, [kk_done])
            pool.wait_ge(consts_done.sem, 1)

            def back(n, par):
                pool.wait_ge(relu_done.sem, relu_done.all(n))
                pool.wait_ge(v_ps.sem, v_ps.all(n - 1))
                pool.tensor_tensor(kk[:, :, :], relu[:, :, :], relu[:, :, :], ALU.mult).then_inc(kk_done.sem, 1)

            def step(n, par):
                ln.gpsimd_rstd(pool, n + 1)
                back(n, par)

            over_batches(pool, lambda: ln.gpsimd_rstd(pool, 0), step, back)

        @block.scalar
        def _(act):
            grant(act, [relu_done, gate_done])
            act.wait_ge(weights_in.sem, 16 * 6)

            def back(n, par):
                act.wait_ge(k_ps.sem, k_ps.all(n))
                act.wait_ge(kk_done.sem, kk_done.all(n - 1))
                act.activation(relu[:, :, :], ps_k[:, :, :], ACT.Relu).then_inc(relu_done.sem, 1)
                act.wait_ge(r_ps.sem, r_ps.all(n))
                act.wait_ge(gated_done.sem, gated_done.all(n - 1))
                act.activation(gate[:, :, :], ps_r[:, :, :], ACT.Tanh, scale=0.5).then_inc(gate_done.sem, 1)

            def step(n, par):
                ln.scalar_out(act, n + 1, (xc, prev))
                back(n, par)

            over_batches(act, lambda: ln.scalar_out(act, 0, (xc, prev)), step, back)

        @block.tensor
        def _(pe):
            grant(pe, [ln.turned_done, r_ps, v_ps])
            pe.wait_ge(weights_in.sem, 16 * 6)

            def back(n, par):
                pe.wait_ge(mixed_done.sem, mixed_done.all(n))
                pe.wait_ge(relu_done.sem, relu_done.all(n - 1))
                for m in range(CT):
                    for c in range(CT):
                        r = pe.matmul(ps_k[:, m, :], wk[:, c, m * P:(m + 1) * P], xk[par][:, c, :],
                                      start=c == 0, stop=c == CT - 1)
                r.then_inc(k_ps.sem, 1)
                pe.wait_ge(gate_done.sem, gate_done.all(n - 1))
                for t in range(TT):
                    for c in range(CT):
                        r = pe.matmul(ps_r[:, t, :], xr[par][:, c, t * P:(t + 1) * P], wr[:, c, :],
                                      start=c == 0, stop=c == CT - 1)
                r.then_inc(r_ps.sem, 1)
                pe.wait_ge(kk_done.sem, kk_done.all(n))
                pe.wait_ge(gated_done.sem, gated_done.all(n - 1))
                for t in range(TT):
                    for c in range(CT):
                        r = pe.matmul(ps_v[:, t, :], kk[:, c, t * P:(t + 1) * P], wv[:, c, :],
                                      start=c == 0, stop=c == CT - 1)
                r.then_inc(v_ps.sem, 1)

            def step(n, par):
                ln.tensor_turn(pe, n + 1)
                back(n, par)

            over_batches(pe, lambda: ln.tensor_turn(pe, 0), step, back)


def attention(nc, held, name, x_in, x_out, source, mask, weights, cross):
    with ExitStack() as ctx:
        def sb(tile, shape):
            return ctx.enter_context(nc.sbuf_tensor(f"{name}_{tile}", shape, F32))

        sem = counter(held, nc, name)

        wq, wk, wv, wo = (sb(f"w{f}", [P, CT, C]) for f in "qkvo")
        vecs = sb("vecs", [P, 5, CT])
        ln_s, ln_b, b_q, b_k, b_v = (vecs[:, i, :] for i in range(5))
        bq_scaled = sb("bq_scaled", [P, CT])
        bo = sb("bo", [P, C])
        fixed = sb("fixed", [P, 3, P])
        ident = fixed[:, 0, :]
        half = sb("half", [P, TT])
        x = [sb(f"x{i}", [P, TT, C]) for i in range(2)]
        lnT = sb("lnT", [P, CT, L])
        src = sb("src", [P, CT, L]) if cross else lnT
        qT = [sb(f"qT{i}", [P, CT, L]) for i in range(2)]
        kT = [sb(f"kT{i}", [P, CT, L]) for i in range(2)]
        v = [sb(f"v{i}", [P, TT, C]) for i in range(2)]
        masks = 2 if cross else 1
        mask_in = [sb(f"mask_in{i}", [P, TT, L]) for i in range(masks)]
        mask_neg = [sb(f"mask_neg{i}", [P, TT, L]) for i in range(masks)]
        mask_add = [sb(f"mask_add{i}", [P, TT, L]) for i in range(masks)]
        low = [sb(f"low{i}", [P, TT, L]) for i in range(2)]
        low_min = [sb(f"low_min{i}", [P, TT]) for i in range(2)]
        prob = [sb(f"prob{i}", [P, TT, L]) for i in range(2)]
        probT = [sb(f"probT{i}", [P, TT, L]) for i in range(2)]
        row_sum = sb("row_sum", [P, TT, NH])
        row_inv = sb("row_inv", [P, TT, NH])
        mixed = sb("mixed", [P, TT, C])
        mixedT = sb("mixedT", [P, CT, L])
        ps_dense = ctx.enter_context(nc.psum_tensor(f"{name}_ps_dense", [P, CT, L], F32))
        ps_score = [ctx.enter_context(nc.psum_tensor(f"{name}_ps_score{i}", [P, TT, L], F32)) for i in range(2)]
        ps_turn = [ctx.enter_context(nc.psum_tensor(f"{name}_ps_turn{i}", [P, TT, L], F32)) for i in range(2)]
        ps_mixed = ctx.enter_context(nc.psum_tensor(f"{name}_ps_mixed", [P, TT, C], F32))
        dense_rows = ps_dense[:, :, :].rearrange("p (t a) l -> p t (a l)", t=TT)

        weights_in = sem("weights_in", 0)
        passed = sem("passed", 0)
        consts_done = sem("consts_done", 0)
        x_loaded = sem("x_loaded", 16)
        src_loaded = sem("src_loaded", 16)
        mask_loaded = sem("mask_loaded", 16)
        x_stored = sem("x_stored", 16, 2)
        mask_flipped = sem("mask_flipped", 1, 1)
        mask_done = sem("mask_done", 1)
        biased = sem("biased", 1)
        q_ps = sem("q_ps", 1)
        k_ps = sem("k_ps", 1)
        v_ps = sem("v_ps", 1, 1)
        q_out = sem("q_out", 1)
        k_out = sem("k_out", 1)
        v_out = sem("v_out", 1)
        score_ps = sem("score_ps", NH, 2)
        masked = sem("masked", NH, 1)
        low_done = sem("low_done", NH, 2)
        prob_done = sem("prob_done", NH, 1)
        prob_ps = sem("prob_ps", NH, 1)
        probT_done = sem("probT_done", NH, 1)
        mixed_ps = sem("mixed_ps", NH, 2)
        inv_done = sem("inv_done", 1)
        mixed_done = sem("mixed_done", 1, 1)
        mixed_turned = sem("mixed_turned", 1, 1)
        mixedT_done = sem("mixedT_done", 1, 1)
        out_ps = sem("out_ps", 1)
        x_added = sem("x_added", 1, 1)

        ln = LayerNorm(ctx, nc, name, sem, x, x_loaded, ps_dense,
                       lambda eng, n: eng.wait_ge(mixedT_done.sem, mixedT_done.all(n - 2)),
                       lambda c: lnT[:, c, :],
                       lambda eng, n: eng.wait_ge(v_ps.sem, v_ps.all(n - 1)),
                       ln_s, ln_b, ident, half, passed)
        mixedT_done.ahead = 2

        block = ctx.enter_context(nc.Block())
        LOADS = [(vecs, "vecs"), (fixed, "fixed"), (wq, "q"), (wk, "k"), (wv, "v"), (wo, "o")]

        @block.sync
        def _(sp):
            grant(sp, [x_stored])
            for tile, w in LOADS:
                sp.dma_start(tile[:, :, :], weights[w]).then_inc(weights_in.sem, 16)
            sp.dma_start(bo[:, :], weights["bo"].unsqueeze(0).broadcast_to([P, C])).then_inc(weights_in.sem, 16)

            def load_mask(n, par):
                sp.dma_start(mask_in[par][:, :, :], mask[n, 0, :, :].rearrange("(t p) k -> p t k", p=P))\
                  .then_inc(mask_loaded.sem, 16)

            def load(n, par):
                sp.wait_ge(ln.stats_done.sem, ln.stats_done.all(n - 1))
                sp.sem_inc(passed.sem, 1)
                sp.wait_ge(x_stored.sem, x_stored.all(n - 2))
                sp.sem_inc(passed.sem, 1)
                sp.dma_start(x[par][:, :, :], x_in[n, :, :].rearrange("(t p) c -> p t c", p=P))\
                  .then_inc(x_loaded.sem, 16)
                if cross:
                    sp.wait_ge(v_ps.sem, v_ps.all(n - 1))
                    sp.sem_inc(passed.sem, 1)
                    sp.dma_start(src[:, :, :], source[n, :, :].rearrange("(c p) l -> p c l", p=P))\
                      .then_inc(src_loaded.sem, 16)
                    sp.wait_ge(mask_flipped.sem, mask_flipped.all(n - 1))
                    sp.sem_inc(passed.sem, 1)
                    sp.wait_ge(low_done.sem, low_done.all(n - 2))
                    sp.sem_inc(passed.sem, 1)
                    load_mask(n, par)

            def store(n, par):
                sp.wait_ge(x_added.sem, x_added.all(n))
                sp.sem_inc(passed.sem, 1)
                sp.dma_start(x_out[n, :, :].rearrange("(t p) c -> p t c", p=P), x[par][:, :, :])\
                  .then_inc(x_stored.sem, 16)

            def first():
                load(0, 0)
                if not cross:
                    load_mask(0, 0)

            def step(n, par):
                load(n + 1, 1 - par)
                store(n, par)

            def last(n, par):
                store(n, par)
                sp.wait_ge(x_stored.sem, x_stored.all(n))

            over_batches(sp, first, step, last)

        @block.vector
        def _(dve):
            dve.memset(half[:, :], -0.5).then_inc(consts_done.sem, 1)
            grant(dve, [ln.stats_done, masked, low_done, mixed_done, x_added])
            dve.wait_ge(weights_in.sem, 16 * 7)
            dve.tensor_scalar(bq_scaled[:, :], b_q, HD ** -0.5, None, ALU.mult).then_inc(consts_done.sem, 1)

            def softmax_low(n, par, h):
                m = par if cross else 0
                dve.wait_ge(score_ps.sem, score_ps.at(n, h + 1))
                if h == 0:
                    if cross:
                        dve.wait_ge(mask_done.sem, mask_done.all(n))
                    else:
                        dve.wait_ge(mask_done.sem, 1)
                dve.wait_ge(prob_done.sem, prob_done.at(n, h - 1))
                dve.tensor_tensor(low[h % 2][:, :, :], ps_score[h % 2][:, :, :], mask_neg[m][:, :, :], ALU.mult)\
                   .then_inc(masked.sem, 1)
                dve.wait_ge(masked.sem, masked.at(n, h + 1))
                dve.sem_inc(passed.sem, 1)
                for t in range(TT):
                    r = dve.tensor_tensor_reduce(low[h % 2][:, t, :], low[h % 2][:, t, :], mask_add[m][:, t, :],
                                                 1.0, 3.0e38, ALU.add, ALU.min, low_min[h % 2][:, t:t + 1])
                r.then_inc(low_done.sem, 1)

            def back(n, par):
                dve.wait_ge(prob_done.sem, prob_done.all(n))
                dve.reciprocal(row_inv[:, :, :], row_sum[:, :, :]).then_inc(inv_done.sem, 1)
                dve.wait_ge(inv_done.sem, inv_done.all(n))
                dve.wait_ge(mixed_ps.sem, mixed_ps.all(n))
                dve.wait_ge(mixed_turned.sem, mixed_turned.all(n - 1))
                for t in range(TT):
                    r = dve.tensor_tensor(mixed[:, t, :].rearrange("p (h d) -> p h d", h=NH),
                                          ps_mixed[:, t, :].rearrange("p (h d) -> p h d", h=NH),
                                          row_inv[:, t, :].unsqueeze(2).broadcast_to([P, NH, HD]), ALU.mult)
                r.then_inc(mixed_done.sem, 1)
                dve.wait_ge(out_ps.sem, out_ps.all(n))
                dve.wait_ge(biased.sem, biased.all(n))
                dve.tensor_tensor(x[par][:, :, :], x[par][:, :, :], ps_mixed[:, :, :], ALU.add)\
                   .then_inc(x_added.sem, 1)

            def first():
                ln.vector_moments(dve, 0, 0)
                ln.vector_normalise(dve, 0, 0)

            def step(n, par):
                for h in range(NH):
                    softmax_low(n, par, h)
                    if h == 0:
                        ln.vector_moments(dve, n + 1, 1 - par)
                    if h == 1:
                        ln.vector_normalise(dve, n + 1, 1 - par)
                back(n, par)

            def last(n, par):
                for h in range(NH):
                    softmax_low(n, par, h)
                back(n, par)

            over_batches(dve, first, step, last)

        @block.gpsimd
        def _(pool):
            grant(pool, [mask_flipped])
            pool.wait_ge(consts_done.sem, 1)
            pool.wait_ge(weights_in.sem, 16 * 7)

            def masks_of(n, par):
                if cross:
                    pool.wait_ge(low_done.sem, low_done.all(n - 2))
                    pool.sem_inc(passed.sem, 1)
                pool.wait_ge(mask_loaded.sem, mask_loaded.all(n))
                pool.sem_inc(passed.sem, 1)
                pool.tensor_scalar(mask_neg[par][:, :, :], mask_in[par][:, :, :], -1.0, None, ALU.mult)
                pool.tensor_scalar(mask_add[par][:, :, :], mask_in[par][:, :, :], -1.0, 1.0, ALU.mult, ALU.add)\
                    .then_inc(mask_flipped.sem, 1)
                pool.wait_ge(mask_flipped.sem, mask_flipped.all(n))
                pool.sem_inc(passed.sem, 1)
                pool.tensor_scalar(mask_add[par][:, :, :], mask_add[par][:, :, :], 10000.0, None, ALU.mult)\
                    .then_inc(mask_done.sem, 1)

            def add_bias(n, par):
                pool.wait_ge(ln.normed_done.sem, ln.normed_done.all(n))
                pool.tensor_tensor(x[par][:, :, :], x[par][:, :, :],
                                   bo[:, :].unsqueeze(1).broadcast_to([P, TT, C]), ALU.add).then_inc(biased.sem, 1)

            def front(n, par):
                ln.gpsimd_rstd(pool, n)
                if cross:
                    masks_of(n, par)
                add_bias(n, par)

            def first():
                if not cross:
                    masks_of(0, 0)
                front(0, 0)

            over_batches(pool, first, lambda n, par: front(n + 1, 1 - par), lambda n, par: None)

        @block.scalar
        def _(act):
            grant(act, [prob_done, probT_done, mixedT_done])
            act.wait_ge(consts_done.sem, 2)

            def q_copy(n, par):
                act.wait_ge(q_ps.sem, q_ps.all(n))
                act.wait_ge(score_ps.sem, score_ps.all(n - 2))
                for c in range(CT):
                    r = act.activation(qT[par][:, c, :], ps_dense[:, c, :], ACT.Identity,
                                       bias=bq_scaled[:, c:c + 1], scale=HD ** -0.5)
                r.then_inc(q_out.sem, 1)

            def k_copy(n, par):
                act.wait_ge(k_ps.sem, k_ps.all(n))
                for c in range(CT):
                    r = act.activation(kT[par][:, c, :], ps_dense[:, c, :], ACT.Identity, bias=b_k[:, c:c + 1])
                r.then_inc(k_out.sem, 1)

            def v_copy(n, par):
                act.wait_ge(v_ps.sem, v_ps.all(n))
                act.wait_ge(mixed_ps.sem, mixed_ps.all(n - 2))
                act.activation(v[par][:, :, :], dense_rows, ACT.Copy).then_inc(v_out.sem, 1)

            def exps(n, h):
                act.wait_ge(low_done.sem, low_done.at(n, h + 1))
                act.wait_ge(prob_ps.sem, prob_ps.at(n, h - 1))
                if h == 0:
                    act.wait_ge(mixed_done.sem, mixed_done.all(n - 1))
                for t in range(TT):
                    r = act.activation(prob[h % 2][:, t, :], low[h % 2][:, t, :], ACT.Exp,
                                       bias=low_min[h % 2][:, t:t + 1], scale=-1.0,
                                       accum_out=row_sum[:, t, h:h + 1])
                r.then_inc(prob_done.sem, 1)

            def prob_copy(n, h):
                act.wait_ge(prob_ps.sem, prob_ps.at(n, h + 1))
                act.wait_ge(mixed_ps.sem, mixed_ps.at(n, h - 1))
                act.activation(probT[h % 2][:, :, :], ps_turn[h % 2][:, :, :], ACT.Copy).then_inc(probT_done.sem, 1)

            def back(n, par):
                act.wait_ge(mixed_turned.sem, mixed_turned.all(n))
                for c in range(CT):
                    r = act.activation(mixedT[:, c, :], ps_dense[:, c, :], ACT.Identity, bias=b_v[:, c:c + 1])
                r.then_inc(mixedT_done.sem, 1)

            def first():
                ln.scalar_out(act, 0)
                q_copy(0, 0)
                k_copy(0, 0)
                v_copy(0, 0)

            def heads(n, par, front):
                for h in range(NH + 1):
                    if h < NH:
                        exps(n, h)
                    if h >= 1:
                        prob_copy(n, h - 1)
                    if front and h == 2:
                        ln.scalar_out(act, n + 1)
                    if front and h == 6:
                        q_copy(n + 1, 1 - par)
                    if front and h == 10:
                        k_copy(n + 1, 1 - par)
                    if front and h == 14:
                        v_copy(n + 1, 1 - par)
                back(n, par)

            over_batches(act, first, lambda n, par: heads(n, par, True), lambda n, par: heads(n, par, False))

        @block.tensor
        def _(pe):
            grant(pe, [ln.turned_done, v_ps, score_ps, prob_ps, mixed_ps, mixed_turned])
            pe.wait_ge(weights_in.sem, 16 * 7)

            def q_part(n, m):
                if m == 0:
                    pe.wait_ge(ln.out_done.sem, ln.out_done.all(n))
                for c in range(CT):
                    r = pe.matmul(ps_dense[:, m, :], wq[:, c, m * P:(m + 1) * P], lnT[:, c, :],
                                  start=c == 0, stop=c == CT - 1)
                if m == CT - 1:
                    r.then_inc(q_ps.sem, 1)

            def k_part(n, m):
                if m == 0:
                    pe.wait_ge(q_out.sem, q_out.all(n))
                    if cross:
                        pe.wait_ge(src_loaded.sem, src_loaded.all(n))
                for c in range(CT):
                    r = pe.matmul(ps_dense[:, m, :], wk[:, c, m * P:(m + 1) * P], src[:, c, :],
                                  start=c == 0, stop=c == CT - 1)
                if m == CT - 1:
                    r.then_inc(k_ps.sem, 1)

            def v_part(n, m):
                t, half_of_c = m // 2, m % 2
                if m == 0:
                    pe.wait_ge(k_out.sem, k_out.all(n))
                for c in range(2 * half_of_c, 2 * half_of_c + 2):
                    r = pe.matmul(dense_rows[:, t, :], src[:, c, t * P:(t + 1) * P], wv[:, c, :],
                                  start=c == 0, stop=c == CT - 1)
                if m == 3:
                    r.then_inc(v_ps.sem, 1)

            def score(n, par, h):
                c, row = h // HC, (h % HC) * HD
                if h == 0:
                    pe.wait_ge(v_out.sem, v_out.all(n))
                pe.wait_ge(low_done.sem, low_done.at(n, h - 1))
                for t in range(TT):
                    r = pe.matmul(ps_score[h % 2][:, t, :], qT[par][row:row + HD, c, t * P:(t + 1) * P],
                                  kT[par][row:row + HD, c, :], start=True, stop=True)
                r.then_inc(score_ps.sem, 1)

            def turn(n, h):
                pe.wait_ge(prob_done.sem, prob_done.at(n, h + 1))
                pe.wait_ge(probT_done.sem, probT_done.at(n, h - 1))
                for k in range(TT):
                    for t in range(TT):
                        r = pe.transpose(ps_turn[h % 2][:, k, t * P:(t + 1) * P],
                                         prob[h % 2][:, t, k * P:(k + 1) * P], ident)
                r.then_inc(prob_ps.sem, 1)

            def mix(n, par, h):
                pe.wait_ge(probT_done.sem, probT_done.at(n, h + 1))
                if h == 0:
                    pe.wait_ge(x_added.sem, x_added.all(n - 1))
                for t in range(TT):
                    for k in range(TT):
                        r = pe.matmul(ps_mixed[:, t, h * HD:(h + 1) * HD], probT[h % 2][:, k, t * P:(t + 1) * P],
                                      v[par][:, k, h * HD:(h + 1) * HD], start=k == 0, stop=k == TT - 1)
                r.then_inc(mixed_ps.sem, 1)

            def back(n, ahead):
                pe.wait_ge(mixed_done.sem, mixed_done.all(n))
                pe.wait_ge(v_out.sem, v_out.all(n + ahead))
                for t in range(TT):
                    for c in range(CT):
                        r = pe.transpose(ps_dense[:, c, t * P:(t + 1) * P], mixed[:, t, c * P:(c + 1) * P], ident)
                r.then_inc(mixed_turned.sem, 1)
                pe.wait_ge(mixedT_done.sem, mixedT_done.all(n))
                for t in range(TT):
                    for c in range(CT):
                        r = pe.matmul(ps_mixed[:, t, :], mixedT[:, c, t * P:(t + 1) * P], wo[:, c, :],
                                      start=c == 0, stop=c == CT - 1)
                r.then_inc(out_ps.sem, 1)

            def first():
                ln.tensor_turn(pe, 0)
                for part in (q_part, k_part, v_part):
                    for m in range(4):
                        part(0, m)

            def heads(n, par, front):
                for h in range(NH + 2):
                    if front and h == 2:
                        ln.tensor_turn(pe, n + 1)
                    if front and 3 <= h < 15:
                        (q_part, k_part, v_part)[(h - 3) // 4](n + 1, (h - 3) % 4)
                    if h < NH:
                        score(n, par, h)
                    if 1 <= h <= NH:
                        turn(n, h - 1)
                    if h >= 2:
                        mix(n, par, h - 2)
                back(n, int(front))

            over_batches(pe, first, lambda n, par: heads(n, par, True), lambda n, par: heads(n, par, False))


def mlp(nc, held, x_in, x_out, weights):
    GROUPS = FF // C
    with ExitStack() as ctx:
        def sb(name, shape):
            return ctx.enter_context(nc.sbuf_tensor(f"ff_{name}", shape, F32))

        sem = counter(held, nc, "ff")

        w1 = sb("w1", [P, CT, FF])
        w2 = sb("w2", [P, FF // P, C])
        vecs = sb("vecs", [P, 2, CT])
        b1 = sb("b1", [P, FF // P])
        b2 = sb("b2", [P, C])
        fixed = sb("fixed", [P, 3, P])
        half = sb("half", [P, TT])
        x = [sb(f"x{i}", [P, TT, C]) for i in range(2)]
        lnT = sb("lnT", [P, CT, L])
        pre = [sb(f"pre{i}", [P, CT, L]) for i in range(2)]
        poly = [sb(f"poly{i}", [P, CT, L]) for i in range(2)]
        tanh = [sb(f"tanh{i}", [P, CT, L]) for i in range(2)]
        hid = [sb(f"hid{i}", [P, FF // P, L]) for i in range(2)]
        ps_turn = ctx.enter_context(nc.psum_tensor("ff_ps_turn", [P, CT, L], F32))
        ps_hid = [ctx.enter_context(nc.psum_tensor(f"ff_ps_hid{i}", [P, CT, L], F32)) for i in range(2)]
        ps_out = ctx.enter_context(nc.psum_tensor("ff_ps_out", [P, TT, C], F32))

        weights_in = sem("weights_in", 0)
        passed = sem("passed", 0)
        consts_done = sem("consts_done", 0)
        x_loaded = sem("x_loaded", 16)
        x_stored = sem("x_stored", 16, 2)
        biased = sem("biased", 1)
        hid_ps = sem("hid_ps", GROUPS, 1)
        pre_done = sem("pre_done", GROUPS, 1)
        sq_done = sem("sq_done", GROUPS)
        poly_done = sem("poly_done", GROUPS)
        cube_done = sem("cube_done", GROUPS)
        tanh_done = sem("tanh_done", GROUPS, 1)
        hid_done = sem("hid_done", GROUPS, 1)
        out_ps = sem("out_ps", 1, 2)
        x_added = sem("x_added", 1, 1)

        ln = LayerNorm(ctx, nc, "ff", sem, x, x_loaded, ps_turn,
                       lambda eng, n: eng.wait_ge(ln_out().sem, ln_out().all(n - 1)),
                       lambda c: lnT[:, c, :],
                       lambda eng, n: eng.wait_ge(hid_ps.sem, hid_ps.all(n - 1)),
                       vecs[:, 0, :], vecs[:, 1, :], fixed[:, 0, :], half, passed)
        ln.out_done.ahead = 1

        def ln_out():
            return ln.out_done

        block = ctx.enter_context(nc.Block())

        @block.sync
        def _(sp):
            grant(sp, [x_stored])
            for tile, w in [(vecs, "vecs"), (fixed, "fixed"), (w1, "w1"), (w2, "w2")]:
                sp.dma_start(tile[:, :, :], weights[w]).then_inc(weights_in.sem, 16)
            sp.dma_start(b1[:, :], weights["b1"]).then_inc(weights_in.sem, 16)
            sp.dma_start(b2[:, :], weights["b2"].unsqueeze(0).broadcast_to([P, C])).then_inc(weights_in.sem, 16)

            def load(n, par):
                sp.wait_ge(ln.stats_done.sem, ln.stats_done.all(n - 1))
                sp.sem_inc(passed.sem, 1)
                sp.wait_ge(x_stored.sem, x_stored.all(n - 2))
                sp.sem_inc(passed.sem, 1)
                sp.dma_start(x[par][:, :, :], x_in[n, :, :].rearrange("(t p) c -> p t c", p=P))\
                  .then_inc(x_loaded.sem, 16)

            def store(n, par):
                sp.wait_ge(x_added.sem, x_added.all(n))
                sp.sem_inc(passed.sem, 1)
                sp.dma_start(x_out[n, :, :].rearrange("(t p) c -> p t c", p=P), x[par][:, :, :])\
                  .then_inc(x_stored.sem, 16)

            def step(n, par):
                load(n + 1, 1 - par)
                store(n, par)

            def last(n, par):
                store(n, par)
                sp.wait_ge(x_stored.sem, x_stored.all(n))

            over_batches(sp, lambda: load(0, 0), step, last)

        @block.vector
        def _(dve):
            dve.memset(half[:, :], -0.5).then_inc(consts_done.sem, 1)
            grant(dve, [ln.stats_done, hid_done, x_added])
            dve.wait_ge(weights_in.sem, 16 * 6)

            def norm(n, par):
                ln.vector_moments(dve, n, par)
                ln.vector_normalise(dve, n, par)

            def square(n, g):
                dve.wait_ge(pre_done.sem, pre_done.at(n, g + 1))
                dve.tensor_tensor(poly[g % 2][:, :, :], pre[g % 2][:, :, :], pre[g % 2][:, :, :], ALU.mult)\
                   .then_inc(sq_done.sem, 1)
                dve.wait_ge(sq_done.sem, sq_done.at(n, g + 1))
                dve.tensor_scalar(poly[g % 2][:, :, :], poly[g % 2][:, :, :], 0.044715, 1.0, ALU.mult, ALU.add)\
                   .then_inc(poly_done.sem, 1)

            def gelu(n, par, g):
                dve.wait_ge(tanh_done.sem, tanh_done.at(n, g + 1))
                if g == 0:
                    dve.wait_ge(out_ps.sem, out_ps.all(n - 2))
                dve.scalar_tensor_tensor(hid[par][:, g * CT:(g + 1) * CT, :], tanh[g % 2][:, :, :], 1.0,
                                         pre[g % 2][:, :, :], ALU.add, ALU.mult).then_inc(hid_done.sem, 1)

            def hidden(n, par):
                for g in range(GROUPS + 1):
                    if g < GROUPS:
                        square(n, g)
                    if g >= 1:
                        gelu(n, par, g - 1)

            def back(n, par):
                dve.wait_ge(out_ps.sem, out_ps.all(n))
                dve.wait_ge(biased.sem, biased.all(n))
                dve.scalar_tensor_tensor(x[par][:, :, :], ps_out[:, :, :], 0.5, x[par][:, :, :], ALU.mult, ALU.add)\
                   .then_inc(x_added.sem, 1)

            def first():
                norm(0, 0)
                hidden(0, 0)

            def step(n, par):
                norm(n + 1, 1 - par)
                back(n, par)
                hidden(n + 1, 1 - par)

            over_batches(dve, first, step, back)

        @block.gpsimd
        def _(pool):
            pool.wait_ge(consts_done.sem, 1)
            pool.wait_ge(weights_in.sem, 16 * 6)

            def front(n, par):
                ln.gpsimd_rstd(pool, n)
                pool.wait_ge(ln.normed_done.sem, ln.normed_done.all(n))
                pool.tensor_tensor(x[par][:, :, :], x[par][:, :, :],
                                   b2[:, :].unsqueeze(1).broadcast_to([P, TT, C]), ALU.add).then_inc(biased.sem, 1)
                for g in range(GROUPS):
                    pool.wait_ge(poly_done.sem, poly_done.at(n, g + 1))
                    pool.tensor_tensor(poly[g % 2][:, :, :], poly[g % 2][:, :, :], pre[g % 2][:, :, :], ALU.mult)\
                        .then_inc(cube_done.sem, 1)

            over_batches(pool, lambda: front(0, 0), lambda n, par: front(n + 1, 1 - par), lambda n, par: None)

        @block.scalar
        def _(act):
            grant(act, [ln.out_done, pre_done, tanh_done])
            act.wait_ge(weights_in.sem, 16 * 6)

            def pre_copy(n, g):
                act.wait_ge(hid_ps.sem, hid_ps.at(n, g + 1))
                act.wait_ge(hid_done.sem, hid_done.at(n, g - 1))
                for c in range(CT):
                    r = act.activation(pre[g % 2][:, c, :], ps_hid[g % 2][:, c, :], ACT.Identity,
                                       bias=b1[:, g * CT + c:g * CT + c + 1])
                r.then_inc(pre_done.sem, 1)

            def tanhs(n, g):
                act.wait_ge(cube_done.sem, cube_done.at(n, g + 1))
                act.activation(tanh[g % 2][:, :, :], poly[g % 2][:, :, :], ACT.Tanh, scale=0.7978845608028654)\
                   .then_inc(tanh_done.sem, 1)

            def front(n):
                ln.scalar_out(act, n)
                for g in range(GROUPS + 1):
                    if g < GROUPS:
                        pre_copy(n, g)
                    if g >= 1:
                        tanhs(n, g - 1)

            over_batches(act, lambda: front(0), lambda n, par: front(n + 1), lambda n, par: None)

        @block.tensor
        def _(pe):
            grant(pe, [ln.turned_done, hid_ps, out_ps])
            pe.wait_ge(weights_in.sem, 16 * 6)

            def hidden(n):
                for g in range(GROUPS):
                    if g == 0:
                        pe.wait_ge(ln.out_done.sem, ln.out_done.all(n))
                    pe.wait_ge(pre_done.sem, pre_done.at(n, g - 1))
                    for m in range(CT):
                        for c in range(CT):
                            r = pe.matmul(ps_hid[g % 2][:, m, :], w1[:, c, (g * CT + m) * P:(g * CT + m + 1) * P],
                                          lnT[:, c, :], start=c == 0, stop=c == CT - 1)
                    r.then_inc(hid_ps.sem, 1)

            def back(n, par):
                pe.wait_ge(x_added.sem, x_added.all(n - 1))
                for k in range(FF // P):
                    if k % CT == 0:
                        pe.wait_ge(hid_done.sem, hid_done.at(n, k // CT + 1))
                    for t in range(TT):
                        r = pe.matmul(ps_out[:, t, :], hid[par][:, k, t * P:(t + 1) * P], w2[:, k, :],
                                      start=k == 0, stop=k == FF // P - 1)
                r.then_inc(out_ps.sem, 1)

            def first():
                ln.tensor_turn(pe, 0)
                hidden(0)

            def step(n, par):
                ln.tensor_turn(pe, n + 1)
                back(n, par)
                hidden(n + 1)

            over_batches(pe, first, step, back)


def build(nc, ins, out, scratch):
    held = []
    xs, v_rows = scratch
    ctx_rows = ins["ctx"]
    first_state = ctx_rows[:, 2:2 + S, :].rearrange("b s c -> b (s c)").rearrange("b (p s) -> b p s", s=S)
    time_mix(nc, held, ins["x"], xs[0], first_state, v_rows, ins)
    end_phase(nc, held)
    channel_mix(nc, held, xs[0], xs[1], ins)
    end_phase(nc, held)
    attention(nc, held, "sa", xs[1], xs[2], None, ins["mask_1x1xSxS2_fc1"],
              {"vecs": ins["sa_vecs"], "fixed": ins["fixed"], "q": ins["sa_q"], "k": ins["sa_k"], "v": ins["sa_v"],
               "o": ins["sa_o"], "bo": ins["b_ao"]}, False)
    end_phase(nc, held)
    attention(nc, held, "ca", xs[2], xs[3], ins["ctxT"], ins["mask_Bx1xSxS2_ff1"],
              {"vecs": ins["ca_vecs"], "fixed": ins["fixed"], "q": ins["ca_q"], "k": ins["ca_k"], "v": ins["ca_v"],
               "o": ins["ca_o"], "bo": ins["b_co"]}, True)
    end_phase(nc, held)
    mlp(nc, held, xs[3], out, {"vecs": ins["ff_vecs"], "fixed": ins["fixed"], "w1": ins["w1"], "w2": ins["w2"],
                         "b1": ins["b1"], "b2": ins["b2"]})


def fixed_matrices():
    import numpy as np
    k = np.arange(P)
    same_head = (k[:, None] // S == k[None, :] // S).astype(np.float32)
    eye = np.eye(P, dtype=np.float32)
    centre = eye - same_head / S
    fixed = np.stack([eye, same_head, centre], axis=1)
    pick = np.stack([same_head * ((k[None, :] % S == s) - 1.0 / S) for s in range(S)], axis=1).astype(np.float32)
    head_sum = np.zeros((P, CT, C // S), np.float32)
    for c in range(CT):
        head_sum[k, c, c * HT + k // S] = 1.0 / S
    head_out = np.ascontiguousarray((head_sum > 0).astype(np.float32).transpose(2, 1, 0))
    return {"fixed": fixed, "pick": pick, "head_sum": head_sum, "head_out": head_out}


def layouts(inputs):
    import numpy as np
    a = {k: np.asarray(v) for k, v in inputs.items()}

    def rows(w):
        return np.ascontiguousarray(w.reshape(-1, P, w.shape[1]).transpose(1, 0, 2))

    def columns(*vs):
        return np.ascontiguousarray(np.stack([v.reshape(-1, P).T for v in vs], axis=1))

    t, u = "L0_xattn_", "L1_xattn_"
    out = {"x": a["x"], "ctx": a["ctx_2048"], "ctxT": np.ascontiguousarray(a["ctx_2048"].transpose(0, 2, 1)),
           "mask_1x1xSxS2_fc1": a["mask_1x1xSxS2_fc1"], "mask_Bx1xSxS2_ff1": a["mask_Bx1xSxS2_ff1"]}
    for w in ("Wr", "Wk", "Wv", "Wg", "Wo", "fWk", "fWr", "fWv"):
        out[w] = rows(a[t + w].T)
    for i in range(2):
        out[f"prev{i}"] = np.ascontiguousarray(a["ctx_2048"][:, i].reshape(B, CT, P).transpose(2, 0, 1))
    out["maa_w1"], out["decay_w1"] = rows(a[t + "maa_w1"]), rows(a[t + "decay_w1"])
    out["maa_w2"] = np.ascontiguousarray(a[t + "maa_w2"].reshape(5 * DM, C))
    out["decay_w2"] = a[t + "decay_w2"]
    out["time_vecs"] = columns(*[a[t + v].reshape(C) for v in TIME_VECS])
    out["chan_vecs"] = columns(*[a[t + v] for v in CHAN_VECS])
    for p, w, b, ln in (("sa", a[u + "w_qkv"], a[u + "b_qkv"], "ln1"),
                        ("ca", np.concatenate([a[u + "w_q"], a[u + "w_kv"]], axis=1),
                         np.concatenate([a[u + "b_q"], a[u + "b_kv"]]), "ln2")):
        for i, f in enumerate("qkv"):
            out[f"{p}_{f}"] = rows(w[:, i * C:(i + 1) * C])
        out[f"{p}_vecs"] = columns(a[f"{u}{ln}_s"], a[f"{u}{ln}_b"], *[b[i * C:(i + 1) * C] for i in range(3)])
    out["sa_o"], out["ca_o"] = rows(a[u + "w_ao"]), rows(a[u + "w_co"])
    out["b_ao"], out["b_co"] = a[u + "b_ao"], a[u + "b_co"]
    out["ff_vecs"] = columns(a[u + "ln3_s"], a[u + "ln3_b"])
    out["w1"], out["w2"] = rows(a[u + "w1"]), rows(a[u + "w2"])
    out["b1"] = np.ascontiguousarray(a[u + "b1"].reshape(-1, P).T)
    out["b2"] = a[u + "b2"]
    out.update(fixed_matrices())
    return out


def kernel(**inputs):
    import numpy as np
    import concourse.bacc as bacc
    from concourse.bass_utils import run_bass_kernel_spmd as run

    nc = bacc.Bacc("TRN2", target_bir_lowering=False, num_devices=1)
    arrays, ins = {}, {}
    for name, a in layouts(inputs).items():
        arrays[f"in_{name}"] = a
        ins[name] = nc.dram_tensor(f"in_{name}", a.shape, mybir.dt.from_np(a.dtype), kind="ExternalInput").ap()
    out = nc.dram_tensor("out_0", (B, L, C), F32, kind="ExternalOutput").ap()
    xs = [nc.dram_tensor(f"x_stage{i}", (B, L, C), F32, kind="Internal").ap() for i in range(4)]
    v_rows = [nc.dram_tensor(f"v_rows{i}", (C, L), F32, kind="Internal").ap() for i in range(2)]
    build(nc, ins, out, (xs, v_rows))
    r = run(nc, [arrays], core_ids=[0])
    return r.results[0]["out_0"]
```

```python
from contextlib import ExitStack

import concourse.bass as bass
from concourse import mybir

F32 = mybir.dt.float32
F32R = mybir.dt.float32r
ALU = mybir.AluOpType
ACT = mybir.ActivationFunctionType
AX = mybir.AxisListType

P = 128
B = 8
L = 256
C = 512
CT = C // P
TT = L // P
S = 16
HT = P // S
NH = 16
HD = C // NH
HC = P // HD
DM = 32
DD = 64
FF = 4 * C
EPS = 1e-5
UNITS = 8
UW = S // 2
RING = 4

TIME_VECS = ["ln1_w", "ln1_b", "maa_x", "maa_w", "maa_k", "maa_v", "maa_r", "maa_g",
             "time_decay", "faaaa", "gn_w", "gn_b"]
CHAN_VECS = ["ln2_w", "ln2_b", "fmaa_k", "fmaa_r"]


class Count:

    def __init__(self, sem, per, ahead=0):
        self.sem, self.per, self.ahead = sem, per, ahead

    def at(self, n, k):
        return (n + self.ahead) * self.per + k

    def all(self, n):
        return (n + self.ahead + 1) * self.per


def counter(held, nc, phase):
    def make(name, per, ahead=0):
        held.append(nc.alloc_semaphore(name=f"{phase}_{name}"))
        return Count(held[-1], per, ahead)
    return make


def end_phase(nc, held):
    nc.clear_and_free_semaphores(held)
    nc.all_engine_barrier()
    held.clear()


def grant(eng, counts):
    for c in counts:
        if c.ahead:
            eng.sem_inc(c.sem, c.ahead * c.per)


def over_batches(eng, first, step, last):
    first()
    with eng.Fori(0, B // 2 - 1) as i:
        for par in range(2):
            step(i * 2 + par, par)
    step(B - 2, 0)
    last(B - 1, 1)


def over_three_stages(eng, start, step, finish):
    start()
    step(0, 0, False, True)
    with eng.Fori(0, B // 2 - 1) as i:
        for par in (1, 0):
            step(i * 2 + (2 - par), par, True, True)
    step(B - 1, 1, True, False)
    finish(B - 1)


class LayerNorm:

    def __init__(self, ctx, nc, name, sem, x, x_loaded, turned, turned_free, out, out_free, scale, shift, ident, half,
                 passed, parts=1):
        sb = lambda tile, shape: ctx.enter_context(nc.sbuf_tensor(f"{name}_ln_{tile}", shape, F32))
        self.nc, self.x, self.x_loaded, self.passed = nc, x, x_loaded, passed
        self.turned, self.turned_free, self.out, self.out_free = turned, turned_free, out, out_free
        self.scale, self.shift, self.ident, self.half = scale, shift, ident, half
        self.stats = sb("stats", [P, TT, 6])
        self.moments = sb("moments", [P, TT, 2])
        self.var = sb("var", [P, TT])
        self.rstd = sb("rstd", [P, TT])
        self.normed = sb("normed", [P, TT, C])
        self.stats_done = sem("ln_stats_done", 1, 1)
        self.moments_done = sem("ln_moments_done", 1)
        self.var_done = sem("ln_var_done", 1)
        self.rstd_done = sem("ln_rstd_done", 1)
        self.normed_done = sem("ln_normed_done", 1)
        self.parts = parts
        self.turned_done = sem("ln_turned_done", parts, 1)
        self.out_done = sem("ln_out_done", parts)

    def vector_moments(self, dve, n, par):
        dve.wait_ge(self.x_loaded.sem, self.x_loaded.all(n))
        for t in range(TT):
            r = dve.bn_stats(self.stats[:, t, :], self.x[par][:, t, :])
        r.then_inc(self.stats_done.sem, 1)
        dve.wait_ge(self.stats_done.sem, self.stats_done.all(n))
        dve.sem_inc(self.passed.sem, 1)
        for t in range(TT):
            r = dve.bn_aggr(self.moments[:, t, :], self.stats[:, t, :])
        r.then_inc(self.moments_done.sem, 1)
        dve.wait_ge(self.moments_done.sem, self.moments_done.all(n))
        dve.tensor_scalar(self.var[:, :], self.moments[:, :, 1], EPS, None, ALU.add).then_inc(self.var_done.sem, 1)

    def gpsimd_rstd(self, pool, n):
        pool.wait_ge(self.var_done.sem, self.var_done.all(n))
        pool.tensor_tensor(self.rstd[:, :], self.var[:, :], self.half[:, 0:TT], ALU.pow).then_inc(self.rstd_done.sem, 1)

    def vector_normalise(self, dve, n, par):
        dve.wait_ge(self.rstd_done.sem, self.rstd_done.all(n))
        dve.wait_ge(self.turned_done.sem, self.turned_done.all(n - 1))
        for t in range(TT):
            r = dve.tensor_scalar(self.normed[:, t, :], self.x[par][:, t, :], self.moments[:, t, 0:1],
                                  self.rstd[:, t:t + 1], ALU.subtract, ALU.mult)
        r.then_inc(self.normed_done.sem, 1)

    def channels(self, part):
        return range(part * CT // self.parts, (part + 1) * CT // self.parts)

    def tensor_turn(self, pe, n, part=0):
        pe.wait_ge(self.normed_done.sem, self.normed_done.all(n))
        self.turned_free(pe, n, part)
        for t in range(TT):
            for c in self.channels(part):
                r = pe.transpose(self.turned[:, c, t * P:(t + 1) * P], self.normed[:, t, c * P:(c + 1) * P],
                                 self.ident)
        r.then_inc(self.turned_done.sem, 1)

    def scalar_out(self, act, n, part=0, before=None):
        act.wait_ge(self.turned_done.sem, self.turned_done.at(n, part + 1))
        self.out_free(act, n)
        if before:
            tile, prev = before
            act.activation(tile[:, :, 0], prev[:, n, :], ACT.Copy)
        for c in self.channels(part):
            r = act.activation(self.out(c), self.turned[:, c, :], ACT.Identity,
                               bias=self.shift[:, c:c + 1], scale=self.scale[:, c:c + 1])
        r.then_inc(self.out_done.sem, 1)


def time_mix(nc, held, x_in, x_out, first_state, v_rows, weights):
    with ExitStack() as ctx:
        def sb(name, shape):
            return ctx.enter_context(nc.sbuf_tensor(f"tm_{name}", shape, F32))

        sem = counter(held, nc, "tm")

        w_proj = {f: sb(f"w_{f}", [P, CT, C]) for f in "vkrgo"}
        w_mix1 = sb("w_mix1", [P, CT, 5 * DM])
        w_mix2 = sb("w_mix2", [P, C])
        w_mix2g = sb("w_mix2g", [DM, C])
        w_dec1 = sb("w_dec1", [P, CT, DD])
        w_dec2 = sb("w_dec2", [DD, C])
        vecs = sb("vecs", [P, len(TIME_VECS), CT])
        fixed = sb("fixed", [P, 3, P])
        pick = sb("pick", [P, S, P])
        head_sum = sb("head_sum", [P, CT, C // S])
        head_out = sb("head_out", [C // S, CT, P])
        prev = sb("prev", [P, B, CT])
        half = sb("half", [P, TT])
        eps = sb("eps", [P, 1])
        vec = {name: vecs[:, i, :] for i, name in enumerate(TIME_VECS)}
        ident, head_ones, centre = fixed[:, 0, :], fixed[:, 1, :], fixed[:, 2, :]

        x = [sb(f"x{i}", [P, TT, C]) for i in range(2)]
        res = sb("res", [P, TT, C])
        xa = sb("xa", [P, CT, L + 1])
        shift = sb("shift", [P, CT, L])
        mixed = [sb(f"mixed{i}", [P, CT, L]) for i in range(2)]
        mix_act = sb("mix_act", [P, L])
        mix_actg = sb("mix_actg", [DM, L])
        dec_act = sb("dec_act", [DD, L])
        decay_e = sb("decay_e", [P, CT, L])
        wT = [sb(f"wT{i}", [P, CT, L]) for i in range(2)]
        kT = [sb(f"kT{i}", [P, CT, L + 1]) for i in range(2)]
        vT = sb("vT", [P, CT, L + 1])
        rT = [sb(f"rT{i}", [P, CT, L]) for i in range(2)]
        gT = [sb(f"gT{i}", [P, CT, L]) for i in range(2)]
        g_half = sb("g_half", [P, CT, L])
        rkf = sb("rkf", [P, CT, L])
        now = sb("now", [P, CT, L])
        s0 = [sb(f"s0_{i}", [P, CT, S]) for i in range(2)]
        unit = [sb(f"unit{i}", [P, UW, L]) for i in range(RING)]
        y_sb = sb("y_sb", [P, CT, L])
        y_sq = decay_e
        head_rstd = sb("head_rstd", [C // S, L])
        yg = sb("yg", [P, CT, L])
        bank = [ctx.enter_context(nc.psum_tensor(f"tm_ps{i}", [P, CT, L], F32)) for i in range(4)]
        ps_turn, ps_mix, ps_proj, ps_y = bank

        weights_in = sem("weights_in", 0)
        passed = sem("passed", 0)
        first_in = sem("first_in", 0)
        proj_in = sem("proj_in", 0)
        x_loaded = sem("x_loaded", 16)
        res_loaded = sem("res_loaded", 16)
        s0_loaded = sem("s0_loaded", 16)
        v_stored = sem("v_stored", 16, 1)
        unit_loaded = [sem(f"unit{r}_loaded", 16 * UNITS // RING) for r in range(RING)]
        x_stored = sem("x_stored", 16, 1)
        consts_done = sem("consts_done", 0)
        shift_done = sem("shift_done", 1)
        mix_in_done = sem("mix_in_done", 1)
        mix_hidden = sem("mix_hidden", 1)
        mix_acted = sem("mix_acted", 1)
        mix_ps = sem("mix_ps", 5)
        mix_scaled = sem("mix_scaled", 5, 1)
        mix_added = sem("mix_added", 5, 1)
        dec_hidden = sem("dec_hidden", 1)
        dec_acted = sem("dec_acted", 1)
        proj_ps = sem("proj_ps", 5, 1)
        proj_out = sem("proj_out", 5, 1)
        decay_exp = sem("decay_exp", 1)
        g_done = sem("g_done", 1, 1)
        rkf_done = sem("rkf_done", 1)
        now_ps = sem("now_ps", 1, 1)
        now_done = sem("now_done", 1, 1)
        kv_done = sem("kv_done", UNITS, 2)
        scanned = sem("scanned", UNITS)
        read_out = sem("read_out", UNITS, 2)
        unit_summed = sem("unit_summed", UNITS, 1)
        y_copied = sem("y_copied", 1, 1)
        y_squared = sem("y_squared", 1)
        var_ps = sem("var_ps", 1)
        std_done = sem("std_done", 1, 2)
        rstd_done = sem("rstd_done", 1)
        rstd_ps = sem("rstd_ps", 1)
        y_normed = sem("y_normed", 1, 2)
        y_scaled = sem("y_scaled", 1)
        yg_done = sem("yg_done", 1, 2)
        out_ps = sem("out_ps", 1)
        x_added = sem("x_added", 1, 3)

        def turn_free(eng, n, _):
            eng.wait_ge(now_done.sem, now_done.all(n - 1))

        def xa_free(eng, n):
            eng.wait_ge(mix_added.sem, mix_added.all(n - 1))

        ln = LayerNorm(ctx, nc, "tm", sem, x, x_loaded, ps_turn, turn_free, lambda c: xa[:, c, 1:L + 1], xa_free,
                       vec["ln1_w"], vec["ln1_b"], ident, half, passed)

        ORDER = ["maa_v", "maa_k", "maa_r", "maa_w", "maa_g"]
        ln.normed_done.ahead = 2
        ROW = {"maa_w": 0, "maa_k": 1, "maa_v": 2, "maa_r": 3, "maa_g": 4}

        block = ctx.enter_context(nc.Block())

        @block.sync
        def _(sp):
            grant(sp, [x_stored, v_stored])
            loads = [(fixed, "fixed"), (vecs, "time_vecs"), (prev, "prev1"), (w_mix1, "maa_w1")]
            for tile, name in loads:
                sp.dma_start(tile[:, :, :], weights[name]).then_inc(first_in.sem, 16)
            sp.dma_start(w_mix2[:, :], weights["maa_w2"][0:P, :]).then_inc(first_in.sem, 16)
            sp.dma_start(w_mix2g[:, :], weights["maa_w2"][P:P + DM, :]).then_inc(first_in.sem, 16)

            def load(n, par):
                sp.wait_ge(ln.stats_done.sem, ln.stats_done.all(n - 1))
                sp.sem_inc(passed.sem, 1)
                sp.wait_ge(ln.normed_done.sem, ln.normed_done.all(n - 2))
                sp.sem_inc(passed.sem, 1)
                sp.dma_start(x[par][:, :, :], x_in[n, :, :].rearrange("(t p) c -> p t c", p=P))\
                  .then_inc(x_loaded.sem, 16)
                sp.wait_ge(kv_done.sem, kv_done.all(n - 2))
                sp.sem_inc(passed.sem, 1)
                sp.dma_start(s0[par][:, :, :], first_state[n, :, :].rearrange("(c p) s -> p c s", p=P))\
                  .then_inc(s0_loaded.sem, 16)

            def store_v(n, par):
                sp.wait_ge(proj_out.sem, proj_out.at(n, 1))
                sp.dma_start(v_rows[par].rearrange("(c p) l -> p c l", p=P), vT[:, :, 0:L])\
                  .then_inc(v_stored.sem, 16)
                sp.wait_ge(v_stored.sem, v_stored.all(n))
                sp.sem_inc(passed.sem, 1)

            def load_unit(n, par, u):
                sp.wait_ge(unit_summed.sem, unit_summed.at(n, u + 1 - RING))
                c, h = u // 2, u % 2
                rows = v_rows[par].rearrange("(h s) l -> h (s l)", s=S)
                src = rows[c * HT:(c + 1) * HT, h * UW * L:(h + 1) * UW * L]
                sp.dma_start(unit[u % RING][:, :, :].rearrange("p s l -> p (s l)"),
                             src.unsqueeze(1).broadcast_to([HT, S, UW * L])).then_inc(unit_loaded[u % RING].sem, 16)

            def load_residual(n):
                sp.wait_ge(x_stored.sem, x_stored.all(n - 1))
                sp.sem_inc(passed.sem, 1)
                sp.dma_start(res[:, :, :], x_in[n, :, :].rearrange("(t p) c -> p t c", p=P))\
                  .then_inc(res_loaded.sem, 16)

            def start():
                load(0, 0)
                for tile, name in [(w_proj["v"], "Wv"), (w_proj["k"], "Wk"), (w_proj["r"], "Wr"),
                                   (w_dec1, "decay_w1")]:
                    sp.dma_start(tile[:, :, :], weights[name]).then_inc(proj_in.sem, 16)
                sp.dma_start(w_dec2[:, :], weights["decay_w2"]).then_inc(proj_in.sem, 16)
                for tile, name in [(w_proj["g"], "Wg"), (pick, "pick"), (head_sum, "head_sum"), (w_proj["o"], "Wo"),
                                   (head_out, "head_out")]:
                    sp.dma_start(tile[:, :, :], weights[name]).then_inc(weights_in.sem, 16)
                store_v(0, 0)
                for u in range(RING - 1):
                    load_unit(0, 0, u)

            def step(n, par, prev_batch, next_batch):
                if next_batch:
                    load(n + 1, 1 - par)
                if prev_batch:
                    load_residual(n - 1)
                for u in range(RING - 1, UNITS):
                    load_unit(n, par, u)
                if next_batch:
                    store_v(n + 1, 1 - par)
                    for u in range(RING - 1):
                        load_unit(n + 1, 1 - par, u)

            def finish(n):
                load_residual(n)
                sp.wait_ge(x_stored.sem, x_stored.all(n))

            over_three_stages(sp, start, step, finish)

        @block.vector
        def _(dve):
            dve.memset(half[:, :], -0.5).then_inc(consts_done.sem, 1)
            dve.memset(eps[:, :], EPS).then_inc(consts_done.sem, 1)
            dve.memset(kT[0][:, :, 0:1], 0.0).then_inc(consts_done.sem, 1)
            dve.memset(kT[1][:, :, 0:1], 0.0).then_inc(consts_done.sem, 1)
            dve.memset(vT[:, :, 0:1], 0.0).then_inc(consts_done.sem, 1)
            grant(dve, [ln.stats_done, ln.normed_done, mix_scaled, read_out, now_done, g_done, yg_done, x_added, y_normed])
            dve.wait_ge(first_in.sem, 16 * 6)

            def shifts(n, par):
                dve.wait_ge(ln.out_done.sem, ln.out_done.all(n))
                dve.tensor_tensor(shift[:, :, :], xa[:, :, 0:L], xa[:, :, 1:L + 1], ALU.subtract)\
                   .then_inc(shift_done.sem, 1)
                dve.wait_ge(shift_done.sem, shift_done.all(n))
                dve.wait_ge(proj_ps.sem, proj_ps.all(n - 1))
                for c in range(CT):
                    r = dve.scalar_tensor_tensor(mixed[1][:, c, :], shift[:, c, :], vec["maa_x"][:, c:c + 1],
                                                 xa[:, c, 1:L + 1], ALU.mult, ALU.add)
                r.then_inc(mix_in_done.sem, 1)

            def mix(n, j):
                dve.wait_ge(mix_ps.sem, mix_ps.at(n, j + 1))
                if j >= 2:
                    dve.wait_ge(proj_ps.sem, proj_ps.at(n, j - 1))
                for c in range(CT):
                    r = dve.scalar_tensor_tensor(mixed[j % 2][:, c, :], ps_mix[:, c, :], vec[ORDER[j]][:, c:c + 1],
                                                 shift[:, c, :], ALU.add, ALU.mult)
                r.then_inc(mix_scaled.sem, 1)

            def silu(n, par):
                dve.wait_ge(proj_out.sem, proj_out.at(n, 5))
                dve.scalar_tensor_tensor(gT[par][:, :, :], gT[par][:, :, :], 1.0, g_half[:, :, :], ALU.add, ALU.mult)\
                   .then_inc(g_done.sem, 1)

            def rkf_part(n, par):
                dve.wait_ge(proj_out.sem, proj_out.at(n, 3))
                dve.wait_ge(now_ps.sem, now_ps.all(n - 1))
                for c in range(CT):
                    r = dve.scalar_tensor_tensor(rkf[:, c, :], kT[par][:, c, 1:L + 1], vec["faaaa"][:, c:c + 1],
                                                 rT[par][:, c, :], ALU.mult, ALU.mult)
                r.then_inc(rkf_done.sem, 1)

            def now_part(n, par):
                dve.wait_ge(now_ps.sem, now_ps.all(n))
                dve.wait_ge(unit_summed.sem, unit_summed.at(n - 1, UNITS - 1))
                dve.tensor_tensor(now[:, :, :], ps_turn[:, :, :], vT[:, :, 1:L + 1], ALU.mult)\
                   .then_inc(now_done.sem, 1)

            def unit_part(n, par, u):
                c = u // 2
                dve.wait_ge(kv_done.sem, kv_done.at(n, u + 1))
                if u == 0:
                    dve.wait_ge(decay_exp.sem, decay_exp.all(n))
                buf = unit[u % RING]
                for s in range(UW):
                    r = dve.tensor_tensor_scan(buf[:, s, 1:L], wT[par][:, c, 0:L - 1], buf[:, s, 1:L],
                                               buf[:, s, 0:1], ALU.mult, ALU.add)
                r.then_inc(scanned.sem, 1)
                dve.wait_ge(scanned.sem, scanned.at(n, u + 1))
                dve.tensor_tensor(buf[:, :, :], buf[:, :, :],
                                  rT[par][:, c, :].unsqueeze(1).broadcast_to([P, UW, L]), ALU.mult)\
                   .then_inc(read_out.sem, 1)

            def norm_rstd(n):
                dve.wait_ge(std_done.sem, std_done.all(n))
                dve.reciprocal(head_rstd[:, :], head_rstd[:, :]).then_inc(rstd_done.sem, 1)

            def norm_apply(n):
                dve.wait_ge(rstd_ps.sem, rstd_ps.all(n))
                dve.tensor_tensor(y_sb[:, :, :], y_sb[:, :, :], ps_turn[:, :, :], ALU.mult).then_inc(y_normed.sem, 1)

            def gate(n, par):
                dve.wait_ge(y_scaled.sem, y_scaled.all(n))
                dve.wait_ge(g_done.sem, g_done.all(n))
                dve.tensor_tensor(yg[:, :, :], y_sb[:, :, :], gT[par][:, :, :], ALU.mult).then_inc(yg_done.sem, 1)

            def residual(n):
                dve.wait_ge(out_ps.sem, out_ps.all(n))
                dve.wait_ge(res_loaded.sem, res_loaded.all(n))
                dve.tensor_tensor(res[:, :, :], res[:, :, :],
                                  ps_mix[:, :, :].rearrange("p (t a) l -> p t (a l)", t=TT), ALU.add)\
                   .then_inc(x_added.sem, 1)

            def start():
                ln.vector_moments(dve, 0, 0)
                ln.vector_normalise(dve, 0, 0)
                shifts(0, 0)
                for j in range(5):
                    mix(0, j)
                rkf_part(0, 0)
                now_part(0, 0)

            def step(n, par, prev_batch, next_batch):
                for u in range(UNITS):
                    if next_batch:
                        if u == 0:
                            ln.vector_moments(dve, n + 1, 1 - par)
                        if u >= 3:
                            mix(n + 1, u - 3)
                        if u == 7:
                            rkf_part(n + 1, 1 - par)
                    if prev_batch:
                        if u == 3:
                            norm_rstd(n - 1)
                        if u == 4:
                            norm_apply(n - 1)
                        if u == 5:
                            gate(n - 1, 1 - par)
                    unit_part(n, par, u)
                    if next_batch:
                        if u == 0:
                            ln.vector_normalise(dve, n + 1, 1 - par)
                        if u == 1:
                            shifts(n + 1, 1 - par)
                        if u == 7:
                            now_part(n + 1, 1 - par)
                    if u == 2:
                        silu(n, par)
                    if prev_batch and u == 7:
                        residual(n - 1)

            def finish(n):
                norm_rstd(n)
                norm_apply(n)
                gate(n, n % 2)
                residual(n)

            over_three_stages(dve, start, step, finish)

        @block.gpsimd
        def _(pool):
            grant(pool, [mix_added, kv_done])
            pool.wait_ge(consts_done.sem, 5)

            def add(n, j):
                pool.wait_ge(mix_scaled.sem, mix_scaled.at(n, j + 1))
                pool.tensor_tensor(mixed[j % 2][:, :, :], mixed[j % 2][:, :, :], xa[:, :, 1:L + 1], ALU.add)\
                    .then_inc(mix_added.sem, 1)

            def unit_part(n, par, u):
                c, h = u // 2, u % 2
                buf = unit[u % RING]
                pool.wait_ge(unit_loaded[u % RING].sem, unit_loaded[u % RING].at(n, 16 * (u // RING + 1)))
                if u == 0:
                    pool.wait_ge(proj_out.sem, proj_out.at(n, 2))
                    pool.wait_ge(s0_loaded.sem, s0_loaded.all(n))
                pool.tensor_tensor(buf[:, :, 1:L], buf[:, :, 1:L],
                                   kT[par][:, c, 1:L].unsqueeze(1).broadcast_to([P, UW, L - 1]), ALU.mult)
                pool.tensor_copy(buf[:, :, 0:1], s0[par][:, c, h * UW:(h + 1) * UW].unsqueeze(2))\
                    .then_inc(kv_done.sem, 1)

            def start():
                ln.gpsimd_rstd(pool, 0)
                for j in range(5):
                    add(0, j)

            def step(n, par, prev_batch, next_batch):
                unit_part(n, par, 0)
                for u in range(UNITS):
                    if next_batch and u == 0:
                        ln.gpsimd_rstd(pool, n + 1)
                    if u + 1 < UNITS:
                        unit_part(n, par, u + 1)
                    if next_batch and u >= 3:
                        add(n + 1, u - 3)

            over_three_stages(pool, start, step, lambda n: None)

        @block.scalar
        def _(act):
            grant(act, [proj_out, std_done, y_copied])
            act.wait_ge(first_in.sem, 16 * 6)
            act.wait_ge(consts_done.sem, 5)

            def mix_tanh(n):
                act.wait_ge(mix_hidden.sem, mix_hidden.all(n))
                act.activation(mix_act[:, :], ps_turn[:, 0, :], ACT.Tanh)
                act.activation(mix_actg[:, :], ps_turn[0:DM, 1, :], ACT.Tanh).then_inc(mix_acted.sem, 1)

            def v_out(n, par):
                act.wait_ge(proj_ps.sem, proj_ps.at(n, 1))
                act.wait_ge(now_done.sem, now_done.all(n - 1))
                act.wait_ge(v_stored.sem, v_stored.all(n - 1))
                act.wait_ge(read_out.sem, read_out.all(n - 2))
                act.activation(vT[:, :, 1:L + 1], ps_proj[:, :, :], ACT.Copy).then_inc(proj_out.sem, 1)

            def k_out(n, par):
                act.wait_ge(proj_ps.sem, proj_ps.at(n, 2))
                act.activation(kT[par][:, :, 1:L + 1], ps_proj[:, :, :], ACT.Copy).then_inc(proj_out.sem, 1)

            def r_out(n, par):
                act.wait_ge(proj_ps.sem, proj_ps.at(n, 3))
                act.activation(rT[par][:, :, :], ps_proj[:, :, :], ACT.Copy).then_inc(proj_out.sem, 1)

            def decay(n, par):
                act.wait_ge(dec_hidden.sem, dec_hidden.all(n))
                act.activation(dec_act[:, :], ps_proj[0:DD, 0, :], ACT.Tanh).then_inc(dec_acted.sem, 1)
                act.wait_ge(proj_ps.sem, proj_ps.at(n, 4))
                for c in range(CT):
                    r = act.activation(decay_e[:, c, :], ps_proj[:, c, :], ACT.Exp, bias=vec["time_decay"][:, c:c + 1])
                r.then_inc(proj_out.sem, 1)
                act.wait_ge(proj_out.sem, proj_out.at(n, 4))
                act.activation(wT[par][:, :, :], decay_e[:, :, :], ACT.Exp, scale=-1.0).then_inc(decay_exp.sem, 1)

            def g_out(n, par):
                act.wait_ge(proj_ps.sem, proj_ps.at(n, 5))
                act.wait_ge(yg_done.sem, yg_done.all(n - 2))
                act.wait_ge(g_done.sem, g_done.all(n - 1))
                act.activation(gT[par][:, :, :], ps_proj[:, :, :], ACT.Tanh, scale=0.5)
                act.activation(g_half[:, :, :], ps_proj[:, :, :], ACT.Copy, scale=0.5).then_inc(proj_out.sem, 1)

            def y_out(n):
                act.wait_ge(unit_summed.sem, unit_summed.all(n))
                act.wait_ge(yg_done.sem, yg_done.all(n - 1))
                act.activation(y_sb[:, :, :], ps_y[:, :, :], ACT.Copy).then_inc(y_copied.sem, 1)

            def y_square(n, later):
                act.wait_ge(y_copied.sem, y_copied.all(n))
                act.wait_ge(decay_exp.sem, decay_exp.all(n + later))
                act.activation(y_sq[:, :, :], y_sb[:, :, :], ACT.Square).then_inc(y_squared.sem, 1)

            def norm_std(n):
                act.wait_ge(var_ps.sem, var_ps.all(n))
                act.activation(head_rstd[:, :], ps_proj[0:C // S, 0, :], ACT.Sqrt, bias=eps[0:C // S, 0:1])\
                   .then_inc(std_done.sem, 1)

            def store(n):
                act.wait_ge(x_added.sem, x_added.all(n))
                act.sem_inc(passed.sem, 1)
                act.dma_start(x_out[n, :, :].rearrange("(t p) c -> p t c", p=P), res[:, :, :])\
                   .then_inc(x_stored.sem, 16)

            def norm_scale(n):
                act.wait_ge(y_normed.sem, y_normed.all(n))
                for c in range(CT):
                    r = act.activation(y_sb[:, c, :], y_sb[:, c, :], ACT.Identity,
                                       bias=vec["gn_b"][:, c:c + 1], scale=vec["gn_w"][:, c:c + 1])
                r.then_inc(y_scaled.sem, 1)

            def start():
                ln.scalar_out(act, 0, before=(xa, prev))
                mix_tanh(0)
                v_out(0, 0)
                k_out(0, 0)
                r_out(0, 0)
                decay(0, 0)

            def step(n, par, prev_batch, next_batch):
                if prev_batch:
                    y_square(n - 1, 1)
                g_out(n, par)
                if next_batch:
                    ln.scalar_out(act, n + 1, before=(xa, prev))
                if next_batch:
                    mix_tanh(n + 1)
                if prev_batch:
                    norm_std(n - 1)
                if next_batch:
                    v_out(n + 1, 1 - par)
                if prev_batch:
                    norm_scale(n - 1)
                if next_batch:
                    k_out(n + 1, 1 - par)
                    r_out(n + 1, 1 - par)
                    decay(n + 1, 1 - par)
                y_out(n)
                if prev_batch:
                    store(n - 1)

            def finish(n):
                y_square(n, 0)
                norm_std(n)
                norm_scale(n)
                store(n)

            over_three_stages(act, start, step, finish)

        @block.tensor
        def _(pe):
            grant(pe, [ln.turned_done, proj_ps, now_ps, unit_summed])
            pe.wait_ge(first_in.sem, 16 * 6)

            def hidden(n):
                pe.wait_ge(mix_in_done.sem, mix_in_done.all(n))
                pe.wait_ge(ln.out_done.sem, ln.out_done.all(n))
                for c in range(CT):
                    pe.matmul(ps_turn[:, 0, :], w_mix1[:, c, 0:P], mixed[1][:, c, :], start=c == 0, stop=c == CT - 1)
                for c in range(CT):
                    r = pe.matmul(ps_turn[0:DM, 1, :], w_mix1[:, c, P:P + DM], mixed[1][:, c, :],
                                  start=c == 0, stop=c == CT - 1)
                r.then_inc(mix_hidden.sem, 1)

            def mixer(n, j):
                if j == 0:
                    pe.wait_ge(mix_acted.sem, mix_acted.all(n))
                    pe.wait_ge(mix_scaled.sem, mix_scaled.all(n - 1))
                    pe.wait_ge(x_added.sem, x_added.all(n - 3))
                else:
                    pe.wait_ge(mix_scaled.sem, mix_scaled.at(n, j))
                row = ROW[ORDER[j]] * DM
                for c in range(CT):
                    if row < P:
                        w, a = w_mix2[row:row + DM, c * P:(c + 1) * P], mix_act[row:row + DM, :]
                    else:
                        w, a = w_mix2g[:, c * P:(c + 1) * P], mix_actg[:, :]
                    r = pe.matmul(ps_mix[:, c, :], w, a, start=True, stop=True)
                r.then_inc(mix_ps.sem, 1)

            def project(n, j, f):
                pe.wait_ge(mix_added.sem, mix_added.at(n, j + 1))
                if j == 0:
                    pe.wait_ge(std_done.sem, std_done.all(n - 2))
                else:
                    pe.wait_ge(proj_out.sem, proj_out.at(n, j))
                for m in range(CT):
                    for c in range(CT):
                        r = pe.matmul(ps_proj[:, m, :], w_proj[f][:, c, m * P:(m + 1) * P], mixed[j % 2][:, c, :],
                                      start=c == 0, stop=c == CT - 1)
                r.then_inc(proj_ps.sem, 1)

            def decay_hidden(n):
                pe.wait_ge(mix_added.sem, mix_added.at(n, 4))
                pe.wait_ge(proj_out.sem, proj_out.at(n, 3))
                for c in range(CT):
                    r = pe.matmul(ps_proj[0:DD, 0, :], w_dec1[:, c, :], mixed[1][:, c, :],
                                  start=c == 0, stop=c == CT - 1)
                r.then_inc(dec_hidden.sem, 1)

            def decay_out(n):
                pe.wait_ge(dec_acted.sem, dec_acted.all(n))
                for c in range(CT):
                    r = pe.matmul(ps_proj[:, c, :], w_dec2[:, c * P:(c + 1) * P], dec_act[:, :],
                                  start=True, stop=True)
                r.then_inc(proj_ps.sem, 1)

            def now_part(n):
                pe.wait_ge(rkf_done.sem, rkf_done.all(n))
                pe.wait_ge(mix_acted.sem, mix_acted.all(n))
                pe.wait_ge(y_normed.sem, y_normed.all(n - 2))
                for c in range(CT):
                    r = pe.matmul(ps_turn[:, c, :], head_ones, rkf[:, c, :], start=True, stop=True)
                r.then_inc(now_ps.sem, 1)

            def unit_part(n, u):
                c, h = u // 2, u % 2
                if u == 0:
                    pe.wait_ge(y_copied.sem, y_copied.all(n - 1))
                    pe.wait_ge(now_done.sem, now_done.all(n))
                if h == 0:
                    pe.matmul(ps_y[:, c, :], centre, now[:, c, :], start=True, stop=False)
                pe.wait_ge(read_out.sem, read_out.at(n, u + 1))
                for s in range(UW):
                    r = pe.matmul(ps_y[:, c, :], pick[:, h * UW + s, :], unit[u % RING][:, s, :],
                                  start=False, stop=h == 1 and s == UW - 1)
                r.then_inc(unit_summed.sem, 1)

            def variance(n, later):
                pe.wait_ge(y_squared.sem, y_squared.all(n))
                pe.wait_ge(proj_out.sem, proj_out.all(n + later))
                for c in range(CT):
                    r = pe.matmul(ps_proj[0:C // S, 0, :], head_sum[:, c, :], y_sq[:, c, :],
                                  start=c == 0, stop=c == CT - 1)
                r.then_inc(var_ps.sem, 1)

            def spread_rstd(n, later):
                pe.wait_ge(rstd_done.sem, rstd_done.all(n))
                if later == 2:
                    pe.wait_ge(mix_acted.sem, mix_acted.all(n + 2))
                else:
                    pe.wait_ge(now_done.sem, now_done.all(n + later))
                for c in range(CT):
                    r = pe.matmul(ps_turn[:, c, :], head_out[:, c, :], head_rstd[:, :], start=True, stop=True)
                r.then_inc(rstd_ps.sem, 1)

            def output(n, later):
                pe.wait_ge(yg_done.sem, yg_done.all(n))
                pe.wait_ge(mix_scaled.sem, mix_scaled.all(n + later))
                out = ps_mix[:, :, :].rearrange("p (t a) l -> p t (a l)", t=TT)
                for t in range(TT):
                    for c in range(CT):
                        r = pe.matmul(out[:, t, :], yg[:, c, t * P:(t + 1) * P], w_proj["o"][:, c, :],
                                      start=c == 0, stop=c == CT - 1)
                r.then_inc(out_ps.sem, 1)

            def start():
                ln.tensor_turn(pe, 0)
                hidden(0)
                mixer(0, 0)
                mixer(0, 1)
                pe.wait_ge(proj_in.sem, 16 * 5)
                for j in range(3):
                    project(0, j, "vkr"[j])
                    mixer(0, j + 2)
                decay_hidden(0)
                now_part(0)
                decay_out(0)
                pe.wait_ge(weights_in.sem, 16 * 5)

            def step(n, par, prev_batch, next_batch):
                for u in range(UNITS):
                    if u == 0:
                        project(n, 4, "g")
                    if u == 1:
                        if next_batch:
                            ln.tensor_turn(pe, n + 1)
                    if u == 2:
                        if next_batch:
                            hidden(n + 1)
                        if prev_batch:
                            variance(n - 1, 1)
                        if next_batch:
                            mixer(n + 1, 0)
                    if u == 3:
                        if next_batch:
                            mixer(n + 1, 1)
                        if prev_batch:
                            spread_rstd(n - 1, 2 if next_batch else 1)
                    if next_batch and u in (4, 5, 6):
                        project(n + 1, u - 4, "vkr"[u - 4])
                        mixer(n + 1, u - 2)
                    if u == 7:
                        if next_batch:
                            decay_hidden(n + 1)
                            now_part(n + 1)
                            decay_out(n + 1)
                        if prev_batch:
                            output(n - 1, 2 if next_batch else 1)
                    unit_part(n, u)

            def finish(n):
                variance(n, 0)
                spread_rstd(n, 0)
                output(n, 0)

            over_three_stages(pe, start, step, finish)


def channel_mix(nc, held, x_in, x_out, weights):
    with ExitStack() as ctx:
        def sb(name, shape):
            return ctx.enter_context(nc.sbuf_tensor(f"cm_{name}", shape, F32))

        sem = counter(held, nc, "cm")

        wk, wr, wv = (sb(f"w{f}", [P, CT, C]) for f in "krv")
        vecs = sb("vecs", [P, len(CHAN_VECS), CT])
        vec = {name: vecs[:, i, :] for i, name in enumerate(CHAN_VECS)}
        fixed = sb("fixed", [P, 3, P])
        prev = sb("prev", [P, B, CT])
        half = sb("half", [P, TT])
        x = [sb(f"x{i}", [P, TT, C]) for i in range(2)]
        xc = sb("xc", [P, CT, L + 1])
        shift = sb("shift", [P, CT, L])
        xk = [sb(f"xk{i}", [P, CT, L]) for i in range(2)]
        xr = [sb(f"xr{i}", [P, CT, L]) for i in range(2)]
        relu = sb("relu", [P, CT, L])
        kk = sb("kk", [P, CT, L])
        gate = sb("gate", [P, TT, C])
        gated = sb("gated", [P, TT, C])
        res = sb("res", [P, TT, C])
        ps_turn = ctx.enter_context(nc.psum_tensor("cm_ps_turn", [P, CT, L], F32))
        ps_k = ctx.enter_context(nc.psum_tensor("cm_ps_k", [P, CT, L], F32))
        ps_r = ctx.enter_context(nc.psum_tensor("cm_ps_r", [P, TT, C], F32))
        ps_v = ctx.enter_context(nc.psum_tensor("cm_ps_v", [P, TT, C], F32))

        first_in = sem("first_in", 0)
        w_in = {f: sem(f"w{f}_in", 0) for f in "krv"}
        passed = sem("passed", 0)
        consts_done = sem("consts_done", 0)
        x_loaded = sem("x_loaded", 16)
        res_loaded = sem("res_loaded", 16)
        x_stored = sem("x_stored", 16, 1)
        shift_done = sem("shift_done", 1)
        mixed_done = sem("mixed_done", 1, 1)
        k_ps = sem("k_ps", 1)
        r_ps = sem("r_ps", 1, 2)
        v_ps = sem("v_ps", 1, 1)
        relu_done = sem("relu_done", 1, 1)
        kk_done = sem("kk_done", 1, 1)
        gate_done = sem("gate_done", 1, 1)
        gated_done = sem("gated_done", 1, 1)
        x_added = sem("x_added", 1, 1)

        ln = LayerNorm(ctx, nc, "cm", sem, x, x_loaded, ps_turn,
                       lambda eng, n, _: eng.wait_ge(mixed_done.sem, mixed_done.all(n - 1)),
                       lambda c: xc[:, c, 1:L + 1],
                       lambda eng, n: eng.wait_ge(mixed_done.sem, mixed_done.all(n - 1)),
                       vec["ln2_w"], vec["ln2_b"], fixed[:, 0, :], half, passed)
        ln.normed_done.ahead = 2

        block = ctx.enter_context(nc.Block())

        @block.sync
        def _(sp):
            grant(sp, [x_stored])

            def load(n, par):
                sp.wait_ge(ln.stats_done.sem, ln.stats_done.all(n - 1))
                sp.sem_inc(passed.sem, 1)
                sp.wait_ge(ln.normed_done.sem, ln.normed_done.all(n - 2))
                sp.sem_inc(passed.sem, 1)
                sp.dma_start(x[par][:, :, :], x_in[n, :, :].rearrange("(t p) c -> p t c", p=P))\
                  .then_inc(x_loaded.sem, 16)

            def residual(n):
                sp.wait_ge(x_stored.sem, x_stored.all(n - 1))
                sp.sem_inc(passed.sem, 1)
                sp.dma_start(res[:, :, :], x_in[n, :, :].rearrange("(t p) c -> p t c", p=P))\
                  .then_inc(res_loaded.sem, 16)
                sp.wait_ge(x_added.sem, x_added.all(n))
                sp.sem_inc(passed.sem, 1)
                sp.dma_start(x_out[n, :, :].rearrange("(t p) c -> p t c", p=P), res[:, :, :])\
                  .then_inc(x_stored.sem, 16)

            def first():
                sp.dma_start(x[0][:, :, :], x_in[0, :, :].rearrange("(t p) c -> p t c", p=P))\
                  .then_inc(x_loaded.sem, 16)
                for tile, name in [(fixed, "fixed"), (vecs, "chan_vecs"), (prev, "prev0")]:
                    sp.dma_start(tile[:, :, :], weights[name]).then_inc(first_in.sem, 16)
                for tile, f in [(wk, "k"), (wr, "r"), (wv, "v")]:
                    sp.dma_start(tile[:, :, :], weights["fW" + f]).then_inc(w_in[f].sem, 16)

            def step(n, par):
                load(n + 1, 1 - par)
                residual(n)

            def last(n, par):
                residual(n)
                sp.wait_ge(x_stored.sem, x_stored.all(n))

            over_batches(sp, first, step, last)

        @block.vector
        def _(dve):
            dve.memset(half[:, :], -0.5).then_inc(consts_done.sem, 1)
            grant(dve, [ln.stats_done, ln.normed_done, mixed_done, gated_done, x_added])
            dve.wait_ge(first_in.sem, 16 * 3)

            def front(n, par):
                ln.vector_moments(dve, n, par)
                ln.vector_normalise(dve, n, par)
                dve.wait_ge(ln.out_done.sem, ln.out_done.all(n))
                dve.tensor_tensor(shift[:, :, :], xc[:, :, 0:L], xc[:, :, 1:L + 1], ALU.subtract)\
                   .then_inc(shift_done.sem, 1)
                dve.wait_ge(shift_done.sem, shift_done.all(n))
                dve.wait_ge(r_ps.sem, r_ps.all(n - 2))
                for tile, f in ((xk[par], "fmaa_k"), (xr[par], "fmaa_r")):
                    for c in range(CT):
                        r = dve.scalar_tensor_tensor(tile[:, c, :], shift[:, c, :], vec[f][:, c:c + 1],
                                                     xc[:, c, 1:L + 1], ALU.mult, ALU.add)
                r.then_inc(mixed_done.sem, 1)

            def back(n, par):
                dve.wait_ge(v_ps.sem, v_ps.all(n))
                dve.wait_ge(gate_done.sem, gate_done.all(n))
                dve.wait_ge(x_added.sem, x_added.all(n - 1))
                dve.scalar_tensor_tensor(gated[:, :, :], gate[:, :, :], 1.0, ps_v[:, :, :], ALU.add, ALU.mult)\
                   .then_inc(gated_done.sem, 1)
                dve.wait_ge(gated_done.sem, gated_done.all(n))
                dve.wait_ge(res_loaded.sem, res_loaded.all(n))
                dve.scalar_tensor_tensor(res[:, :, :], gated[:, :, :], 0.5, res[:, :, :], ALU.mult, ALU.add)\
                   .then_inc(x_added.sem, 1)

            def step(n, par):
                front(n + 1, 1 - par)
                back(n, par)

            over_batches(dve, lambda: front(0, 0), step, back)

        @block.gpsimd
        def _(pool):
            grant(pool, [kk_done])
            pool.wait_ge(consts_done.sem, 1)

            def back(n, par):
                pool.wait_ge(relu_done.sem, relu_done.all(n))
                pool.wait_ge(v_ps.sem, v_ps.all(n - 1))
                pool.tensor_tensor(kk[:, :, :], relu[:, :, :], relu[:, :, :], ALU.mult).then_inc(kk_done.sem, 1)

            def step(n, par):
                ln.gpsimd_rstd(pool, n + 1)
                back(n, par)

            over_batches(pool, lambda: ln.gpsimd_rstd(pool, 0), step, back)

        @block.scalar
        def _(act):
            grant(act, [relu_done, gate_done])
            act.wait_ge(first_in.sem, 16 * 3)

            def back(n, par, next_batch):
                act.wait_ge(k_ps.sem, k_ps.all(n))
                act.wait_ge(kk_done.sem, kk_done.all(n - 1))
                act.activation(relu[:, :, :], ps_k[:, :, :], ACT.Relu).then_inc(relu_done.sem, 1)
                if next_batch:
                    ln.scalar_out(act, n + 1, before=(xc, prev))
                act.wait_ge(r_ps.sem, r_ps.all(n))
                act.wait_ge(gated_done.sem, gated_done.all(n - 1))
                act.activation(gate[:, :, :], ps_r[:, :, :], ACT.Tanh, scale=0.5).then_inc(gate_done.sem, 1)

            def step(n, par):
                back(n, par, True)

            over_batches(act, lambda: ln.scalar_out(act, 0, before=(xc, prev)), step, lambda n, par: back(n, par, False))

        @block.tensor
        def _(pe):
            grant(pe, [ln.turned_done, r_ps, v_ps])
            pe.wait_ge(first_in.sem, 16 * 3)

            def back(n, par, next_batch):
                pe.wait_ge(mixed_done.sem, mixed_done.all(n))
                pe.wait_ge(relu_done.sem, relu_done.all(n - 1))
                for m in range(CT):
                    for c in range(CT):
                        r = pe.matmul(ps_k[:, m, :], wk[:, c, m * P:(m + 1) * P], xk[par][:, c, :],
                                      start=c == 0, stop=c == CT - 1)
                r.then_inc(k_ps.sem, 1)
                if next_batch:
                    ln.tensor_turn(pe, n + 1)
                pe.wait_ge(gate_done.sem, gate_done.all(n - 1))
                for t in range(TT):
                    for c in range(CT):
                        r = pe.matmul(ps_r[:, t, :], xr[par][:, c, t * P:(t + 1) * P], wr[:, c, :],
                                      start=c == 0, stop=c == CT - 1)
                r.then_inc(r_ps.sem, 1)
                pe.wait_ge(kk_done.sem, kk_done.all(n))
                pe.wait_ge(gated_done.sem, gated_done.all(n - 1))
                for t in range(TT):
                    for c in range(CT):
                        r = pe.matmul(ps_v[:, t, :], kk[:, c, t * P:(t + 1) * P], wv[:, c, :],
                                      start=c == 0, stop=c == CT - 1)
                r.then_inc(v_ps.sem, 1)

            def step(n, par):
                back(n, par, True)

            def first():
                ln.tensor_turn(pe, 0)
                for f in "krv":
                    pe.wait_ge(w_in[f].sem, 16)

            over_batches(pe, first, step, lambda n, par: back(n, par, False))


def attention(nc, held, name, x_in, x_out, source, mask, weights, cross):
    with ExitStack() as ctx:
        def sb(tile, shape):
            return ctx.enter_context(nc.sbuf_tensor(f"{name}_{tile}", shape, F32))

        sem = counter(held, nc, name)
        HEADS = 4
        TURN, MIX = 2, 4

        wq, wk, wv, wo = (sb(f"w{f}", [P, CT, C]) for f in "qkvo")
        vecs = sb("vecs", [P, 5, CT])
        ln_s, ln_b, b_q, b_k, b_v = (vecs[:, i, :] for i in range(5))
        bq_scaled = sb("bq_scaled", [P, CT])
        bo = sb("bo", [P, C])
        fixed = sb("fixed", [P, 3, P])
        ident = fixed[:, 0, :]
        half = sb("half", [P, TT])
        x = [sb(f"x{i}", [P, TT, C]) for i in range(2)]
        lnT = sb("lnT", [P, CT, L])
        src = sb("src", [P, CT, L]) if cross else lnT
        qT = [sb(f"qT{i}", [P, CT, L]) for i in range(2)]
        kT = [sb(f"kT{i}", [P, CT, L]) for i in range(2)]
        v = [sb(f"v{i}", [P, TT, C]) for i in range(2)]
        masks = 2 if cross else 1
        mask_in = [sb(f"mask_in{i}", [P, TT, L]) for i in range(masks)]
        mask_neg = [sb(f"mask_neg{i}", [P, TT, L]) for i in range(masks)]
        mask_add = [sb(f"mask_add{i}", [P, TT, L]) for i in range(masks)]
        low = [sb(f"low{i}", [P, TT, L]) for i in range(HEADS)]
        low_min = [sb(f"low_min{i}", [P, TT]) for i in range(HEADS)]
        prob = [sb(f"prob{i}", [P, TT, L]) for i in range(HEADS)]
        probT = [sb(f"probT{i}", [P, TT, L]) for i in range(HEADS)]
        row_sum = [sb(f"row_sum{i}", [P, TT, NH]) for i in range(2)]
        row_inv = sb("row_inv", [P, TT, NH])
        mixed = sb("mixed", [P, TT, C])
        mixedT = sb("mixedT", [P, CT, L])
        res = sb("res", [P, TT, C])
        ps_dense = ctx.enter_context(nc.psum_tensor(f"{name}_ps_dense", [P, CT, L], F32))
        ps_score = [ctx.enter_context(nc.psum_tensor(f"{name}_ps_score{i}", [P, TT, L], F32)) for i in range(2)]
        ps_turn = [ctx.enter_context(nc.psum_tensor(f"{name}_ps_turn{i}", [P, TT, L], F32)) for i in range(2)]
        ps_mixed = ctx.enter_context(nc.psum_tensor(f"{name}_ps_mixed", [P, TT, C], F32))
        dense_rows = ps_dense[:, :, :].rearrange("p (t a) l -> p t (a l)", t=TT)

        first_in = sem("first_in", 0)
        w_in = {f: sem(f"w{f}_in", 0) for f in "qkvo"}
        passed = sem("passed", 0)
        consts_done = sem("consts_done", 0)
        x_loaded = sem("x_loaded", 16)
        src_loaded = sem("src_loaded", 16)
        mask_loaded = sem("mask_loaded", 16)
        x_stored = sem("x_stored", 16, 1)
        res_loaded = sem("res_loaded", 16)
        mask_flipped = sem("mask_flipped", 1, 1)
        mask_done = sem("mask_done", 1)
        biased = sem("biased", 1)
        q_ps = sem("q_ps", 2)
        k_ps = sem("k_ps", 2)
        v_ps = sem("v_ps", 2, 1)
        q_out = sem("q_out", 2)
        k_out = sem("k_out", 2)
        v_out = sem("v_out", 2, 1)
        score_ps = sem("score_ps", NH, 2)
        masked = sem("masked", NH, 1)
        low_done = sem("low_done", NH, 2)
        prob_done = sem("prob_done", NH, 1)
        prob_ps = sem("prob_ps", NH, 1)
        probT_done = sem("probT_done", NH, 1)
        mixed_ps = sem("mixed_ps", NH, 2)
        inv_done = sem("inv_done", 1)
        mixed_done = sem("mixed_done", 1, 2)
        mixed_turned = sem("mixed_turned", 2, 1)
        mixedT_done = sem("mixedT_done", 2)
        out_ps = sem("out_ps", 2, 1)
        x_added = sem("x_added", 2, 2)

        ln = LayerNorm(ctx, nc, name, sem, x, x_loaded, ps_dense,
                       lambda eng, n, bank: eng.wait_ge(v_out.sem, v_out.at(n - 1, bank + 1)),
                       lambda c: lnT[:, c, :],
                       lambda eng, n: eng.wait_ge(v_ps.sem, v_ps.all(n - 1)),
                       ln_s, ln_b, ident, half, passed, parts=2)
        ln.normed_done.ahead = 2

        block = ctx.enter_context(nc.Block())

        @block.sync
        def _(sp):
            grant(sp, [x_stored])

            def load_mask(n, par):
                sp.dma_start(mask_in[par][:, :, :], mask[n, 0, :, :].rearrange("(t p) k -> p t k", p=P))\
                  .then_inc(mask_loaded.sem, 16)

            def load(n, par):
                sp.wait_ge(ln.stats_done.sem, ln.stats_done.all(n - 1))
                sp.sem_inc(passed.sem, 1)
                sp.wait_ge(ln.normed_done.sem, ln.normed_done.all(n - 2))
                sp.sem_inc(passed.sem, 1)
                sp.dma_start(x[par][:, :, :], x_in[n, :, :].rearrange("(t p) c -> p t c", p=P))\
                  .then_inc(x_loaded.sem, 16)
                if cross:
                    sp.wait_ge(v_ps.sem, v_ps.all(n - 1))
                    sp.sem_inc(passed.sem, 1)
                    sp.dma_start(src[:, :, :], source[n, :, :].rearrange("(c p) l -> p c l", p=P))\
                      .then_inc(src_loaded.sem, 16)
                    sp.wait_ge(mask_flipped.sem, mask_flipped.all(n - 1))
                    sp.sem_inc(passed.sem, 1)
                    sp.wait_ge(low_done.sem, low_done.all(n - 2))
                    sp.sem_inc(passed.sem, 1)
                    load_mask(n, par)

            def load_residual(n):
                sp.wait_ge(x_stored.sem, x_stored.all(n - 1))
                sp.sem_inc(passed.sem, 1)
                sp.dma_start(res[:, :, :], x_in[n, :, :].rearrange("(t p) c -> p t c", p=P))\
                  .then_inc(res_loaded.sem, 16)

            def store(n):
                sp.wait_ge(x_added.sem, x_added.all(n))
                sp.sem_inc(passed.sem, 1)
                sp.dma_start(x_out[n, :, :].rearrange("(t p) c -> p t c", p=P), res[:, :, :])\
                  .then_inc(x_stored.sem, 16)

            def start():
                sp.dma_start(x[0][:, :, :], x_in[0, :, :].rearrange("(t p) c -> p t c", p=P))\
                  .then_inc(x_loaded.sem, 16)
                for tile, w in [(fixed, "fixed"), (vecs, "vecs")]:
                    sp.dma_start(tile[:, :, :], weights[w]).then_inc(first_in.sem, 16)
                sp.dma_start(wq[:, :, :], weights["q"]).then_inc(w_in["q"].sem, 16)
                if cross:
                    sp.dma_start(src[:, :, :], source[0, :, :].rearrange("(c p) l -> p c l", p=P))\
                      .then_inc(src_loaded.sem, 16)
                    load_mask(0, 0)
                for tile, w in [(wk, "k"), (wv, "v"), (wo, "o")]:
                    sp.dma_start(tile[:, :, :], weights[w]).then_inc(w_in[w].sem, 16)
                sp.dma_start(bo[:, :], weights["bo"].unsqueeze(0).broadcast_to([P, C])).then_inc(w_in["o"].sem, 16)
                if not cross:
                    load_mask(0, 0)

            def step(n, par, prev_batch, next_batch):
                if prev_batch:
                    load_residual(n - 1)
                if next_batch:
                    load(n + 1, 1 - par)
                if prev_batch:
                    store(n - 1)

            def finish(n):
                load_residual(n)
                store(n)
                sp.wait_ge(x_stored.sem, x_stored.all(n))

            over_three_stages(sp, start, step, finish)

        @block.vector
        def _(dve):
            dve.memset(half[:, :], -0.5).then_inc(consts_done.sem, 1)
            grant(dve, [ln.stats_done, ln.normed_done, masked, low_done, mixed_done, x_added])
            dve.wait_ge(first_in.sem, 16 * 2)
            dve.tensor_scalar(bq_scaled[:, :], b_q, HD ** -0.5, None, ALU.mult).then_inc(consts_done.sem, 1)

            def softmax_low(n, par, h):
                m = par if cross else 0
                dve.wait_ge(score_ps.sem, score_ps.at(n, h + 1))
                if h == 0:
                    if cross:
                        dve.wait_ge(mask_done.sem, mask_done.all(n))
                    else:
                        dve.wait_ge(mask_done.sem, 1)
                dve.wait_ge(prob_done.sem, prob_done.at(n, h + 1 - HEADS))
                low_h = low[h % HEADS]
                dve.tensor_tensor(low_h[:, :, :], ps_score[h % 2][:, :, :], mask_neg[m][:, :, :], ALU.mult)\
                   .then_inc(masked.sem, 1)
                dve.wait_ge(masked.sem, masked.at(n, h + 1))
                dve.sem_inc(passed.sem, 1)
                for t in range(TT):
                    r = dve.tensor_tensor_reduce(low_h[:, t, :], low_h[:, t, :], mask_add[m][:, t, :],
                                                 1.0, 3.0e38, ALU.add, ALU.min, low_min[h % HEADS][:, t:t + 1])
                r.then_inc(low_done.sem, 1)

            def invert_sums(n, par):
                dve.wait_ge(prob_done.sem, prob_done.all(n))
                dve.wait_ge(mixed_done.sem, mixed_done.all(n - 1))
                dve.reciprocal(row_inv[:, :, :], row_sum[par][:, :, :]).then_inc(inv_done.sem, 1)

            def normalise(n):
                dve.wait_ge(inv_done.sem, inv_done.all(n))
                dve.wait_ge(mixed_ps.sem, mixed_ps.all(n))
                dve.wait_ge(mixed_turned.sem, mixed_turned.all(n - 1))
                for t in range(TT):
                    r = dve.tensor_tensor(mixed[:, t, :].rearrange("p (h d) -> p h d", h=NH),
                                          ps_mixed[:, t, :].rearrange("p (h d) -> p h d", h=NH),
                                          row_inv[:, t, :].unsqueeze(2).broadcast_to([P, NH, HD]), ALU.mult)
                r.then_inc(mixed_done.sem, 1)

            def residual(n, t):
                dve.wait_ge(out_ps.sem, out_ps.at(n, t + 1))
                dve.wait_ge(biased.sem, biased.all(n))
                dve.tensor_tensor(res[:, t, :], res[:, t, :], dense_rows[:, t, :], ALU.add).then_inc(x_added.sem, 1)

            def start():
                ln.vector_moments(dve, 0, 0)
                ln.vector_normalise(dve, 0, 0)

            def step(n, par, prev_batch, next_batch):
                for h in range(NH):
                    if prev_batch:
                        if h == 2:
                            invert_sums(n - 1, 1 - par)
                        if h == 4:
                            normalise(n - 1)
                        if h in (9, 10):
                            residual(n - 1, h - 9)
                    if next_batch:
                        if h == 0:
                            ln.vector_moments(dve, n + 1, 1 - par)
                        if h == 1:
                            ln.vector_normalise(dve, n + 1, 1 - par)
                    softmax_low(n, par, h)

            def finish(n):
                invert_sums(n, n % 2)
                normalise(n)
                for t in range(TT):
                    residual(n, t)

            over_three_stages(dve, start, step, finish)

        @block.gpsimd
        def _(pool):
            grant(pool, [mask_flipped])
            pool.wait_ge(consts_done.sem, 1)

            def masks_of(n, par):
                if cross:
                    pool.wait_ge(low_done.sem, low_done.all(n - 2))
                    pool.sem_inc(passed.sem, 1)
                pool.wait_ge(mask_loaded.sem, mask_loaded.all(n))
                pool.sem_inc(passed.sem, 1)
                pool.tensor_scalar(mask_neg[par][:, :, :], mask_in[par][:, :, :], -1.0, None, ALU.mult)
                pool.tensor_scalar(mask_add[par][:, :, :], mask_in[par][:, :, :], -1.0, 1.0, ALU.mult, ALU.add)\
                    .then_inc(mask_flipped.sem, 1)
                pool.wait_ge(mask_flipped.sem, mask_flipped.all(n))
                pool.sem_inc(passed.sem, 1)
                pool.tensor_scalar(mask_add[par][:, :, :], mask_add[par][:, :, :], 10000.0, None, ALU.mult)\
                    .then_inc(mask_done.sem, 1)

            def add_bias(n):
                pool.wait_ge(res_loaded.sem, res_loaded.all(n))
                pool.wait_ge(w_in["o"].sem, 16 * 2)
                pool.tensor_tensor(res[:, :, :], res[:, :, :],
                                   bo[:, :].unsqueeze(1).broadcast_to([P, TT, C]), ALU.add).then_inc(biased.sem, 1)

            def start():
                ln.gpsimd_rstd(pool, 0)
                masks_of(0, 0)

            def step(n, par, prev_batch, next_batch):
                if prev_batch:
                    add_bias(n - 1)
                if next_batch:
                    ln.gpsimd_rstd(pool, n + 1)
                    if cross:
                        masks_of(n + 1, 1 - par)

            over_three_stages(pool, start, step, add_bias)

        @block.scalar
        def _(act):
            grant(act, [prob_done, probT_done, v_out])
            act.wait_ge(consts_done.sem, 2)

            def q_copy(n, par, bank):
                act.wait_ge(q_ps.sem, q_ps.at(n, bank + 1))
                act.wait_ge(score_ps.sem, score_ps.all(n - 2))
                for c in (2 * bank, 2 * bank + 1):
                    r = act.activation(qT[par][:, c, :], ps_dense[:, c, :], ACT.Identity,
                                       bias=bq_scaled[:, c:c + 1], scale=HD ** -0.5)
                r.then_inc(q_out.sem, 1)

            def k_copy(n, par, bank):
                act.wait_ge(k_ps.sem, k_ps.at(n, bank + 1))
                for c in (2 * bank, 2 * bank + 1):
                    r = act.activation(kT[par][:, c, :], ps_dense[:, c, :], ACT.Identity, bias=b_k[:, c:c + 1])
                r.then_inc(k_out.sem, 1)

            def v_copy(n, par, t):
                act.wait_ge(v_ps.sem, v_ps.at(n, t + 1))
                act.wait_ge(mixed_ps.sem, mixed_ps.all(n - 2))
                act.activation(v[par][:, t, :], dense_rows[:, t, :], ACT.Copy).then_inc(v_out.sem, 1)

            def exps(n, par, h):
                act.wait_ge(low_done.sem, low_done.at(n, h + 1))
                act.wait_ge(prob_ps.sem, prob_ps.at(n, h + 1 - HEADS))
                if h == 0:
                    act.wait_ge(mixed_done.sem, mixed_done.all(n - 2))
                for t in range(TT):
                    r = act.activation(prob[h % HEADS][:, t, :], low[h % HEADS][:, t, :], ACT.Exp,
                                       bias=low_min[h % HEADS][:, t:t + 1], scale=-1.0,
                                       accum_out=row_sum[par][:, t, h:h + 1])
                r.then_inc(prob_done.sem, 1)

            def prob_copy(n, h):
                act.wait_ge(prob_ps.sem, prob_ps.at(n, h + 1))
                act.wait_ge(mixed_ps.sem, mixed_ps.at(n, h + 1 - HEADS))
                act.activation(probT[h % HEADS][:, :, :], ps_turn[h % 2][:, :, :], ACT.Copy)\
                   .then_inc(probT_done.sem, 1)

            def mixed_copy(n, bank):
                act.wait_ge(mixed_turned.sem, mixed_turned.at(n, bank + 1))
                act.wait_ge(out_ps.sem, out_ps.all(n - 1))
                for c in (2 * bank, 2 * bank + 1):
                    r = act.activation(mixedT[:, c, :], ps_dense[:, c, :], ACT.Identity, bias=b_v[:, c:c + 1])
                r.then_inc(mixedT_done.sem, 1)

            def start():
                for bank in range(2):
                    ln.scalar_out(act, 0, bank)
                for bank in range(2):
                    q_copy(0, 0, bank)
                for bank in range(2):
                    k_copy(0, 0, bank)

            def step(n, par, prev_batch, next_batch):
                for h in range(NH):
                    if h in (0, 2):
                        v_copy(n, par, h // 2)
                    if next_batch:
                        if h in (3, 4):
                            ln.scalar_out(act, n + 1, h - 3)
                        if h in (11, 12):
                            q_copy(n + 1, 1 - par, h - 11)
                        if h in (13, 14):
                            k_copy(n + 1, 1 - par, h - 13)
                    if prev_batch and h in (6, 7):
                        mixed_copy(n - 1, h - 6)
                    exps(n, par, h)
                    if h >= TURN:
                        prob_copy(n, h - TURN)
                    elif prev_batch:
                        prob_copy(n - 1, h - TURN + NH)

            def finish(n):
                for h in range(NH - TURN, NH):
                    prob_copy(n, h)
                for bank in range(2):
                    mixed_copy(n, bank)

            over_three_stages(act, start, step, finish)

        @block.tensor
        def _(pe):
            grant(pe, [ln.turned_done, v_ps, score_ps, prob_ps, mixed_ps, mixed_turned, out_ps])
            pe.wait_ge(first_in.sem, 16 * 2)

            def q_part(n, m):
                if m == 0:
                    pe.wait_ge(ln.out_done.sem, ln.out_done.all(n))
                if m % 2 == 0:
                    pe.wait_ge(x_added.sem, x_added.at(n - 2, m // 2 + 1))
                for c in range(CT):
                    r = pe.matmul(ps_dense[:, m, :], wq[:, c, m * P:(m + 1) * P], lnT[:, c, :],
                                  start=c == 0, stop=c == CT - 1)
                if m % 2 == 1:
                    r.then_inc(q_ps.sem, 1)

            def k_part(n, m):
                if m % 2 == 0:
                    pe.wait_ge(q_out.sem, q_out.at(n, m // 2 + 1))
                if cross and m == 0:
                    pe.wait_ge(src_loaded.sem, src_loaded.all(n))
                for c in range(CT):
                    r = pe.matmul(ps_dense[:, m, :], wk[:, c, m * P:(m + 1) * P], src[:, c, :],
                                  start=c == 0, stop=c == CT - 1)
                if m % 2 == 1:
                    r.then_inc(k_ps.sem, 1)

            def v_part(n, m):
                t, half_of_c = m // 2, m % 2
                if half_of_c == 0:
                    pe.wait_ge(k_out.sem, k_out.at(n, t + 1))
                for c in range(2 * half_of_c, 2 * half_of_c + 2):
                    r = pe.matmul(dense_rows[:, t, :], src[:, c, t * P:(t + 1) * P], wv[:, c, :],
                                  start=c == 0, stop=c == CT - 1)
                if half_of_c == 1:
                    r.then_inc(v_ps.sem, 1)

            def score(n, par, h):
                c, row = h // HC, (h % HC) * HD
                if h == 0:
                    pe.wait_ge(k_out.sem, k_out.all(n))
                pe.wait_ge(masked.sem, masked.at(n, h - 1))
                for t in range(TT):
                    r = pe.matmul(ps_score[h % 2][:, t, :], qT[par][row:row + HD, c, t * P:(t + 1) * P],
                                  kT[par][row:row + HD, c, :], start=True, stop=True)
                r.then_inc(score_ps.sem, 1)

            def turn(n, h):
                pe.wait_ge(prob_done.sem, prob_done.at(n, h + 1))
                pe.wait_ge(probT_done.sem, probT_done.at(n, h - 1))
                for k in range(TT):
                    for t in range(TT):
                        r = pe.transpose(ps_turn[h % 2][:, k, t * P:(t + 1) * P],
                                         prob[h % HEADS][:, t, k * P:(k + 1) * P], ident)
                r.then_inc(prob_ps.sem, 1)

            def mix(n, par, h):
                pe.wait_ge(probT_done.sem, probT_done.at(n, h + 1))
                if h == 0:
                    pe.wait_ge(v_out.sem, v_out.all(n))
                    pe.wait_ge(mixed_done.sem, mixed_done.all(n - 1))
                for t in range(TT):
                    for k in range(TT):
                        r = pe.matmul(ps_mixed[:, t, h * HD:(h + 1) * HD], probT[h % HEADS][:, k, t * P:(t + 1) * P],
                                      v[par][:, k, h * HD:(h + 1) * HD], start=k == 0, stop=k == TT - 1)
                r.then_inc(mixed_ps.sem, 1)

            def turn_mixed(n, bank, later):
                pe.wait_ge(mixed_done.sem, mixed_done.all(n))
                if later == 2:
                    pe.wait_ge(ln.out_done.sem, ln.out_done.at(n + 2, bank + 1))
                else:
                    pe.wait_ge(v_out.sem, v_out.at(n + later, bank + 1))
                for t in range(TT):
                    for c in (2 * bank, 2 * bank + 1):
                        r = pe.transpose(ps_dense[:, c, t * P:(t + 1) * P], mixed[:, t, c * P:(c + 1) * P], ident)
                r.then_inc(mixed_turned.sem, 1)

            def output(n, m):
                t, half_of_c = m // 2, m % 2
                pe.wait_ge(mixedT_done.sem, mixedT_done.at(n, max(t, half_of_c) + 1))
                for c in range(2 * half_of_c, 2 * half_of_c + 2):
                    r = pe.matmul(dense_rows[:, t, :], mixedT[:, c, t * P:(t + 1) * P], wo[:, c, :],
                                  start=c == 0, stop=c == CT - 1)
                if half_of_c == 1:
                    r.then_inc(out_ps.sem, 1)

            def start():
                for bank in range(2):
                    ln.tensor_turn(pe, 0, bank)
                pe.wait_ge(w_in["q"].sem, 16)
                for m in range(4):
                    q_part(0, m)
                pe.wait_ge(w_in["k"].sem, 16)
                for m in range(4):
                    k_part(0, m)
                pe.wait_ge(w_in["v"].sem, 16)
                for m in range(2):
                    v_part(0, m)
                pe.wait_ge(w_in["o"].sem, 16 * 2)

            def step(n, par, prev_batch, next_batch):
                for h in range(NH):
                    score(n, par, h)
                    if h in (0, 1):
                        v_part(n, h + 2)
                    if prev_batch:
                        if h in (5, 6):
                            turn_mixed(n - 1, h - 5, 2 if next_batch else 1)
                        if h == 7:
                            output(n - 1, 0)
                        if h == 8:
                            output(n - 1, 1)
                            output(n - 1, 2)
                        if h == 9:
                            output(n - 1, 3)
                    if next_batch:
                        if h in (2, 3):
                            ln.tensor_turn(pe, n + 1, h - 2)
                        if h in (10, 11):
                            q_part(n + 1, 2 * (h - 10))
                            q_part(n + 1, 2 * (h - 10) + 1)
                        if h in (12, 13):
                            k_part(n + 1, 2 * (h - 12))
                            k_part(n + 1, 2 * (h - 12) + 1)
                        if h in (14, 15):
                            v_part(n + 1, h - 14)
                    if h >= TURN:
                        turn(n, h - TURN)
                    elif prev_batch:
                        turn(n - 1, h - TURN + NH)
                    if h >= MIX:
                        mix(n, par, h - MIX)
                    elif prev_batch:
                        mix(n - 1, 1 - par, h - MIX + NH)

            def finish(n):
                for h in range(NH - TURN, NH):
                    turn(n, h)
                for h in range(NH - MIX, NH):
                    mix(n, n % 2, h)
                for bank in range(2):
                    turn_mixed(n, bank, 0)
                for m in range(4):
                    output(n, m)

            over_three_stages(pe, start, step, finish)


def mlp(nc, held, x_in, x_out, weights):
    GROUPS = FF // C
    CHUNKS = 2 * GROUPS
    STAGES = 4
    with ExitStack() as ctx:
        def sb(name, shape, dtype=F32):
            return ctx.enter_context(nc.sbuf_tensor(f"ff_{name}", shape, dtype))

        sem = counter(held, nc, "ff")

        w1 = [sb(f"w1_{part}", [P, CT, FF], F32R) for part in ("hi", "lo")]
        w2 = [sb(f"w2_{part}", [P, FF // P, C], F32R) for part in ("hi", "lo")]
        stage = [sb(f"stage{i}", [P, CT * L]) for i in range(STAGES)]
        vecs = sb("vecs", [P, 2, CT])
        b1 = sb("b1", [P, FF // P])
        b2 = sb("b2", [P, C])
        fixed = sb("fixed", [P, 3, P])
        half = sb("half", [P, TT])
        x = [sb(f"x{i}", [P, TT, C]) for i in range(2)]
        lnT = sb("lnT", [P, CT, L])
        lnT_parts = [sb(f"lnT_{part}", [P, CT, L], F32R) for part in ("hi", "lo")]
        pre = [sb(f"pre{i}", [P, CT, L]) for i in range(2)]
        gel = [sb(f"gel{i}", [P, CT, L]) for i in range(2)]
        hid = [[sb(f"hid_{part}{i}", [P, CT, L], F32R) for i in range(2)] for part in ("hi", "lo")]
        ps_turn = ctx.enter_context(nc.psum_tensor("ff_ps_turn", [P, CT, L], F32))
        ps_hid = [ctx.enter_context(nc.psum_tensor(f"ff_ps_hid{i}", [P, CT, L], F32)) for i in range(2)]
        ps_out = ctx.enter_context(nc.psum_tensor("ff_ps_out", [P, TT, C], F32))

        first_in = sem("first_in", 0)
        b2_in = sem("b2_in", 0)
        staged = [sem(f"staged{i}", 0) for i in range(STAGES)]
        w_hi_done = sem("w_hi_done", 0)
        w_done = sem("w_done", 0)
        passed = sem("passed", 0)
        consts_done = sem("consts_done", 0)
        x_loaded = sem("x_loaded", 16)
        x_stored = sem("x_stored", 16, 2)
        biased = sem("biased", 1)
        ln_hi_done = sem("ln_hi_done", 1)
        ln_done = sem("ln_done", 1)
        hid_ps = sem("hid_ps", GROUPS, 1)
        pre_done = sem("pre_done", GROUPS, 1)
        sq_done = sem("sq_done", GROUPS)
        poly_done = sem("poly_done", GROUPS)
        cube_done = sem("cube_done", GROUPS)
        tanh_done = sem("tanh_done", GROUPS)
        gelu_done = sem("gelu_done", GROUPS, 1)
        hid_hi_done = sem("hid_hi_done", GROUPS)
        hid_done = sem("hid_done", GROUPS, 1)
        out_ps = sem("out_ps", GROUPS, 1)
        x_added = sem("x_added", 1, 1)

        ln = LayerNorm(ctx, nc, "ff", sem, x, x_loaded, ps_turn,
                       lambda eng, n, _: eng.wait_ge(ln_out().sem, ln_out().all(n - 1)),
                       lambda c: lnT[:, c, :],
                       lambda eng, n: eng.wait_ge(ln_done.sem, ln_done.all(n - 1)),
                       vecs[:, 0, :], vecs[:, 1, :], fixed[:, 0, :], half, passed)
        ln.out_done.ahead = 1
        ln_done.ahead = 1

        def ln_out():
            return ln.out_done

        def chunk(i):
            if i < CHUNKS:
                cols = slice(i * L, (i + 1) * L)
                w, parts = weights["w1"][:, :, cols], [part[:, :, cols] for part in w1]
                return w, parts, stage[i % STAGES][:, :].rearrange("p (c l) -> p c l", l=L)
            k = slice(2 * (i - CHUNKS), 2 * (i - CHUNKS) + 2)
            w, parts = weights["w2"][:, k, :], [part[:, k, :] for part in w2]
            return w, parts, stage[i % STAGES][:, :].rearrange("p (k c) -> p k c", c=C)

        block = ctx.enter_context(nc.Block())

        @block.sync
        def _(sp):
            grant(sp, [x_stored])

            def load(n, par):
                sp.wait_ge(ln.stats_done.sem, ln.stats_done.all(n - 1))
                sp.sem_inc(passed.sem, 1)
                sp.wait_ge(x_stored.sem, x_stored.all(n - 2))
                sp.sem_inc(passed.sem, 1)
                sp.dma_start(x[par][:, :, :], x_in[n, :, :].rearrange("(t p) c -> p t c", p=P))\
                  .then_inc(x_loaded.sem, 16)

            def store(n, par):
                sp.wait_ge(x_added.sem, x_added.all(n))
                sp.sem_inc(passed.sem, 1)
                sp.dma_start(x_out[n, :, :].rearrange("(t p) c -> p t c", p=P), x[par][:, :, :])\
                  .then_inc(x_stored.sem, 16)

            def first():
                sp.dma_start(x[0][:, :, :], x_in[0, :, :].rearrange("(t p) c -> p t c", p=P))\
                  .then_inc(x_loaded.sem, 16)
                for tile, w in [(fixed, "fixed"), (vecs, "vecs")]:
                    sp.dma_start(tile[:, :, :], weights[w]).then_inc(first_in.sem, 16)
                sp.dma_start(b1[:, :], weights["b1"]).then_inc(first_in.sem, 16)
                for i in range(2 * CHUNKS):
                    w, _, tile = chunk(i)
                    if i >= STAGES:
                        sp.wait_ge(w_done.sem, i + 1 - STAGES)
                    sp.dma_start(tile, w).then_inc(staged[i % STAGES].sem, 16)
                    if i == 1:
                        sp.dma_start(b2[:, :], weights["b2"].unsqueeze(0).broadcast_to([P, C])).then_inc(b2_in.sem, 16)

            def step(n, par):
                load(n + 1, 1 - par)
                store(n, par)

            def last(n, par):
                store(n, par)
                sp.wait_ge(x_stored.sem, x_stored.all(n))

            over_batches(sp, first, step, last)

        @block.vector
        def _(dve):
            dve.memset(half[:, :], -0.5).then_inc(consts_done.sem, 1)
            grant(dve, [ln.stats_done, ln_done, gelu_done, hid_done, x_added])
            dve.wait_ge(first_in.sem, 16 * 3)

            def weight_lo(i):
                _, parts, tile = chunk(i)
                dve.wait_ge(w_hi_done.sem, i + 1)
                dve.tensor_tensor(parts[1], tile, parts[0], ALU.subtract).then_inc(w_done.sem, 1)

            def norm(n, par):
                ln.vector_moments(dve, n, par)
                ln.vector_normalise(dve, n, par)

            def ln_lo(n):
                dve.wait_ge(ln_hi_done.sem, ln_hi_done.all(n))
                dve.wait_ge(hid_ps.sem, hid_ps.all(n - 1))
                dve.tensor_tensor(lnT_parts[1][:, :, :], lnT[:, :, :], lnT_parts[0][:, :, :], ALU.subtract)\
                   .then_inc(ln_done.sem, 1)

            def square(n, g):
                u, poly = pre[g % 2][:, :, :], gel[g % 2][:, :, :]
                dve.wait_ge(pre_done.sem, pre_done.at(n, g + 1))
                dve.wait_ge(hid_done.sem, hid_done.at(n, g - 1))
                dve.tensor_tensor(poly, u, u, ALU.mult).then_inc(sq_done.sem, 1)
                dve.wait_ge(sq_done.sem, sq_done.at(n, g + 1))
                dve.tensor_scalar(poly, poly, 0.044715, 1.0, ALU.mult, ALU.add).then_inc(poly_done.sem, 1)

            def gelu(n, g):
                tanh, u = gel[g % 2][:, :, :], pre[g % 2][:, :, :]
                dve.wait_ge(tanh_done.sem, tanh_done.at(n, g + 1))
                dve.wait_ge(out_ps.sem, out_ps.at(n, g - 1))
                dve.scalar_tensor_tensor(hid[0][g % 2][:, :, :], tanh, 1.0, u, ALU.add, ALU.mult)\
                   .then_inc(hid_hi_done.sem, 1)
                dve.wait_ge(hid_hi_done.sem, hid_hi_done.at(n, g + 1))
                dve.scalar_tensor_tensor(tanh, tanh, 1.0, u, ALU.add, ALU.mult).then_inc(gelu_done.sem, 1)
                dve.wait_ge(gelu_done.sem, gelu_done.at(n, g + 1))
                dve.tensor_tensor(hid[1][g % 2][:, :, :], gel[g % 2][:, :, :], hid[0][g % 2][:, :, :], ALU.subtract)\
                   .then_inc(hid_done.sem, 1)

            def back(n, par):
                dve.wait_ge(out_ps.sem, out_ps.all(n))
                dve.wait_ge(biased.sem, biased.all(n))
                dve.scalar_tensor_tensor(x[par][:, :, :], ps_out[:, :, :], 0.5, x[par][:, :, :], ALU.mult, ALU.add)\
                   .then_inc(x_added.sem, 1)

            def first():
                norm(0, 0)
                for i in range(2):
                    weight_lo(i)
                ln_lo(0)
                for i in range(2, CHUNKS):
                    weight_lo(i)
                square(0, 0)
                for i in range(CHUNKS, 2 * CHUNKS):
                    weight_lo(i)

            def step(n, par):
                square(n, 1)
                gelu(n, 0)
                square(n, 2)
                gelu(n, 1)
                norm(n + 1, 1 - par)
                square(n, 3)
                gelu(n, 2)
                ln_lo(n + 1)
                gelu(n, 3)
                square(n + 1, 0)
                back(n, par)

            def last(n, par):
                for g in range(1, GROUPS):
                    square(n, g)
                    gelu(n, g - 1)
                gelu(n, GROUPS - 1)
                back(n, par)

            over_batches(dve, first, step, last)

        @block.gpsimd
        def _(pool):
            pool.wait_ge(consts_done.sem, 1)

            def cube(n, g):
                pool.wait_ge(poly_done.sem, poly_done.at(n, g + 1))
                pool.tensor_tensor(gel[g % 2][:, :, :], gel[g % 2][:, :, :], pre[g % 2][:, :, :], ALU.mult)\
                    .then_inc(cube_done.sem, 1)

            def front(n, par):
                ln.gpsimd_rstd(pool, n)
                pool.wait_ge(ln.normed_done.sem, ln.normed_done.all(n))
                pool.wait_ge(b2_in.sem, 16)
                pool.tensor_tensor(x[par][:, :, :], x[par][:, :, :],
                                   b2[:, :].unsqueeze(1).broadcast_to([P, TT, C]), ALU.add).then_inc(biased.sem, 1)

            def first():
                front(0, 0)
                cube(0, 0)

            def step(n, par):
                cube(n, 1)
                cube(n, 2)
                front(n + 1, 1 - par)
                cube(n, 3)
                cube(n + 1, 0)

            def last(n, par):
                for g in range(1, GROUPS):
                    cube(n, g)

            over_batches(pool, first, step, last)

        @block.scalar
        def _(act):
            grant(act, [ln.out_done, pre_done])
            act.wait_ge(first_in.sem, 16 * 3)

            def weight_hi(i):
                _, parts, tile = chunk(i)
                act.wait_ge(staged[i % STAGES].sem, 16 * (i // STAGES + 1))
                act.activation(parts[0], tile, ACT.Copy).then_inc(w_hi_done.sem, 1)

            def ln_hi(n):
                ln.scalar_out(act, n)
                act.wait_ge(ln.out_done.sem, ln.out_done.all(n))
                act.wait_ge(hid_ps.sem, hid_ps.all(n - 1))
                act.activation(lnT_parts[0][:, :, :], lnT[:, :, :], ACT.Copy).then_inc(ln_hi_done.sem, 1)

            def pre_copy(n, g):
                act.wait_ge(hid_ps.sem, hid_ps.at(n, g + 1))
                act.wait_ge(gelu_done.sem, gelu_done.at(n, g - 1))
                for c in range(CT):
                    r = act.activation(pre[g % 2][:, c, :], ps_hid[g % 2][:, c, :], ACT.Identity,
                                       bias=b1[:, g * CT + c:g * CT + c + 1])
                r.then_inc(pre_done.sem, 1)

            def tanhs(n, g):
                act.wait_ge(cube_done.sem, cube_done.at(n, g + 1))
                act.activation(gel[g % 2][:, :, :], gel[g % 2][:, :, :], ACT.Tanh, scale=0.7978845608028654)\
                   .then_inc(tanh_done.sem, 1)

            def first():
                for i in range(2):
                    weight_hi(i)
                ln_hi(0)
                for i in range(2, CHUNKS):
                    weight_hi(i)
                pre_copy(0, 0)
                for i in range(CHUNKS, 2 * CHUNKS):
                    weight_hi(i)

            def step(n, par):
                for g in range(1, GROUPS):
                    tanhs(n, g - 1)
                    pre_copy(n, g)
                ln_hi(n + 1)
                tanhs(n, GROUPS - 1)
                pre_copy(n + 1, 0)

            def last(n, par):
                for g in range(1, GROUPS):
                    tanhs(n, g - 1)
                    pre_copy(n, g)
                tanhs(n, GROUPS - 1)

            over_batches(act, first, step, last)

        @block.tensor
        def _(pe):
            grant(pe, [ln.turned_done, hid_ps, out_ps])
            pe.wait_ge(first_in.sem, 16 * 3)
            PRODUCTS = [(0, 0), (0, 1), (1, 0)]

            def hidden(n, g):
                if g == 0:
                    pe.wait_ge(ln_done.sem, ln_done.all(n))
                pe.wait_ge(pre_done.sem, pre_done.at(n, g - 1))
                for m in range(CT):
                    cols = slice((g * CT + m) * P, (g * CT + m + 1) * P)
                    for c in range(CT):
                        for i, (a, b) in enumerate(PRODUCTS):
                            r = pe.matmul(ps_hid[g % 2][:, m, :], w1[a][:, c, cols], lnT_parts[b][:, c, :],
                                          start=c == 0 and i == 0, stop=c == CT - 1 and i == 2)
                r.then_inc(hid_ps.sem, 1)

            def output(n, g):
                if g == 0:
                    pe.wait_ge(x_added.sem, x_added.all(n - 1))
                pe.wait_ge(hid_done.sem, hid_done.at(n, g + 1))
                for k in range(CT):
                    for i, (a, b) in enumerate(PRODUCTS):
                        for t in range(TT):
                            r = pe.matmul(ps_out[:, t, :], hid[a][g % 2][:, k, t * P:(t + 1) * P],
                                          w2[b][:, g * CT + k, :], start=g == 0 and k == 0 and i == 0,
                                          stop=g == GROUPS - 1 and k == CT - 1 and i == 2)
                r.then_inc(out_ps.sem, 1)

            def middle(n):
                hidden(n, 1)
                hidden(n, 2)
                output(n, 0)
                hidden(n, 3)
                output(n, 1)

            def first():
                ln.tensor_turn(pe, 0)
                pe.wait_ge(w_done.sem, 2)
                hidden(0, 0)
                pe.wait_ge(w_done.sem, 2 * CHUNKS)

            def step(n, par):
                middle(n)
                ln.tensor_turn(pe, n + 1)
                output(n, 2)
                hidden(n + 1, 0)
                output(n, 3)

            def last(n, par):
                middle(n)
                output(n, 2)
                output(n, 3)

            over_batches(pe, first, step, last)


def build(nc, ins, out, scratch):
    held = []
    xs, v_rows = scratch
    ctx_rows = ins["ctx"]
    first_state = ctx_rows[:, 2:2 + S, :].rearrange("b s c -> b (s c)").rearrange("b (p s) -> b p s", s=S)
    time_mix(nc, held, ins["x"], xs[0], first_state, v_rows, ins)
    end_phase(nc, held)
    channel_mix(nc, held, xs[0], xs[1], ins)
    end_phase(nc, held)
    attention(nc, held, "sa", xs[1], xs[2], None, ins["mask_1x1xSxS2_fc1"],
              {"vecs": ins["sa_vecs"], "fixed": ins["fixed"], "q": ins["sa_q"], "k": ins["sa_k"], "v": ins["sa_v"],
               "o": ins["sa_o"], "bo": ins["b_ao"]}, False)
    end_phase(nc, held)
    attention(nc, held, "ca", xs[2], xs[3], ins["ctxT"], ins["mask_Bx1xSxS2_ff1"],
              {"vecs": ins["ca_vecs"], "fixed": ins["fixed"], "q": ins["ca_q"], "k": ins["ca_k"], "v": ins["ca_v"],
               "o": ins["ca_o"], "bo": ins["b_co"]}, True)
    end_phase(nc, held)
    mlp(nc, held, xs[3], out, {"vecs": ins["ff_vecs"], "fixed": ins["fixed"], "w1": ins["w1"], "w2": ins["w2"],
                         "b1": ins["b1"], "b2": ins["b2"]})


def fixed_matrices():
    import numpy as np
    k = np.arange(P)
    same_head = (k[:, None] // S == k[None, :] // S).astype(np.float32)
    eye = np.eye(P, dtype=np.float32)
    centre = eye - same_head / S
    fixed = np.stack([eye, same_head, centre], axis=1)
    pick = np.stack([same_head * ((k[None, :] % S == s) - 1.0 / S) for s in range(S)], axis=1).astype(np.float32)
    head_sum = np.zeros((P, CT, C // S), np.float32)
    for c in range(CT):
        head_sum[k, c, c * HT + k // S] = 1.0 / S
    head_out = np.ascontiguousarray((head_sum > 0).astype(np.float32).transpose(2, 1, 0))
    return {"fixed": fixed, "pick": pick, "head_sum": head_sum, "head_out": head_out}


def layouts(inputs):
    import numpy as np
    a = {k: np.asarray(v) for k, v in inputs.items()}

    def rows(w):
        return np.ascontiguousarray(w.reshape(-1, P, w.shape[1]).transpose(1, 0, 2))

    def columns(*vs):
        return np.ascontiguousarray(np.stack([v.reshape(-1, P).T for v in vs], axis=1))

    t, u = "L0_xattn_", "L1_xattn_"
    out = {"x": a["x"], "ctx": a["ctx_2048"], "ctxT": np.ascontiguousarray(a["ctx_2048"].transpose(0, 2, 1)),
           "mask_1x1xSxS2_fc1": a["mask_1x1xSxS2_fc1"], "mask_Bx1xSxS2_ff1": a["mask_Bx1xSxS2_ff1"]}
    for w in ("Wr", "Wk", "Wv", "Wg", "Wo", "fWk", "fWr", "fWv"):
        out[w] = rows(a[t + w].T)
    for i in range(2):
        out[f"prev{i}"] = np.ascontiguousarray(a["ctx_2048"][:, i].reshape(B, CT, P).transpose(2, 0, 1))
    out["maa_w1"], out["decay_w1"] = rows(a[t + "maa_w1"]), rows(a[t + "decay_w1"])
    out["maa_w2"] = np.ascontiguousarray(a[t + "maa_w2"].reshape(5 * DM, C))
    out["decay_w2"] = a[t + "decay_w2"]
    out["time_vecs"] = columns(*[a[t + v].reshape(C) for v in TIME_VECS])
    out["chan_vecs"] = columns(*[a[t + v] for v in CHAN_VECS])
    for p, w, b, ln in (("sa", a[u + "w_qkv"], a[u + "b_qkv"], "ln1"),
                        ("ca", np.concatenate([a[u + "w_q"], a[u + "w_kv"]], axis=1),
                         np.concatenate([a[u + "b_q"], a[u + "b_kv"]]), "ln2")):
        for i, f in enumerate("qkv"):
            out[f"{p}_{f}"] = rows(w[:, i * C:(i + 1) * C])
        out[f"{p}_vecs"] = columns(a[f"{u}{ln}_s"], a[f"{u}{ln}_b"], *[b[i * C:(i + 1) * C] for i in range(3)])
    out["sa_o"], out["ca_o"] = rows(a[u + "w_ao"]), rows(a[u + "w_co"])
    out["b_ao"], out["b_co"] = a[u + "b_ao"], a[u + "b_co"]
    out["ff_vecs"] = columns(a[u + "ln3_s"], a[u + "ln3_b"])
    out["w1"], out["w2"] = rows(a[u + "w1"]), rows(a[u + "w2"])
    out["b1"] = np.ascontiguousarray(a[u + "b1"].reshape(-1, P).T)
    out["b2"] = a[u + "b2"]
    out.update(fixed_matrices())
    return out


def kernel(**inputs):
    import numpy as np
    import concourse.bacc as bacc
    from concourse.bass_utils import run_bass_kernel_spmd as run

    nc = bacc.Bacc("TRN2", target_bir_lowering=False, num_devices=1)
    arrays, ins = {}, {}
    for name, a in layouts(inputs).items():
        arrays[f"in_{name}"] = a
        ins[name] = nc.dram_tensor(f"in_{name}", a.shape, mybir.dt.from_np(a.dtype), kind="ExternalInput").ap()
    out = nc.dram_tensor("out_0", (B, L, C), F32, kind="ExternalOutput").ap()
    xs = [nc.dram_tensor(f"x_stage{i}", (B, L, C), F32, kind="Internal").ap() for i in range(4)]
    v_rows = [nc.dram_tensor(f"v_rows{i}", (C, L), F32, kind="Internal").ap() for i in range(2)]
    build(nc, ins, out, (xs, v_rows))
    r = run(nc, [arrays], core_ids=[0])
    return r.results[0]["out_0"]
```

```python
from contextlib import ExitStack

import concourse.bass as bass
from concourse import mybir

F32 = mybir.dt.float32
F32R = mybir.dt.float32r
ALU = mybir.AluOpType
ACT = mybir.ActivationFunctionType

P = 128
B = 8
L = 256
C = 512
CT = C // P
TT = L // P
S = 16
HT = P // S
NH = 16
HD = C // NH
HC = P // HD
DM = 32
DD = 64
FF = 4 * C
EPS = 1e-5
UNITS = 8
UW = S // 2
RING = 4

TIME_VECS = ["ln1_w", "ln1_b", "maa_x", "maa_w", "maa_k", "maa_v", "maa_r", "maa_g",
             "time_decay", "faaaa", "gn_w", "gn_b"]
CHAN_VECS = ["ln2_w", "ln2_b", "fmaa_k", "fmaa_r"]


class Count:

    def __init__(self, sem, per, ahead=0):
        self.sem, self.per, self.ahead = sem, per, ahead

    def at(self, n, k):
        return (n + self.ahead) * self.per + k

    def all(self, n):
        return (n + self.ahead + 1) * self.per


def counter(held, nc, phase):
    def make(name, per, ahead=0):
        held.append(nc.alloc_semaphore(name=f"{phase}_{name}"))
        return Count(held[-1], per, ahead)
    return make


def end_phase(nc, held):
    nc.clear_and_free_semaphores(held)
    nc.all_engine_barrier()
    held.clear()


def grant(eng, counts):
    for c in counts:
        if c.ahead:
            eng.sem_inc(c.sem, c.ahead * c.per)


def over_batches(eng, first, step, last):
    first()
    with eng.Fori(0, B // 2 - 1) as i:
        for par in range(2):
            step(i * 2 + par, par)
    step(B - 2, 0)
    last(B - 1, 1)


def over_three_stages(eng, start, step, finish):
    start()
    step(0, 0, False, True)
    with eng.Fori(0, B // 2 - 1) as i:
        for par in (1, 0):
            step(i * 2 + (2 - par), par, True, True)
    step(B - 1, 1, True, False)
    finish(B - 1)


class LayerNorm:

    def __init__(self, ctx, nc, name, sem, x, x_loaded, turned, turned_free, out, out_free, scale, shift, ident, half,
                 passed, parts=1):
        sb = lambda tile, shape: ctx.enter_context(nc.sbuf_tensor(f"{name}_ln_{tile}", shape, F32))
        self.nc, self.x, self.x_loaded, self.passed = nc, x, x_loaded, passed
        self.turned, self.turned_free, self.out, self.out_free = turned, turned_free, out, out_free
        self.scale, self.shift, self.ident, self.half = scale, shift, ident, half
        self.stats = sb("stats", [P, TT, 6])
        self.moments = sb("moments", [P, TT, 2])
        self.var = sb("var", [P, TT])
        self.rstd = sb("rstd", [P, TT])
        self.normed = sb("normed", [P, TT, C])
        self.stats_done = sem("ln_stats_done", 1, 1)
        self.moments_done = sem("ln_moments_done", 1)
        self.var_done = sem("ln_var_done", 1)
        self.rstd_done = sem("ln_rstd_done", 1)
        self.normed_done = sem("ln_normed_done", 1)
        self.parts = parts
        self.turned_done = sem("ln_turned_done", parts, 1)
        self.out_done = sem("ln_out_done", parts)

    def vector_moments(self, dve, n, par):
        dve.wait_ge(self.x_loaded.sem, self.x_loaded.all(n))
        for t in range(TT):
            r = dve.bn_stats(self.stats[:, t, :], self.x[par][:, t, :])
        r.then_inc(self.stats_done.sem, 1)
        dve.wait_ge(self.stats_done.sem, self.stats_done.all(n))
        dve.sem_inc(self.passed.sem, 1)
        for t in range(TT):
            r = dve.bn_aggr(self.moments[:, t, :], self.stats[:, t, :])
        r.then_inc(self.moments_done.sem, 1)
        dve.wait_ge(self.moments_done.sem, self.moments_done.all(n))
        dve.tensor_scalar(self.var[:, :], self.moments[:, :, 1], EPS, None, ALU.add).then_inc(self.var_done.sem, 1)

    def gpsimd_rstd(self, pool, n):
        pool.wait_ge(self.var_done.sem, self.var_done.all(n))
        pool.tensor_tensor(self.rstd[:, :], self.var[:, :], self.half[:, 0:TT], ALU.pow).then_inc(self.rstd_done.sem, 1)

    def vector_normalise(self, dve, n, par):
        dve.wait_ge(self.rstd_done.sem, self.rstd_done.all(n))
        dve.wait_ge(self.turned_done.sem, self.turned_done.all(n - 1))
        for t in range(TT):
            r = dve.tensor_scalar(self.normed[:, t, :], self.x[par][:, t, :], self.moments[:, t, 0:1],
                                  self.rstd[:, t:t + 1], ALU.subtract, ALU.mult)
        r.then_inc(self.normed_done.sem, 1)

    def channels(self, part):
        return range(part * CT // self.parts, (part + 1) * CT // self.parts)

    def tensor_turn(self, pe, n, part=0):
        pe.wait_ge(self.normed_done.sem, self.normed_done.all(n))
        self.turned_free(pe, n, part)
        for t in range(TT):
            for c in self.channels(part):
                r = pe.transpose(self.turned[:, c, t * P:(t + 1) * P], self.normed[:, t, c * P:(c + 1) * P],
                                 self.ident)
        r.then_inc(self.turned_done.sem, 1)

    def scalar_out(self, act, n, part=0, before=None):
        act.wait_ge(self.turned_done.sem, self.turned_done.at(n, part + 1))
        self.out_free(act, n)
        if before:
            tile, prev = before
            act.activation(tile[:, :, 0], prev[:, n, :], ACT.Copy)
        for c in self.channels(part):
            r = act.activation(self.out(c), self.turned[:, c, :], ACT.Identity,
                               bias=self.shift[:, c:c + 1], scale=self.scale[:, c:c + 1])
        r.then_inc(self.out_done.sem, 1)


class SplitWeights:
    STAGES = 4

    def __init__(self, ctx, nc, name, sem, chunks):
        self.chunks = chunks
        self.stage = [ctx.enter_context(nc.sbuf_tensor(f"{name}_stage{i}", [P, CT * L], F32))
                      for i in range(self.STAGES)]
        self.staged = [sem(f"staged{i}", 0) for i in range(self.STAGES)]
        self.hi_done = sem("w_hi_done", 0)
        self.done = sem("w_done", 0)

    def tile(self, i):
        return self.stage[i % self.STAGES][:, :].rearrange("p (c l) -> p c l", l=self.chunks[i][3])

    def sync_load(self, sp, i):
        if i >= self.STAGES:
            sp.wait_ge(self.done.sem, i + 1 - self.STAGES)
        sp.dma_start(self.tile(i), self.chunks[i][0]).then_inc(self.staged[i % self.STAGES].sem, 16)

    def scalar_hi(self, act, i):
        act.wait_ge(self.staged[i % self.STAGES].sem, 16 * (i // self.STAGES + 1))
        act.activation(self.chunks[i][1], self.tile(i), ACT.Copy).then_inc(self.hi_done.sem, 1)

    def vector_lo(self, dve, i):
        dve.wait_ge(self.hi_done.sem, i + 1)
        dve.tensor_tensor(self.chunks[i][2], self.tile(i), self.chunks[i][1], ALU.subtract)\
           .then_inc(self.done.sem, 1)


def split_product(pe, out, a, b, start, stop):
    pe.matmul(out, a[0], b[0], start=start, stop=False)
    pe.matmul(out, a[0], b[1], start=False, stop=False)
    return pe.matmul(out, a[1], b[0], start=False, stop=stop)


def time_mix(nc, held, x_in, x_out, first_state, v_rows, weights):
    with ExitStack() as ctx:
        def sb(name, shape):
            return ctx.enter_context(nc.sbuf_tensor(f"tm_{name}", shape, F32))

        sem = counter(held, nc, "tm")

        w_proj = {f: sb(f"w_{f}", [P, CT, C]) for f in "vkrgo"}
        w_mix1 = sb("w_mix1", [P, CT, 5 * DM])
        w_mix2 = sb("w_mix2", [P, C])
        w_mix2g = sb("w_mix2g", [DM, C])
        w_dec1 = sb("w_dec1", [P, CT, DD])
        w_dec2 = sb("w_dec2", [DD, C])
        vecs = sb("vecs", [P, len(TIME_VECS), CT])
        fixed = sb("fixed", [P, 3, P])
        pick = sb("pick", [P, S, P])
        head_sum = sb("head_sum", [P, CT, C // S])
        head_out = sb("head_out", [C // S, CT, P])
        prev = sb("prev", [P, B, CT])
        half = sb("half", [P, TT])
        eps = sb("eps", [P, 1])
        vec = {name: vecs[:, i, :] for i, name in enumerate(TIME_VECS)}
        ident, head_ones, centre = fixed[:, 0, :], fixed[:, 1, :], fixed[:, 2, :]

        x = [sb(f"x{i}", [P, TT, C]) for i in range(2)]
        res = sb("res", [P, TT, C])
        xa = sb("xa", [P, CT, L + 1])
        shift = sb("shift", [P, CT, L])
        mixed = [sb(f"mixed{i}", [P, CT, L]) for i in range(2)]
        mix_act = sb("mix_act", [P, L])
        mix_actg = sb("mix_actg", [DM, L])
        dec_act = sb("dec_act", [DD, L])
        decay_e = sb("decay_e", [P, CT, L])
        wT = [sb(f"wT{i}", [P, CT, L]) for i in range(2)]
        kT = [sb(f"kT{i}", [P, CT, L + 1]) for i in range(2)]
        vT = sb("vT", [P, CT, L + 1])
        rT = [sb(f"rT{i}", [P, CT, L]) for i in range(2)]
        gT = [sb(f"gT{i}", [P, CT, L]) for i in range(2)]
        g_half = sb("g_half", [P, CT, L])
        rkf = sb("rkf", [P, CT, L])
        now = sb("now", [P, CT, L])
        s0 = [sb(f"s0_{i}", [P, CT, S]) for i in range(2)]
        unit = [sb(f"unit{i}", [P, UW, L]) for i in range(RING)]
        y_sb = sb("y_sb", [P, CT, L])
        y_sq = decay_e
        head_rstd = sb("head_rstd", [C // S, L])
        yg = sb("yg", [P, CT, L])
        bank = [ctx.enter_context(nc.psum_tensor(f"tm_ps{i}", [P, CT, L], F32)) for i in range(4)]
        ps_turn, ps_mix, ps_proj, ps_y = bank

        weights_in = sem("weights_in", 0)
        passed = sem("passed", 0)
        first_in = sem("first_in", 0)
        proj_in = sem("proj_in", 0)
        x_loaded = sem("x_loaded", 16)
        res_loaded = sem("res_loaded", 16)
        s0_loaded = sem("s0_loaded", 16)
        v_stored = sem("v_stored", 16, 1)
        unit_loaded = [sem(f"unit{r}_loaded", 16 * UNITS // RING) for r in range(RING)]
        x_stored = sem("x_stored", 16, 1)
        consts_done = sem("consts_done", 0)
        shift_done = sem("shift_done", 1)
        mix_in_done = sem("mix_in_done", 1)
        mix_hidden = sem("mix_hidden", 1)
        mix_acted = sem("mix_acted", 1)
        mix_ps = sem("mix_ps", 5)
        mix_scaled = sem("mix_scaled", 5, 1)
        mix_added = sem("mix_added", 5, 1)
        dec_hidden = sem("dec_hidden", 1)
        dec_acted = sem("dec_acted", 1)
        proj_ps = sem("proj_ps", 5, 1)
        proj_out = sem("proj_out", 5, 1)
        decay_exp = sem("decay_exp", 1)
        g_done = sem("g_done", 1, 1)
        rkf_done = sem("rkf_done", 1)
        now_ps = sem("now_ps", 1, 1)
        now_done = sem("now_done", 1, 1)
        kv_done = sem("kv_done", UNITS, 2)
        scanned = sem("scanned", UNITS)
        read_out = sem("read_out", UNITS, 2)
        unit_summed = sem("unit_summed", UNITS, 1)
        y_copied = sem("y_copied", 1, 1)
        y_squared = sem("y_squared", 1)
        var_ps = sem("var_ps", 1)
        std_done = sem("std_done", 1, 2)
        rstd_done = sem("rstd_done", 1)
        rstd_ps = sem("rstd_ps", 1)
        y_normed = sem("y_normed", 1, 2)
        y_scaled = sem("y_scaled", 1)
        yg_done = sem("yg_done", 1, 2)
        out_ps = sem("out_ps", 1)
        x_added = sem("x_added", 1, 3)

        def turn_free(eng, n, _):
            eng.wait_ge(now_done.sem, now_done.all(n - 1))

        def xa_free(eng, n):
            eng.wait_ge(mix_added.sem, mix_added.all(n - 1))

        ln = LayerNorm(ctx, nc, "tm", sem, x, x_loaded, ps_turn, turn_free, lambda c: xa[:, c, 1:L + 1], xa_free,
                       vec["ln1_w"], vec["ln1_b"], ident, half, passed)

        ORDER = ["maa_v", "maa_k", "maa_r", "maa_w", "maa_g"]
        ln.normed_done.ahead = 2
        ROW = {"maa_w": 0, "maa_k": 1, "maa_v": 2, "maa_r": 3, "maa_g": 4}

        block = ctx.enter_context(nc.Block())

        @block.sync
        def _(sp):
            grant(sp, [x_stored, v_stored])
            loads = [(fixed, "fixed"), (vecs, "time_vecs"), (prev, "prev1"), (w_mix1, "maa_w1")]
            for tile, name in loads:
                sp.dma_start(tile[:, :, :], weights[name]).then_inc(first_in.sem, 16)
            sp.dma_start(w_mix2[:, :], weights["maa_w2"][0:P, :]).then_inc(first_in.sem, 16)
            sp.dma_start(w_mix2g[:, :], weights["maa_w2"][P:P + DM, :]).then_inc(first_in.sem, 16)

            def load(n, par):
                sp.wait_ge(ln.stats_done.sem, ln.stats_done.all(n - 1))
                sp.sem_inc(passed.sem, 1)
                sp.wait_ge(ln.normed_done.sem, ln.normed_done.all(n - 2))
                sp.sem_inc(passed.sem, 1)
                sp.dma_start(x[par][:, :, :], x_in[n, :, :].rearrange("(t p) c -> p t c", p=P))\
                  .then_inc(x_loaded.sem, 16)
                sp.wait_ge(kv_done.sem, kv_done.all(n - 2))
                sp.sem_inc(passed.sem, 1)
                sp.dma_start(s0[par][:, :, :], first_state[n, :, :].rearrange("(c p) s -> p c s", p=P))\
                  .then_inc(s0_loaded.sem, 16)

            def store_v(n, par):
                sp.wait_ge(proj_out.sem, proj_out.at(n, 1))
                sp.dma_start(v_rows[par].rearrange("(c p) l -> p c l", p=P), vT[:, :, 0:L])\
                  .then_inc(v_stored.sem, 16)
                sp.wait_ge(v_stored.sem, v_stored.all(n))
                sp.sem_inc(passed.sem, 1)

            def load_unit(n, par, u):
                sp.wait_ge(unit_summed.sem, unit_summed.at(n, u + 1 - RING))
                c, h = u // 2, u % 2
                rows = v_rows[par].rearrange("(h s) l -> h (s l)", s=S)
                src = rows[c * HT:(c + 1) * HT, h * UW * L:(h + 1) * UW * L]
                sp.dma_start(unit[u % RING][:, :, :].rearrange("p s l -> p (s l)"),
                             src.unsqueeze(1).broadcast_to([HT, S, UW * L])).then_inc(unit_loaded[u % RING].sem, 16)

            def load_residual(n):
                sp.wait_ge(x_stored.sem, x_stored.all(n - 1))
                sp.sem_inc(passed.sem, 1)
                sp.dma_start(res[:, :, :], x_in[n, :, :].rearrange("(t p) c -> p t c", p=P))\
                  .then_inc(res_loaded.sem, 16)

            def start():
                load(0, 0)
                for tile, name in [(w_proj["v"], "Wv"), (w_proj["k"], "Wk"), (w_proj["r"], "Wr"),
                                   (w_dec1, "decay_w1")]:
                    sp.dma_start(tile[:, :, :], weights[name]).then_inc(proj_in.sem, 16)
                sp.dma_start(w_dec2[:, :], weights["decay_w2"]).then_inc(proj_in.sem, 16)
                for tile, name in [(w_proj["g"], "Wg"), (pick, "pick"), (head_sum, "head_sum"), (w_proj["o"], "Wo"),
                                   (head_out, "head_out")]:
                    sp.dma_start(tile[:, :, :], weights[name]).then_inc(weights_in.sem, 16)
                store_v(0, 0)
                for u in range(RING - 1):
                    load_unit(0, 0, u)

            def step(n, par, prev_batch, next_batch):
                if next_batch:
                    load(n + 1, 1 - par)
                if prev_batch:
                    load_residual(n - 1)
                for u in range(RING - 1, UNITS):
                    load_unit(n, par, u)
                if next_batch:
                    store_v(n + 1, 1 - par)
                    for u in range(RING - 1):
                        load_unit(n + 1, 1 - par, u)

            def finish(n):
                load_residual(n)
                sp.wait_ge(x_stored.sem, x_stored.all(n))

            over_three_stages(sp, start, step, finish)

        @block.vector
        def _(dve):
            dve.memset(half[:, :], -0.5).then_inc(consts_done.sem, 1)
            dve.memset(eps[:, :], EPS).then_inc(consts_done.sem, 1)
            dve.memset(kT[0][:, :, 0:1], 0.0).then_inc(consts_done.sem, 1)
            dve.memset(kT[1][:, :, 0:1], 0.0).then_inc(consts_done.sem, 1)
            dve.memset(vT[:, :, 0:1], 0.0).then_inc(consts_done.sem, 1)
            grant(dve, [ln.stats_done, ln.normed_done, mix_scaled, read_out, now_done, g_done, yg_done, x_added, y_normed])
            dve.wait_ge(first_in.sem, 16 * 6)

            def shifts(n, par):
                dve.wait_ge(ln.out_done.sem, ln.out_done.all(n))
                dve.tensor_tensor(shift[:, :, :], xa[:, :, 0:L], xa[:, :, 1:L + 1], ALU.subtract)\
                   .then_inc(shift_done.sem, 1)
                dve.wait_ge(shift_done.sem, shift_done.all(n))
                dve.wait_ge(proj_ps.sem, proj_ps.all(n - 1))
                for c in range(CT):
                    r = dve.scalar_tensor_tensor(mixed[1][:, c, :], shift[:, c, :], vec["maa_x"][:, c:c + 1],
                                                 xa[:, c, 1:L + 1], ALU.mult, ALU.add)
                r.then_inc(mix_in_done.sem, 1)

            def mix(n, j):
                dve.wait_ge(mix_ps.sem, mix_ps.at(n, j + 1))
                if j >= 2:
                    dve.wait_ge(proj_ps.sem, proj_ps.at(n, j - 1))
                for c in range(CT):
                    r = dve.scalar_tensor_tensor(mixed[j % 2][:, c, :], ps_mix[:, c, :], vec[ORDER[j]][:, c:c + 1],
                                                 shift[:, c, :], ALU.add, ALU.mult)
                r.then_inc(mix_scaled.sem, 1)

            def silu(n, par):
                dve.wait_ge(proj_out.sem, proj_out.at(n, 5))
                dve.scalar_tensor_tensor(gT[par][:, :, :], gT[par][:, :, :], 1.0, g_half[:, :, :], ALU.add, ALU.mult)\
                   .then_inc(g_done.sem, 1)

            def rkf_part(n, par):
                dve.wait_ge(proj_out.sem, proj_out.at(n, 3))
                dve.wait_ge(now_ps.sem, now_ps.all(n - 1))
                for c in range(CT):
                    r = dve.scalar_tensor_tensor(rkf[:, c, :], kT[par][:, c, 1:L + 1], vec["faaaa"][:, c:c + 1],
                                                 rT[par][:, c, :], ALU.mult, ALU.mult)
                r.then_inc(rkf_done.sem, 1)

            def now_part(n, par):
                dve.wait_ge(now_ps.sem, now_ps.all(n))
                dve.wait_ge(unit_summed.sem, unit_summed.at(n - 1, UNITS - 1))
                dve.tensor_tensor(now[:, :, :], ps_turn[:, :, :], vT[:, :, 1:L + 1], ALU.mult)\
                   .then_inc(now_done.sem, 1)

            def unit_part(n, par, u):
                c = u // 2
                dve.wait_ge(kv_done.sem, kv_done.at(n, u + 1))
                if u == 0:
                    dve.wait_ge(decay_exp.sem, decay_exp.all(n))
                buf = unit[u % RING]
                for s in range(UW):
                    r = dve.tensor_tensor_scan(buf[:, s, 1:L], wT[par][:, c, 0:L - 1], buf[:, s, 1:L],
                                               buf[:, s, 0:1], ALU.mult, ALU.add)
                r.then_inc(scanned.sem, 1)
                dve.wait_ge(scanned.sem, scanned.at(n, u + 1))
                dve.tensor_tensor(buf[:, :, :], buf[:, :, :],
                                  rT[par][:, c, :].unsqueeze(1).broadcast_to([P, UW, L]), ALU.mult)\
                   .then_inc(read_out.sem, 1)

            def norm_rstd(n):
                dve.wait_ge(std_done.sem, std_done.all(n))
                dve.reciprocal(head_rstd[:, :], head_rstd[:, :]).then_inc(rstd_done.sem, 1)

            def norm_apply(n):
                dve.wait_ge(rstd_ps.sem, rstd_ps.all(n))
                dve.tensor_tensor(y_sb[:, :, :], y_sb[:, :, :], ps_turn[:, :, :], ALU.mult).then_inc(y_normed.sem, 1)

            def gate(n, par):
                dve.wait_ge(y_scaled.sem, y_scaled.all(n))
                dve.wait_ge(g_done.sem, g_done.all(n))
                dve.tensor_tensor(yg[:, :, :], y_sb[:, :, :], gT[par][:, :, :], ALU.mult).then_inc(yg_done.sem, 1)

            def residual(n):
                dve.wait_ge(out_ps.sem, out_ps.all(n))
                dve.wait_ge(res_loaded.sem, res_loaded.all(n))
                dve.tensor_tensor(res[:, :, :], res[:, :, :],
                                  ps_mix[:, :, :].rearrange("p (t a) l -> p t (a l)", t=TT), ALU.add)\
                   .then_inc(x_added.sem, 1)

            def start():
                ln.vector_moments(dve, 0, 0)
                ln.vector_normalise(dve, 0, 0)
                shifts(0, 0)
                for j in range(5):
                    mix(0, j)
                rkf_part(0, 0)
                now_part(0, 0)

            def step(n, par, prev_batch, next_batch):
                for u in range(UNITS):
                    if next_batch:
                        if u == 0:
                            ln.vector_moments(dve, n + 1, 1 - par)
                        if u >= 3:
                            mix(n + 1, u - 3)
                        if u == 7:
                            rkf_part(n + 1, 1 - par)
                    if prev_batch:
                        if u == 5:
                            norm_apply(n - 1)
                        if u == 6:
                            gate(n - 1, 1 - par)
                    unit_part(n, par, u)
                    if next_batch:
                        if u == 0:
                            ln.vector_normalise(dve, n + 1, 1 - par)
                        if u == 1:
                            shifts(n + 1, 1 - par)
                        if u == 7:
                            now_part(n + 1, 1 - par)
                    if u == 2:
                        silu(n, par)
                    if prev_batch and u == 3:
                        norm_rstd(n - 1)
                    if prev_batch and u == 7:
                        residual(n - 1)

            def finish(n):
                norm_rstd(n)
                norm_apply(n)
                gate(n, n % 2)
                residual(n)

            over_three_stages(dve, start, step, finish)

        @block.gpsimd
        def _(pool):
            grant(pool, [mix_added, kv_done])
            pool.wait_ge(consts_done.sem, 5)

            def add(n, j):
                pool.wait_ge(mix_scaled.sem, mix_scaled.at(n, j + 1))
                pool.tensor_tensor(mixed[j % 2][:, :, :], mixed[j % 2][:, :, :], xa[:, :, 1:L + 1], ALU.add)\
                    .then_inc(mix_added.sem, 1)

            def unit_part(n, par, u):
                c, h = u // 2, u % 2
                buf = unit[u % RING]
                pool.wait_ge(unit_loaded[u % RING].sem, unit_loaded[u % RING].at(n, 16 * (u // RING + 1)))
                if u == 0:
                    pool.wait_ge(proj_out.sem, proj_out.at(n, 2))
                    pool.wait_ge(s0_loaded.sem, s0_loaded.all(n))
                pool.tensor_tensor(buf[:, :, 1:L], buf[:, :, 1:L],
                                   kT[par][:, c, 1:L].unsqueeze(1).broadcast_to([P, UW, L - 1]), ALU.mult)
                pool.tensor_copy(buf[:, :, 0:1], s0[par][:, c, h * UW:(h + 1) * UW].unsqueeze(2))\
                    .then_inc(kv_done.sem, 1)

            def start():
                ln.gpsimd_rstd(pool, 0)
                for j in range(5):
                    add(0, j)

            def step(n, par, prev_batch, next_batch):
                unit_part(n, par, 0)
                for u in range(UNITS):
                    if next_batch and u == 0:
                        ln.gpsimd_rstd(pool, n + 1)
                    if u + 1 < UNITS:
                        unit_part(n, par, u + 1)
                    if next_batch and u >= 3:
                        add(n + 1, u - 3)

            over_three_stages(pool, start, step, lambda n: None)

        @block.scalar
        def _(act):
            grant(act, [proj_out, std_done, y_copied])
            act.wait_ge(first_in.sem, 16 * 6)
            act.wait_ge(consts_done.sem, 5)

            def mix_tanh(n):
                act.wait_ge(mix_hidden.sem, mix_hidden.all(n))
                act.activation(mix_act[:, :], ps_turn[:, 0, :], ACT.Tanh)
                act.activation(mix_actg[:, :], ps_turn[0:DM, 1, :], ACT.Tanh).then_inc(mix_acted.sem, 1)

            def v_out(n, par):
                act.wait_ge(proj_ps.sem, proj_ps.at(n, 1))
                act.wait_ge(now_done.sem, now_done.all(n - 1))
                act.wait_ge(v_stored.sem, v_stored.all(n - 1))
                act.wait_ge(read_out.sem, read_out.all(n - 2))
                act.activation(vT[:, :, 1:L + 1], ps_proj[:, :, :], ACT.Copy).then_inc(proj_out.sem, 1)

            def k_out(n, par):
                act.wait_ge(proj_ps.sem, proj_ps.at(n, 2))
                act.activation(kT[par][:, :, 1:L + 1], ps_proj[:, :, :], ACT.Copy).then_inc(proj_out.sem, 1)

            def r_out(n, par):
                act.wait_ge(proj_ps.sem, proj_ps.at(n, 3))
                act.activation(rT[par][:, :, :], ps_proj[:, :, :], ACT.Copy).then_inc(proj_out.sem, 1)

            def decay(n, par):
                act.wait_ge(dec_hidden.sem, dec_hidden.all(n))
                act.activation(dec_act[:, :], ps_proj[0:DD, 0, :], ACT.Tanh).then_inc(dec_acted.sem, 1)
                act.wait_ge(proj_ps.sem, proj_ps.at(n, 4))
                for c in range(CT):
                    r = act.activation(decay_e[:, c, :], ps_proj[:, c, :], ACT.Exp, bias=vec["time_decay"][:, c:c + 1])
                r.then_inc(proj_out.sem, 1)
                act.wait_ge(proj_out.sem, proj_out.at(n, 4))
                act.activation(wT[par][:, :, :], decay_e[:, :, :], ACT.Exp, scale=-1.0).then_inc(decay_exp.sem, 1)

            def g_out(n, par):
                act.wait_ge(proj_ps.sem, proj_ps.at(n, 5))
                act.wait_ge(yg_done.sem, yg_done.all(n - 2))
                act.wait_ge(g_done.sem, g_done.all(n - 1))
                act.activation(gT[par][:, :, :], ps_proj[:, :, :], ACT.Tanh, scale=0.5)
                act.activation(g_half[:, :, :], ps_proj[:, :, :], ACT.Copy, scale=0.5).then_inc(proj_out.sem, 1)

            def y_out(n):
                act.wait_ge(unit_summed.sem, unit_summed.all(n))
                act.wait_ge(yg_done.sem, yg_done.all(n - 1))
                act.activation(y_sb[:, :, :], ps_y[:, :, :], ACT.Copy).then_inc(y_copied.sem, 1)

            def y_square(n, later):
                act.wait_ge(y_copied.sem, y_copied.all(n))
                act.wait_ge(decay_exp.sem, decay_exp.all(n + later))
                act.activation(y_sq[:, :, :], y_sb[:, :, :], ACT.Square).then_inc(y_squared.sem, 1)

            def norm_std(n):
                act.wait_ge(var_ps.sem, var_ps.all(n))
                act.activation(head_rstd[:, :], ps_proj[0:C // S, 0, :], ACT.Sqrt, bias=eps[0:C // S, 0:1])\
                   .then_inc(std_done.sem, 1)

            def store(n):
                act.wait_ge(x_added.sem, x_added.all(n))
                act.sem_inc(passed.sem, 1)
                act.dma_start(x_out[n, :, :].rearrange("(t p) c -> p t c", p=P), res[:, :, :])\
                   .then_inc(x_stored.sem, 16)

            def norm_scale(n):
                act.wait_ge(y_normed.sem, y_normed.all(n))
                for c in range(CT):
                    r = act.activation(y_sb[:, c, :], y_sb[:, c, :], ACT.Identity,
                                       bias=vec["gn_b"][:, c:c + 1], scale=vec["gn_w"][:, c:c + 1])
                r.then_inc(y_scaled.sem, 1)

            def start():
                ln.scalar_out(act, 0, before=(xa, prev))
                mix_tanh(0)
                v_out(0, 0)
                k_out(0, 0)
                r_out(0, 0)
                decay(0, 0)

            def step(n, par, prev_batch, next_batch):
                if prev_batch:
                    y_square(n - 1, 1)
                g_out(n, par)
                if next_batch:
                    ln.scalar_out(act, n + 1, before=(xa, prev))
                if next_batch:
                    mix_tanh(n + 1)
                if prev_batch:
                    norm_std(n - 1)
                if next_batch:
                    v_out(n + 1, 1 - par)
                if prev_batch:
                    norm_scale(n - 1)
                if next_batch:
                    k_out(n + 1, 1 - par)
                    r_out(n + 1, 1 - par)
                    decay(n + 1, 1 - par)
                y_out(n)
                if prev_batch:
                    store(n - 1)

            def finish(n):
                y_square(n, 0)
                norm_std(n)
                norm_scale(n)
                store(n)

            over_three_stages(act, start, step, finish)

        @block.tensor
        def _(pe):
            grant(pe, [ln.turned_done, proj_ps, now_ps, unit_summed])
            pe.wait_ge(first_in.sem, 16 * 6)

            def hidden(n):
                pe.wait_ge(mix_in_done.sem, mix_in_done.all(n))
                pe.wait_ge(ln.out_done.sem, ln.out_done.all(n))
                for c in range(CT):
                    pe.matmul(ps_turn[:, 0, :], w_mix1[:, c, 0:P], mixed[1][:, c, :], start=c == 0, stop=c == CT - 1)
                for c in range(CT):
                    r = pe.matmul(ps_turn[0:DM, 1, :], w_mix1[:, c, P:P + DM], mixed[1][:, c, :],
                                  start=c == 0, stop=c == CT - 1)
                r.then_inc(mix_hidden.sem, 1)

            def mixer(n, j):
                if j == 0:
                    pe.wait_ge(mix_acted.sem, mix_acted.all(n))
                    pe.wait_ge(mix_scaled.sem, mix_scaled.all(n - 1))
                    pe.wait_ge(x_added.sem, x_added.all(n - 3))
                else:
                    pe.wait_ge(mix_scaled.sem, mix_scaled.at(n, j))
                row = ROW[ORDER[j]] * DM
                for c in range(CT):
                    if row < P:
                        w, a = w_mix2[row:row + DM, c * P:(c + 1) * P], mix_act[row:row + DM, :]
                    else:
                        w, a = w_mix2g[:, c * P:(c + 1) * P], mix_actg[:, :]
                    r = pe.matmul(ps_mix[:, c, :], w, a, start=True, stop=True)
                r.then_inc(mix_ps.sem, 1)

            def project(n, j, f):
                pe.wait_ge(mix_added.sem, mix_added.at(n, j + 1))
                if j == 0:
                    pe.wait_ge(std_done.sem, std_done.all(n - 2))
                else:
                    pe.wait_ge(proj_out.sem, proj_out.at(n, j))
                for m in range(CT):
                    for c in range(CT):
                        r = pe.matmul(ps_proj[:, m, :], w_proj[f][:, c, m * P:(m + 1) * P], mixed[j % 2][:, c, :],
                                      start=c == 0, stop=c == CT - 1)
                r.then_inc(proj_ps.sem, 1)

            def decay_hidden(n):
                pe.wait_ge(mix_added.sem, mix_added.at(n, 4))
                pe.wait_ge(proj_out.sem, proj_out.at(n, 3))
                for c in range(CT):
                    r = pe.matmul(ps_proj[0:DD, 0, :], w_dec1[:, c, :], mixed[1][:, c, :],
                                  start=c == 0, stop=c == CT - 1)
                r.then_inc(dec_hidden.sem, 1)

            def decay_out(n):
                pe.wait_ge(dec_acted.sem, dec_acted.all(n))
                for c in range(CT):
                    r = pe.matmul(ps_proj[:, c, :], w_dec2[:, c * P:(c + 1) * P], dec_act[:, :],
                                  start=True, stop=True)
                r.then_inc(proj_ps.sem, 1)

            def now_part(n):
                pe.wait_ge(rkf_done.sem, rkf_done.all(n))
                pe.wait_ge(mix_acted.sem, mix_acted.all(n))
                pe.wait_ge(y_normed.sem, y_normed.all(n - 2))
                for c in range(CT):
                    r = pe.matmul(ps_turn[:, c, :], head_ones, rkf[:, c, :], start=True, stop=True)
                r.then_inc(now_ps.sem, 1)

            def unit_part(n, u):
                c, h = u // 2, u % 2
                if u == 0:
                    pe.wait_ge(y_copied.sem, y_copied.all(n - 1))
                    pe.wait_ge(now_done.sem, now_done.all(n))
                if h == 0:
                    pe.matmul(ps_y[:, c, :], centre, now[:, c, :], start=True, stop=False)
                pe.wait_ge(read_out.sem, read_out.at(n, u + 1))
                for s in range(UW):
                    r = pe.matmul(ps_y[:, c, :], pick[:, h * UW + s, :], unit[u % RING][:, s, :],
                                  start=False, stop=h == 1 and s == UW - 1)
                r.then_inc(unit_summed.sem, 1)

            def variance(n, later):
                pe.wait_ge(y_squared.sem, y_squared.all(n))
                pe.wait_ge(proj_out.sem, proj_out.all(n + later))
                for c in range(CT):
                    r = pe.matmul(ps_proj[0:C // S, 0, :], head_sum[:, c, :], y_sq[:, c, :],
                                  start=c == 0, stop=c == CT - 1)
                r.then_inc(var_ps.sem, 1)

            def spread_rstd(n, later):
                pe.wait_ge(rstd_done.sem, rstd_done.all(n))
                if later == 2:
                    pe.wait_ge(mix_acted.sem, mix_acted.all(n + 2))
                else:
                    pe.wait_ge(now_done.sem, now_done.all(n + later))
                for c in range(CT):
                    r = pe.matmul(ps_turn[:, c, :], head_out[:, c, :], head_rstd[:, :], start=True, stop=True)
                r.then_inc(rstd_ps.sem, 1)

            def output(n, later):
                pe.wait_ge(yg_done.sem, yg_done.all(n))
                pe.wait_ge(mix_scaled.sem, mix_scaled.all(n + later))
                out = ps_mix[:, :, :].rearrange("p (t a) l -> p t (a l)", t=TT)
                for t in range(TT):
                    for c in range(CT):
                        r = pe.matmul(out[:, t, :], yg[:, c, t * P:(t + 1) * P], w_proj["o"][:, c, :],
                                      start=c == 0, stop=c == CT - 1)
                r.then_inc(out_ps.sem, 1)

            def start():
                ln.tensor_turn(pe, 0)
                hidden(0)
                mixer(0, 0)
                mixer(0, 1)
                pe.wait_ge(proj_in.sem, 16 * 5)
                for j in range(3):
                    project(0, j, "vkr"[j])
                    mixer(0, j + 2)
                decay_hidden(0)
                now_part(0)
                decay_out(0)
                pe.wait_ge(weights_in.sem, 16 * 5)

            def step(n, par, prev_batch, next_batch):
                for u in range(UNITS):
                    if u == 0:
                        project(n, 4, "g")
                    if u == 1:
                        if next_batch:
                            ln.tensor_turn(pe, n + 1)
                    if u == 2:
                        if prev_batch:
                            variance(n - 1, 1)
                        if next_batch:
                            hidden(n + 1)
                            mixer(n + 1, 0)
                    if u == 3 and next_batch:
                        mixer(n + 1, 1)
                    if u == 4 and prev_batch:
                        spread_rstd(n - 1, 2 if next_batch else 1)
                    if next_batch and u in (4, 5, 6):
                        project(n + 1, u - 4, "vkr"[u - 4])
                        mixer(n + 1, u - 2)
                    if u == 7:
                        if next_batch:
                            decay_hidden(n + 1)
                            now_part(n + 1)
                            decay_out(n + 1)
                        if prev_batch:
                            output(n - 1, 2 if next_batch else 1)
                    unit_part(n, u)

            def finish(n):
                variance(n, 0)
                spread_rstd(n, 0)
                output(n, 0)

            over_three_stages(pe, start, step, finish)


def channel_mix(nc, held, x_in, x_out, weights):
    with ExitStack() as ctx:
        def sb(name, shape, dtype=F32):
            return ctx.enter_context(nc.sbuf_tensor(f"cm_{name}", shape, dtype))

        def parts(name, shape):
            return [sb(f"{name}_{part}", shape, F32R) for part in ("hi", "lo")]

        sem = counter(held, nc, "cm")

        w = {f: parts(f"w{f}", [P, CT, C]) for f in "krv"}
        chunks = [(weights["fW" + f][:, c:c + 2, :], w[f][0][:, c:c + 2, :], w[f][1][:, c:c + 2, :], C)
                  for f in "krv" for c in (0, 2)]
        vecs = sb("vecs", [P, len(CHAN_VECS), CT])
        vec = {name: vecs[:, i, :] for i, name in enumerate(CHAN_VECS)}
        fixed = sb("fixed", [P, 3, P])
        prev = sb("prev", [P, B, CT])
        half = sb("half", [P, TT])
        x = [sb(f"x{i}", [P, TT, C]) for i in range(2)]
        xc = sb("xc", [P, CT, L + 1])
        shift = sb("shift", [P, CT, L])
        mixed = {f: sb(f"x{f}", [P, CT, L]) for f in "kr"}
        mixed_parts = {f: parts(f"x{f}", [P, CT, L]) for f in "kr"}
        relu = sb("relu", [P, CT, L])
        kk = sb("kk", [P, CT, L])
        kk_parts = parts("kk", [P, CT, L])
        gate = sb("gate", [P, TT, C])
        gated = sb("gated", [P, TT, C])
        res = sb("res", [P, TT, C])
        ps_turn = ctx.enter_context(nc.psum_tensor("cm_ps_turn", [P, CT, L], F32))
        ps_k = ctx.enter_context(nc.psum_tensor("cm_ps_k", [P, CT, L], F32))
        ps_r = ctx.enter_context(nc.psum_tensor("cm_ps_r", [P, TT, C], F32))
        ps_v = ctx.enter_context(nc.psum_tensor("cm_ps_v", [P, TT, C], F32))

        first_in = sem("first_in", 0)
        split = SplitWeights(ctx, nc, "cm", sem, chunks)
        passed = sem("passed", 0)
        consts_done = sem("consts_done", 0)
        x_loaded = sem("x_loaded", 16)
        res_loaded = sem("res_loaded", 16)
        x_stored = sem("x_stored", 16, 1)
        shift_done = sem("shift_done", 1)
        mixed_done = {f: sem(f"x{f}_done", 1, 1) for f in "kr"}
        mixed_hi_done = {f: sem(f"x{f}_hi_done", 1) for f in "kr"}
        mixed_split = {f: sem(f"x{f}_split", 1, 1) for f in "kr"}
        k_ps = sem("k_ps", 1, 1)
        r_ps = sem("r_ps", 1, 2)
        v_ps = sem("v_ps", 1, 1)
        relu_done = sem("relu_done", 1, 1)
        kk_done = sem("kk_done", 1)
        kk_hi_done = sem("kk_hi_done", 1)
        kk_split = sem("kk_split", 1, 1)
        gate_done = sem("gate_done", 1, 1)
        gated_done = sem("gated_done", 1, 1)
        x_added = sem("x_added", 1, 1)

        ln = LayerNorm(ctx, nc, "cm", sem, x, x_loaded, ps_turn,
                       lambda eng, n, _: eng.wait_ge(mixed_done["r"].sem, mixed_done["r"].all(n - 1)),
                       lambda c: xc[:, c, 1:L + 1],
                       lambda eng, n: eng.wait_ge(mixed_done["r"].sem, mixed_done["r"].all(n - 1)),
                       vec["ln2_w"], vec["ln2_b"], fixed[:, 0, :], half, passed)
        ln.normed_done.ahead = 2

        block = ctx.enter_context(nc.Block())

        @block.sync
        def _(sp):
            grant(sp, [x_stored])

            def load(n, par):
                sp.wait_ge(ln.stats_done.sem, ln.stats_done.all(n - 1))
                sp.sem_inc(passed.sem, 1)
                sp.wait_ge(ln.normed_done.sem, ln.normed_done.all(n - 2))
                sp.sem_inc(passed.sem, 1)
                sp.dma_start(x[par][:, :, :], x_in[n, :, :].rearrange("(t p) c -> p t c", p=P))\
                  .then_inc(x_loaded.sem, 16)

            def residual(n):
                sp.wait_ge(x_stored.sem, x_stored.all(n - 1))
                sp.sem_inc(passed.sem, 1)
                sp.dma_start(res[:, :, :], x_in[n, :, :].rearrange("(t p) c -> p t c", p=P))\
                  .then_inc(res_loaded.sem, 16)

            def first():
                sp.dma_start(x[0][:, :, :], x_in[0, :, :].rearrange("(t p) c -> p t c", p=P))\
                  .then_inc(x_loaded.sem, 16)
                for tile, name in [(fixed, "fixed"), (vecs, "chan_vecs"), (prev, "prev0")]:
                    sp.dma_start(tile[:, :, :], weights[name]).then_inc(first_in.sem, 16)
                for i in range(6):
                    split.sync_load(sp, i)

            def step(n, par):
                load(n + 1, 1 - par)
                residual(n)

            def last(n, par):
                residual(n)
                sp.wait_ge(x_stored.sem, x_stored.all(n))

            over_batches(sp, first, step, last)

        @block.vector
        def _(dve):
            dve.memset(half[:, :], -0.5).then_inc(consts_done.sem, 1)
            grant(dve, [ln.stats_done, ln.normed_done, mixed_done["k"], mixed_done["r"], mixed_split["k"], mixed_split["r"],
                        kk_split, gated_done, x_added])
            dve.wait_ge(first_in.sem, 16 * 3)

            def norm(n, par):
                ln.vector_moments(dve, n, par)
                ln.vector_normalise(dve, n, par)

            def mix(n):
                dve.wait_ge(ln.out_done.sem, ln.out_done.all(n))
                dve.tensor_tensor(shift[:, :, :], xc[:, :, 0:L], xc[:, :, 1:L + 1], ALU.subtract)\
                   .then_inc(shift_done.sem, 1)
                dve.wait_ge(shift_done.sem, shift_done.all(n))
                for f in "kr":
                    dve.wait_ge(mixed_split[f].sem, mixed_split[f].all(n - 1))
                    for c in range(CT):
                        r = dve.scalar_tensor_tensor(mixed[f][:, c, :], shift[:, c, :], vec["fmaa_" + f][:, c:c + 1],
                                                     xc[:, c, 1:L + 1], ALU.mult, ALU.add)
                    r.then_inc(mixed_done[f].sem, 1)

            def mixed_lo(n, f, read):
                dve.wait_ge(mixed_hi_done[f].sem, mixed_hi_done[f].all(n))
                dve.wait_ge(read.sem, read.all(n - 1))
                dve.tensor_tensor(mixed_parts[f][1][:, :, :], mixed[f][:, :, :], mixed_parts[f][0][:, :, :],
                                  ALU.subtract).then_inc(mixed_split[f].sem, 1)

            def kk_lo(n):
                dve.wait_ge(kk_hi_done.sem, kk_hi_done.all(n))
                dve.wait_ge(v_ps.sem, v_ps.all(n - 1))
                dve.tensor_tensor(kk_parts[1][:, :, :], kk[:, :, :], kk_parts[0][:, :, :], ALU.subtract)\
                   .then_inc(kk_split.sem, 1)

            def back(n, par):
                dve.wait_ge(v_ps.sem, v_ps.all(n))
                dve.wait_ge(gate_done.sem, gate_done.all(n))
                dve.wait_ge(x_added.sem, x_added.all(n - 1))
                dve.scalar_tensor_tensor(gated[:, :, :], gate[:, :, :], 1.0, ps_v[:, :, :], ALU.add, ALU.mult)\
                   .then_inc(gated_done.sem, 1)
                dve.wait_ge(gated_done.sem, gated_done.all(n))
                dve.wait_ge(res_loaded.sem, res_loaded.all(n))
                dve.scalar_tensor_tensor(res[:, :, :], gated[:, :, :], 0.5, res[:, :, :], ALU.mult, ALU.add)\
                   .then_inc(x_added.sem, 1)

            def first():
                norm(0, 0)
                for i in range(2):
                    split.vector_lo(dve, i)
                mix(0)
                mixed_lo(0, "k", k_ps)
                mixed_lo(0, "r", r_ps)
                for i in range(2, 6):
                    split.vector_lo(dve, i)

            def step(n, par):
                norm(n + 1, 1 - par)
                kk_lo(n)
                mix(n + 1)
                mixed_lo(n + 1, "k", k_ps)
                mixed_lo(n + 1, "r", r_ps)
                back(n, par)

            def last(n, par):
                kk_lo(n)
                back(n, par)

            over_batches(dve, first, step, last)

        @block.gpsimd
        def _(pool):
            pool.wait_ge(consts_done.sem, 1)
            over_batches(pool, lambda: ln.gpsimd_rstd(pool, 0), lambda n, par: ln.gpsimd_rstd(pool, n + 1),
                         lambda n, par: None)

        @block.scalar
        def _(act):
            grant(act, [relu_done, gate_done])
            act.wait_ge(first_in.sem, 16 * 3)

            def mixed_hi(n, f, read):
                act.wait_ge(mixed_done[f].sem, mixed_done[f].all(n))
                act.wait_ge(read.sem, read.all(n - 1))
                act.activation(mixed_parts[f][0][:, :, :], mixed[f][:, :, :], ACT.Copy)\
                   .then_inc(mixed_hi_done[f].sem, 1)

            def squares(n):
                act.wait_ge(k_ps.sem, k_ps.all(n))
                act.activation(relu[:, :, :], ps_k[:, :, :], ACT.Relu).then_inc(relu_done.sem, 1)
                act.wait_ge(relu_done.sem, relu_done.all(n))
                act.wait_ge(kk_split.sem, kk_split.all(n - 1))
                act.activation(kk[:, :, :], relu[:, :, :], ACT.Square).then_inc(kk_done.sem, 1)
                act.wait_ge(kk_done.sem, kk_done.all(n))
                act.wait_ge(v_ps.sem, v_ps.all(n - 1))
                act.activation(kk_parts[0][:, :, :], kk[:, :, :], ACT.Copy).then_inc(kk_hi_done.sem, 1)

            def store(n):
                act.wait_ge(x_added.sem, x_added.all(n))
                act.sem_inc(passed.sem, 1)
                act.dma_start(x_out[n, :, :].rearrange("(t p) c -> p t c", p=P), res[:, :, :])\
                   .then_inc(x_stored.sem, 16)

            def gates(n):
                act.wait_ge(r_ps.sem, r_ps.all(n))
                act.wait_ge(gated_done.sem, gated_done.all(n - 1))
                act.activation(gate[:, :, :], ps_r[:, :, :], ACT.Tanh, scale=0.5).then_inc(gate_done.sem, 1)

            def first():
                for i in range(2):
                    split.scalar_hi(act, i)
                ln.scalar_out(act, 0, before=(xc, prev))
                mixed_hi(0, "k", k_ps)
                mixed_hi(0, "r", r_ps)
                for i in range(2, 6):
                    split.scalar_hi(act, i)

            def step(n, par):
                squares(n)
                ln.scalar_out(act, n + 1, before=(xc, prev))
                mixed_hi(n + 1, "k", k_ps)
                gates(n)
                mixed_hi(n + 1, "r", r_ps)
                store(n)

            def last(n, par):
                squares(n)
                gates(n)
                store(n)

            over_batches(act, first, step, last)

        @block.tensor
        def _(pe):
            grant(pe, [ln.turned_done, k_ps, r_ps, v_ps])
            pe.wait_ge(first_in.sem, 16 * 3)

            def back(n, par, next_batch):
                pe.wait_ge(split.done.sem, 2)
                pe.wait_ge(mixed_split["k"].sem, mixed_split["k"].all(n))
                pe.wait_ge(relu_done.sem, relu_done.all(n - 1))
                for m in range(CT):
                    for c in range(CT):
                        r = split_product(pe, ps_k[:, m, :], [a[:, c, m * P:(m + 1) * P] for a in w["k"]],
                                          [a[:, c, :] for a in mixed_parts["k"]], c == 0, c == CT - 1)
                r.then_inc(k_ps.sem, 1)
                if next_batch:
                    ln.tensor_turn(pe, n + 1)
                pe.wait_ge(split.done.sem, 4)
                pe.wait_ge(mixed_split["r"].sem, mixed_split["r"].all(n))
                pe.wait_ge(gate_done.sem, gate_done.all(n - 1))
                for t in range(TT):
                    for c in range(CT):
                        r = split_product(pe, ps_r[:, t, :], [a[:, c, t * P:(t + 1) * P] for a in mixed_parts["r"]],
                                          [a[:, c, :] for a in w["r"]], c == 0, c == CT - 1)
                r.then_inc(r_ps.sem, 1)
                pe.wait_ge(split.done.sem, 6)
                pe.wait_ge(kk_split.sem, kk_split.all(n))
                pe.wait_ge(gated_done.sem, gated_done.all(n - 1))
                for t in range(TT):
                    for c in range(CT):
                        r = split_product(pe, ps_v[:, t, :], [a[:, c, t * P:(t + 1) * P] for a in kk_parts],
                                          [a[:, c, :] for a in w["v"]], c == 0, c == CT - 1)
                r.then_inc(v_ps.sem, 1)

            def step(n, par):
                back(n, par, True)

            over_batches(pe, lambda: ln.tensor_turn(pe, 0), step, lambda n, par: back(n, par, False))


def attention(nc, held, name, x_in, x_out, source, mask, weights, cross):
    with ExitStack() as ctx:
        def sb(tile, shape, dtype=F32):
            return ctx.enter_context(nc.sbuf_tensor(f"{name}_{tile}", shape, dtype))

        def parts(tile, shape):
            return [sb(f"{tile}_{part}", shape, F32R) for part in ("hi", "lo")]

        sem = counter(held, nc, name)
        HEADS = 4
        TURN, MIX = 2, 4

        wq, wk, wv, wo = (parts(f"w{f}", [P, CT, C]) for f in "qkvo")
        chunks = [(weights[f][:, c:c + 2, :], w[0][:, c:c + 2, :], w[1][:, c:c + 2, :], C)
                  for f, w in (("q", wq), ("k", wk), ("v", wv), ("o", wo)) for c in (0, 2)]
        vecs = sb("vecs", [P, 5, CT])
        ln_s, ln_b, b_q, b_k, b_v = (vecs[:, i, :] for i in range(5))
        bq_scaled = sb("bq_scaled", [P, CT])
        bo = sb("bo", [P, C])
        fixed = sb("fixed", [P, 3, P])
        ident = fixed[:, 0, :]
        half = sb("half", [P, TT])
        x = [sb(f"x{i}", [P, TT, C]) for i in range(2)]
        lnT = sb("lnT", [P, CT, L])
        lnT_parts = parts("lnT", [P, CT, L])
        src = sb("src", [P, CT, L]) if cross else lnT
        src_parts = parts("src", [P, CT, L]) if cross else lnT_parts
        qT, qT_parts = sb("qT", [P, CT, L]), parts("qT", [P, CT, L])
        kT, kT_parts = sb("kT", [P, CT, L]), parts("kT", [P, CT, L])
        v = [sb(f"v{i}", [P, TT, C]) for i in range(2)]
        masks = 2 if cross else 1
        mask_in = [sb(f"mask_in{i}", [P, TT, L]) for i in range(masks)]
        mask_neg = [sb(f"mask_neg{i}", [P, TT, L]) for i in range(masks)]
        mask_add = [sb(f"mask_add{i}", [P, TT, L]) for i in range(masks)]
        low = [sb(f"low{i}", [P, TT, L]) for i in range(2)]
        low_min = [sb(f"low_min{i}", [P, TT]) for i in range(HEADS)]
        prob = [sb(f"prob{i}", [P, TT, L]) for i in range(HEADS)]
        probT = [sb(f"probT{i}", [P, TT, L]) for i in range(HEADS)]
        row_sum = [sb(f"row_sum{i}", [P, TT, NH]) for i in range(2)]
        row_inv = sb("row_inv", [P, TT, NH])
        mixed = sb("mixed", [P, TT, C])
        mixedT = sb("mixedT", [P, CT, L])
        mixedT_parts = parts("mixedT", [P, CT, L])
        res = sb("res", [P, TT, C])
        ps_dense = ctx.enter_context(nc.psum_tensor(f"{name}_ps_dense", [P, CT, L], F32))
        ps_score = [ctx.enter_context(nc.psum_tensor(f"{name}_ps_score{i}", [P, TT, L], F32)) for i in range(2)]
        ps_turn = [ctx.enter_context(nc.psum_tensor(f"{name}_ps_turn{i}", [P, TT, L], F32)) for i in range(2)]
        ps_mixed = ctx.enter_context(nc.psum_tensor(f"{name}_ps_mixed", [P, TT, C], F32))
        dense_rows = ps_dense[:, :, :].rearrange("p (t a) l -> p t (a l)", t=TT)

        first_in = sem("first_in", 0)
        bo_in = sem("bo_in", 0)
        split = SplitWeights(ctx, nc, name, sem, chunks)
        passed = sem("passed", 0)
        consts_done = sem("consts_done", 0)
        x_loaded = sem("x_loaded", 16)
        src_loaded = sem("src_loaded", 16)
        mask_loaded = sem("mask_loaded", 16)
        x_stored = sem("x_stored", 16, 1)
        res_loaded = sem("res_loaded", 16)
        mask_flipped = sem("mask_flipped", 1, 1)
        mask_done = sem("mask_done", 1)
        biased = sem("biased", 1)
        ln_hi_done = sem("ln_hi_done", 2)
        ln_split = sem("ln_split", 2, 1)
        src_hi_done = sem("src_hi_done", 2)
        src_split = sem("src_split", 2, 1)
        mixedT_hi_done = sem("mixedT_hi_done", 2)
        mixedT_split = sem("mixedT_split", 2, 1)
        q_ps = sem("q_ps", 2)
        k_ps = sem("k_ps", 2)
        v_ps = sem("v_ps", 2, 1)
        q_out = sem("q_out", 2)
        k_out = sem("k_out", 2)
        q_hi_done = sem("q_hi_done", 2)
        k_hi_done = sem("k_hi_done", 2)
        q_split = sem("q_split", 2, 1)
        k_split = sem("k_split", 2, 1)
        v_out = sem("v_out", 2, 1)
        score_ps = sem("score_ps", NH, 2)
        masked = sem("masked", NH, 1)
        low_done = sem("low_done", NH, 2)
        prob_done = sem("prob_done", NH, 1)
        prob_ps = sem("prob_ps", NH, 1)
        probT_done = sem("probT_done", NH, 1)
        mixed_ps = sem("mixed_ps", NH, 2)
        inv_done = sem("inv_done", 1)
        mixed_done = sem("mixed_done", 1, 2)
        mixed_turned = sem("mixed_turned", 2, 1)
        mixedT_done = sem("mixedT_done", 2)
        out_ps = sem("out_ps", 2, 1)
        x_added = sem("x_added", 2, 2)

        ln = LayerNorm(ctx, nc, name, sem, x, x_loaded, ps_dense,
                       lambda eng, n, bank: eng.wait_ge(v_out.sem, v_out.at(n - 1, bank + 1)),
                       lambda c: lnT[:, c, :],
                       lambda eng, n: eng.wait_ge(ln_split.sem, ln_split.all(n - 1)),
                       ln_s, ln_b, ident, half, passed, parts=2)
        ln.normed_done.ahead = 2

        block = ctx.enter_context(nc.Block())

        @block.sync
        def _(sp):
            grant(sp, [x_stored])

            def load_mask(n, par):
                sp.dma_start(mask_in[par][:, :, :], mask[n, 0, :, :].rearrange("(t p) k -> p t k", p=P))\
                  .then_inc(mask_loaded.sem, 16)

            def load(n, par):
                sp.wait_ge(ln.stats_done.sem, ln.stats_done.all(n - 1))
                sp.sem_inc(passed.sem, 1)
                sp.wait_ge(ln.normed_done.sem, ln.normed_done.all(n - 2))
                sp.sem_inc(passed.sem, 1)
                sp.dma_start(x[par][:, :, :], x_in[n, :, :].rearrange("(t p) c -> p t c", p=P))\
                  .then_inc(x_loaded.sem, 16)
                if cross:
                    sp.wait_ge(src_split.sem, src_split.all(n - 1))
                    sp.sem_inc(passed.sem, 1)
                    sp.dma_start(src[:, :, :], source[n, :, :].rearrange("(c p) l -> p c l", p=P))\
                      .then_inc(src_loaded.sem, 16)
                    sp.wait_ge(mask_flipped.sem, mask_flipped.all(n - 1))
                    sp.sem_inc(passed.sem, 1)
                    sp.wait_ge(low_done.sem, low_done.all(n - 2))
                    sp.sem_inc(passed.sem, 1)
                    load_mask(n, par)

            def load_residual(n):
                sp.wait_ge(x_stored.sem, x_stored.all(n - 1))
                sp.sem_inc(passed.sem, 1)
                sp.dma_start(res[:, :, :], x_in[n, :, :].rearrange("(t p) c -> p t c", p=P))\
                  .then_inc(res_loaded.sem, 16)

            def store(n):
                sp.wait_ge(x_added.sem, x_added.all(n))
                sp.sem_inc(passed.sem, 1)
                sp.dma_start(x_out[n, :, :].rearrange("(t p) c -> p t c", p=P), res[:, :, :])\
                  .then_inc(x_stored.sem, 16)

            def start():
                sp.dma_start(x[0][:, :, :], x_in[0, :, :].rearrange("(t p) c -> p t c", p=P))\
                  .then_inc(x_loaded.sem, 16)
                for tile, w in [(fixed, "fixed"), (vecs, "vecs")]:
                    sp.dma_start(tile[:, :, :], weights[w]).then_inc(first_in.sem, 16)
                for i in range(2):
                    split.sync_load(sp, i)
                if cross:
                    sp.dma_start(src[:, :, :], source[0, :, :].rearrange("(c p) l -> p c l", p=P))\
                      .then_inc(src_loaded.sem, 16)
                    load_mask(0, 0)
                for i in range(2, 8):
                    split.sync_load(sp, i)
                sp.dma_start(bo[:, :], weights["bo"].unsqueeze(0).broadcast_to([P, C])).then_inc(bo_in.sem, 16)
                if not cross:
                    load_mask(0, 0)

            def step(n, par, prev_batch, next_batch):
                if prev_batch:
                    load_residual(n - 1)
                if next_batch:
                    load(n + 1, 1 - par)
                if prev_batch:
                    store(n - 1)

            def finish(n):
                load_residual(n)
                store(n)
                sp.wait_ge(x_stored.sem, x_stored.all(n))

            over_three_stages(sp, start, step, finish)

        @block.vector
        def _(dve):
            dve.memset(half[:, :], -0.5).then_inc(consts_done.sem, 1)
            grant(dve, [ln.stats_done, ln.normed_done, ln_split, src_split, mixedT_split, q_split, k_split, masked, low_done, mixed_done,
                        x_added])
            dve.wait_ge(first_in.sem, 16 * 2)
            dve.tensor_scalar(bq_scaled[:, :], b_q, HD ** -0.5, None, ALU.mult).then_inc(consts_done.sem, 1)

            def softmax_low(n, par, h):
                m = par if cross else 0
                dve.wait_ge(score_ps.sem, score_ps.at(n, h + 1))
                if h == 0:
                    if cross:
                        dve.wait_ge(mask_done.sem, mask_done.all(n))
                    else:
                        dve.wait_ge(mask_done.sem, 1)
                dve.wait_ge(prob_done.sem, prob_done.at(n, h - 1))
                low_h = low[h % 2]
                dve.tensor_tensor(low_h[:, :, :], ps_score[h % 2][:, :, :], mask_neg[m][:, :, :], ALU.mult)\
                   .then_inc(masked.sem, 1)
                dve.wait_ge(masked.sem, masked.at(n, h + 1))
                dve.sem_inc(passed.sem, 1)
                for t in range(TT):
                    r = dve.tensor_tensor_reduce(low_h[:, t, :], low_h[:, t, :], mask_add[m][:, t, :],
                                                 1.0, 3.0e38, ALU.add, ALU.min, low_min[h % HEADS][:, t:t + 1])
                r.then_inc(low_done.sem, 1)

            def split_tokens(n, whole, halves, hi_done, done, bank):
                c = slice(2 * bank, 2 * bank + 2)
                dve.tensor_copy(halves[0][:, c, :], whole[:, c, :]).then_inc(hi_done.sem, 1)
                dve.wait_ge(hi_done.sem, hi_done.at(n, bank + 1))
                dve.tensor_tensor(halves[1][:, c, :], whole[:, c, :], halves[0][:, c, :], ALU.subtract)\
                   .then_inc(done.sem, 1)

            def split_qk(n, bank):
                for whole, halves, out, hi_done, done in ((qT, qT_parts, q_out, q_hi_done, q_split),
                                                          (kT, kT_parts, k_out, k_hi_done, k_split)):
                    dve.wait_ge(out.sem, out.at(n, bank + 1))
                    dve.wait_ge(score_ps.sem, score_ps.at(n - 1, (bank + 1) * NH // 2))
                    split_tokens(n, whole, halves, hi_done, done, bank)

            def split_ln(n, bank):
                dve.wait_ge(ln.out_done.sem, ln.out_done.at(n, bank + 1))
                dve.wait_ge(v_ps.sem, v_ps.all(n - 1))
                split_tokens(n, lnT, lnT_parts, ln_hi_done, ln_split, bank)

            def split_src(n, bank):
                dve.wait_ge(src_loaded.sem, src_loaded.all(n))
                dve.wait_ge(v_ps.sem, v_ps.all(n - 1))
                split_tokens(n, src, src_parts, src_hi_done, src_split, bank)

            def split_mixed(n, bank):
                dve.wait_ge(mixedT_done.sem, mixedT_done.at(n, bank + 1))
                dve.wait_ge(out_ps.sem, out_ps.all(n - 1))
                split_tokens(n, mixedT, mixedT_parts, mixedT_hi_done, mixedT_split, bank)

            def invert_sums(n, par):
                dve.wait_ge(prob_done.sem, prob_done.all(n))
                dve.wait_ge(mixed_done.sem, mixed_done.all(n - 1))
                dve.reciprocal(row_inv[:, :, :], row_sum[par][:, :, :]).then_inc(inv_done.sem, 1)

            def normalise(n):
                dve.wait_ge(inv_done.sem, inv_done.all(n))
                dve.wait_ge(mixed_ps.sem, mixed_ps.all(n))
                dve.wait_ge(mixed_turned.sem, mixed_turned.all(n - 1))
                for t in range(TT):
                    r = dve.tensor_tensor(mixed[:, t, :].rearrange("p (h d) -> p h d", h=NH),
                                          ps_mixed[:, t, :].rearrange("p (h d) -> p h d", h=NH),
                                          row_inv[:, t, :].unsqueeze(2).broadcast_to([P, NH, HD]), ALU.mult)
                r.then_inc(mixed_done.sem, 1)

            def residual(n, t):
                dve.wait_ge(out_ps.sem, out_ps.at(n, t + 1))
                dve.wait_ge(biased.sem, biased.all(n))
                dve.tensor_tensor(res[:, t, :], res[:, t, :], dense_rows[:, t, :], ALU.add).then_inc(x_added.sem, 1)

            def start():
                ln.vector_moments(dve, 0, 0)
                ln.vector_normalise(dve, 0, 0)
                for i in range(2):
                    split.vector_lo(dve, i)
                for bank in range(2):
                    split_ln(0, bank)
                for i in range(2, 4):
                    split.vector_lo(dve, i)
                if cross:
                    for bank in range(2):
                        split_src(0, bank)
                for i in range(4, 8):
                    split.vector_lo(dve, i)
                split_qk(0, 0)

            def step(n, par, prev_batch, next_batch):
                for h in range(NH):
                    if prev_batch:
                        if h == 2:
                            invert_sums(n - 1, 1 - par)
                        if h == 4:
                            normalise(n - 1)
                        if h in (7, 8):
                            split_mixed(n - 1, h - 7)
                        if h in (10, 11):
                            residual(n - 1, h - 10)
                    if next_batch:
                        if h == 0:
                            ln.vector_moments(dve, n + 1, 1 - par)
                        if h == 1:
                            ln.vector_normalise(dve, n + 1, 1 - par)
                        if h in (6, 9):
                            split_ln(n + 1, (h - 6) // 3)
                        if cross and h in (11, 12):
                            split_src(n + 1, h - 11)
                        if h == 15:
                            split_qk(n + 1, 0)
                    if h == 2:
                        split_qk(n, 1)
                    softmax_low(n, par, h)

            def finish(n):
                invert_sums(n, n % 2)
                normalise(n)
                for bank in range(2):
                    split_mixed(n, bank)
                for t in range(TT):
                    residual(n, t)

            over_three_stages(dve, start, step, finish)

        @block.gpsimd
        def _(pool):
            grant(pool, [mask_flipped])
            pool.wait_ge(consts_done.sem, 1)

            def masks_of(n, par):
                if cross:
                    pool.wait_ge(low_done.sem, low_done.all(n - 2))
                    pool.sem_inc(passed.sem, 1)
                pool.wait_ge(mask_loaded.sem, mask_loaded.all(n))
                pool.sem_inc(passed.sem, 1)
                pool.tensor_scalar(mask_neg[par][:, :, :], mask_in[par][:, :, :], -1.0, None, ALU.mult)
                pool.tensor_scalar(mask_add[par][:, :, :], mask_in[par][:, :, :], -1.0, 1.0, ALU.mult, ALU.add)\
                    .then_inc(mask_flipped.sem, 1)
                pool.wait_ge(mask_flipped.sem, mask_flipped.all(n))
                pool.sem_inc(passed.sem, 1)
                pool.tensor_scalar(mask_add[par][:, :, :], mask_add[par][:, :, :], 10000.0, None, ALU.mult)\
                    .then_inc(mask_done.sem, 1)

            def add_bias(n):
                pool.wait_ge(res_loaded.sem, res_loaded.all(n))
                pool.wait_ge(bo_in.sem, 16)
                pool.tensor_tensor(res[:, :, :], res[:, :, :],
                                   bo[:, :].unsqueeze(1).broadcast_to([P, TT, C]), ALU.add).then_inc(biased.sem, 1)

            def start():
                ln.gpsimd_rstd(pool, 0)
                masks_of(0, 0)

            def step(n, par, prev_batch, next_batch):
                if prev_batch:
                    add_bias(n - 1)
                if next_batch:
                    ln.gpsimd_rstd(pool, n + 1)
                    if cross:
                        masks_of(n + 1, 1 - par)

            over_three_stages(pool, start, step, add_bias)

        @block.scalar
        def _(act):
            grant(act, [prob_done, probT_done, v_out])
            act.wait_ge(consts_done.sem, 2)

            def q_copy(n, bank):
                act.wait_ge(q_ps.sem, q_ps.at(n, bank + 1))
                act.wait_ge(q_split.sem, q_split.at(n - 1, bank + 1))
                for c in (2 * bank, 2 * bank + 1):
                    r = act.activation(qT[:, c, :], ps_dense[:, c, :], ACT.Identity,
                                       bias=bq_scaled[:, c:c + 1], scale=HD ** -0.5)
                r.then_inc(q_out.sem, 1)

            def k_copy(n, bank):
                act.wait_ge(k_ps.sem, k_ps.at(n, bank + 1))
                act.wait_ge(k_split.sem, k_split.at(n - 1, bank + 1))
                for c in (2 * bank, 2 * bank + 1):
                    r = act.activation(kT[:, c, :], ps_dense[:, c, :], ACT.Identity, bias=b_k[:, c:c + 1])
                r.then_inc(k_out.sem, 1)

            def v_copy(n, par, t):
                act.wait_ge(v_ps.sem, v_ps.at(n, t + 1))
                act.wait_ge(mixed_ps.sem, mixed_ps.all(n - 2))
                act.activation(v[par][:, t, :], dense_rows[:, t, :], ACT.Copy).then_inc(v_out.sem, 1)

            def exps(n, par, h):
                act.wait_ge(low_done.sem, low_done.at(n, h + 1))
                act.wait_ge(prob_ps.sem, prob_ps.at(n, h + 1 - HEADS))
                if h == 0:
                    act.wait_ge(mixed_done.sem, mixed_done.all(n - 2))
                for t in range(TT):
                    r = act.activation(prob[h % HEADS][:, t, :], low[h % 2][:, t, :], ACT.Exp,
                                       bias=low_min[h % HEADS][:, t:t + 1], scale=-1.0,
                                       accum_out=row_sum[par][:, t, h:h + 1])
                r.then_inc(prob_done.sem, 1)

            def prob_copy(n, h):
                act.wait_ge(prob_ps.sem, prob_ps.at(n, h + 1))
                act.wait_ge(mixed_ps.sem, mixed_ps.at(n, h + 1 - HEADS))
                act.activation(probT[h % HEADS][:, :, :], ps_turn[h % 2][:, :, :], ACT.Copy)\
                   .then_inc(probT_done.sem, 1)

            def mixed_copy(n, bank):
                act.wait_ge(mixed_turned.sem, mixed_turned.at(n, bank + 1))
                act.wait_ge(mixedT_split.sem, mixedT_split.all(n - 1))
                for c in (2 * bank, 2 * bank + 1):
                    r = act.activation(mixedT[:, c, :], ps_dense[:, c, :], ACT.Identity, bias=b_v[:, c:c + 1])
                r.then_inc(mixedT_done.sem, 1)

            def start():
                for i in range(2):
                    split.scalar_hi(act, i)
                for bank in range(2):
                    ln.scalar_out(act, 0, bank)
                for i in range(2, 4):
                    split.scalar_hi(act, i)
                for bank in range(2):
                    q_copy(0, bank)
                for i in range(4, 8):
                    split.scalar_hi(act, i)
                for bank in range(2):
                    k_copy(0, bank)

            def step(n, par, prev_batch, next_batch):
                for h in range(NH):
                    if h in (1, 3):
                        v_copy(n, par, h // 2)
                    if next_batch:
                        if h in (4, 5):
                            ln.scalar_out(act, n + 1, h - 4)
                        if h in (12, 13):
                            q_copy(n + 1, h - 12)
                        if h in (14, 15):
                            k_copy(n + 1, h - 14)
                    if prev_batch and h in (6, 7):
                        mixed_copy(n - 1, h - 6)
                    exps(n, par, h)
                    if h >= TURN:
                        prob_copy(n, h - TURN)
                    elif prev_batch:
                        prob_copy(n - 1, h - TURN + NH)

            def finish(n):
                for h in range(NH - TURN, NH):
                    prob_copy(n, h)
                for bank in range(2):
                    mixed_copy(n, bank)

            over_three_stages(act, start, step, finish)

        @block.tensor
        def _(pe):
            grant(pe, [ln.turned_done, v_ps, score_ps, prob_ps, mixed_ps, mixed_turned, out_ps])
            pe.wait_ge(first_in.sem, 16 * 2)

            def q_part(n, m):
                if m == 0:
                    pe.wait_ge(ln_split.sem, ln_split.all(n))
                if m % 2 == 0:
                    pe.wait_ge(x_added.sem, x_added.at(n - 2, m // 2 + 1))
                for c in range(CT):
                    r = split_product(pe, ps_dense[:, m, :], [w[:, c, m * P:(m + 1) * P] for w in wq],
                                      [a[:, c, :] for a in lnT_parts], c == 0, c == CT - 1)
                if m % 2 == 1:
                    r.then_inc(q_ps.sem, 1)

            def k_part(n, m):
                if m % 2 == 0:
                    pe.wait_ge(q_out.sem, q_out.at(n, m // 2 + 1))
                if cross and m == 0:
                    pe.wait_ge(src_split.sem, src_split.all(n))
                for c in range(CT):
                    r = split_product(pe, ps_dense[:, m, :], [w[:, c, m * P:(m + 1) * P] for w in wk],
                                      [a[:, c, :] for a in src_parts], c == 0, c == CT - 1)
                if m % 2 == 1:
                    r.then_inc(k_ps.sem, 1)

            def v_part(n, m):
                t, half_of_c = m // 2, m % 2
                if half_of_c == 0:
                    pe.wait_ge(k_out.sem, k_out.at(n, t + 1))
                for c in range(2 * half_of_c, 2 * half_of_c + 2):
                    r = split_product(pe, dense_rows[:, t, :], [a[:, c, t * P:(t + 1) * P] for a in src_parts],
                                      [w[:, c, :] for w in wv], c == 0, c == CT - 1)
                if half_of_c == 1:
                    r.then_inc(v_ps.sem, 1)

            def score(n, h):
                c, row = h // HC, (h % HC) * HD
                if h in (0, NH // 2):
                    pe.wait_ge(q_split.sem, q_split.at(n, h // (NH // 2) + 1))
                    pe.wait_ge(k_split.sem, k_split.at(n, h // (NH // 2) + 1))
                pe.wait_ge(masked.sem, masked.at(n, h - 1))
                for t in range(TT):
                    r = split_product(pe, ps_score[h % 2][:, t, :],
                                      [a[row:row + HD, c, t * P:(t + 1) * P] for a in qT_parts],
                                      [a[row:row + HD, c, :] for a in kT_parts], True, True)
                r.then_inc(score_ps.sem, 1)

            def turn(n, h):
                pe.wait_ge(prob_done.sem, prob_done.at(n, h + 1))
                pe.wait_ge(probT_done.sem, probT_done.at(n, h - 1))
                for k in range(TT):
                    for t in range(TT):
                        r = pe.transpose(ps_turn[h % 2][:, k, t * P:(t + 1) * P],
                                         prob[h % HEADS][:, t, k * P:(k + 1) * P], ident)
                r.then_inc(prob_ps.sem, 1)

            def mix(n, par, h):
                pe.wait_ge(probT_done.sem, probT_done.at(n, h + 1))
                if h == 0:
                    pe.wait_ge(v_out.sem, v_out.all(n))
                    pe.wait_ge(mixed_done.sem, mixed_done.all(n - 1))
                for t in range(TT):
                    for k in range(TT):
                        r = pe.matmul(ps_mixed[:, t, h * HD:(h + 1) * HD], probT[h % HEADS][:, k, t * P:(t + 1) * P],
                                      v[par][:, k, h * HD:(h + 1) * HD], start=k == 0, stop=k == TT - 1)
                r.then_inc(mixed_ps.sem, 1)

            def turn_mixed(n, bank, later):
                pe.wait_ge(mixed_done.sem, mixed_done.all(n))
                if later == 2:
                    pe.wait_ge(ln.out_done.sem, ln.out_done.at(n + 2, bank + 1))
                else:
                    pe.wait_ge(v_out.sem, v_out.at(n + later, bank + 1))
                for t in range(TT):
                    for c in (2 * bank, 2 * bank + 1):
                        r = pe.transpose(ps_dense[:, c, t * P:(t + 1) * P], mixed[:, t, c * P:(c + 1) * P], ident)
                r.then_inc(mixed_turned.sem, 1)

            def output(n, m):
                t, half_of_c = m // 2, m % 2
                pe.wait_ge(mixedT_split.sem, mixedT_split.at(n, max(t, half_of_c) + 1))
                for c in range(2 * half_of_c, 2 * half_of_c + 2):
                    r = split_product(pe, dense_rows[:, t, :], [a[:, c, t * P:(t + 1) * P] for a in mixedT_parts],
                                      [w[:, c, :] for w in wo], c == 0, c == CT - 1)
                if half_of_c == 1:
                    r.then_inc(out_ps.sem, 1)

            def start():
                for bank in range(2):
                    ln.tensor_turn(pe, 0, bank)
                pe.wait_ge(split.done.sem, 2)
                for m in range(4):
                    q_part(0, m)
                pe.wait_ge(split.done.sem, 4)
                for m in range(4):
                    k_part(0, m)
                pe.wait_ge(split.done.sem, 6)
                v_part(0, 0)
                pe.wait_ge(split.done.sem, 8)

            def step(n, par, prev_batch, next_batch):
                for h in range(NH):
                    score(n, h)
                    if h in (0, 1, 2):
                        v_part(n, h + 1)
                    if prev_batch:
                        if h in (5, 6):
                            turn_mixed(n - 1, h - 5, 2 if next_batch else 1)
                        if h == 8:
                            output(n - 1, 0)
                        if h == 9:
                            output(n - 1, 1)
                            output(n - 1, 2)
                        if h == 10:
                            output(n - 1, 3)
                    if next_batch:
                        if h in (3, 4):
                            ln.tensor_turn(pe, n + 1, h - 3)
                        if h in (11, 12):
                            q_part(n + 1, 2 * (h - 11))
                            q_part(n + 1, 2 * (h - 11) + 1)
                        if h in (13, 14):
                            k_part(n + 1, 2 * (h - 13))
                            k_part(n + 1, 2 * (h - 13) + 1)
                        if h == 15:
                            v_part(n + 1, 0)
                    if h >= TURN:
                        turn(n, h - TURN)
                    elif prev_batch:
                        turn(n - 1, h - TURN + NH)
                    if h >= MIX:
                        mix(n, par, h - MIX)
                    elif prev_batch:
                        mix(n - 1, 1 - par, h - MIX + NH)

            def finish(n):
                for h in range(NH - TURN, NH):
                    turn(n, h)
                for h in range(NH - MIX, NH):
                    mix(n, n % 2, h)
                for bank in range(2):
                    turn_mixed(n, bank, 0)
                for m in range(4):
                    output(n, m)

            over_three_stages(pe, start, step, finish)


def mlp(nc, held, x_in, x_out, weights):
    GROUPS = FF // C
    CHUNKS = 2 * GROUPS
    with ExitStack() as ctx:
        def sb(name, shape, dtype=F32):
            return ctx.enter_context(nc.sbuf_tensor(f"ff_{name}", shape, dtype))

        sem = counter(held, nc, "ff")

        w1 = [sb(f"w1_{part}", [P, CT, FF], F32R) for part in ("hi", "lo")]
        w2 = [sb(f"w2_{part}", [P, FF // P, C], F32R) for part in ("hi", "lo")]
        chunks = [(weights["w1"][:, :, i * L:(i + 1) * L], w1[0][:, :, i * L:(i + 1) * L], w1[1][:, :, i * L:(i + 1) * L], L)
                  for i in range(CHUNKS)]
        chunks += [(weights["w2"][:, k:k + 2, :], w2[0][:, k:k + 2, :], w2[1][:, k:k + 2, :], C)
                   for k in range(0, FF // P, 2)]
        vecs = sb("vecs", [P, 2, CT])
        b1 = sb("b1", [P, FF // P])
        b2 = sb("b2", [P, C])
        fixed = sb("fixed", [P, 3, P])
        half = sb("half", [P, TT])
        x = [sb(f"x{i}", [P, TT, C]) for i in range(2)]
        lnT = sb("lnT", [P, CT, L])
        lnT_parts = [sb(f"lnT_{part}", [P, CT, L], F32R) for part in ("hi", "lo")]
        pre = [sb(f"pre{i}", [P, CT, L]) for i in range(2)]
        gel = [sb(f"gel{i}", [P, CT, L]) for i in range(2)]
        hid = [[sb(f"hid_{part}{i}", [P, CT, L], F32R) for i in range(2)] for part in ("hi", "lo")]
        ps_turn = ctx.enter_context(nc.psum_tensor("ff_ps_turn", [P, CT, L], F32))
        ps_hid = [ctx.enter_context(nc.psum_tensor(f"ff_ps_hid{i}", [P, CT, L], F32)) for i in range(2)]
        ps_out = ctx.enter_context(nc.psum_tensor("ff_ps_out", [P, TT, C], F32))

        first_in = sem("first_in", 0)
        b2_in = sem("b2_in", 0)
        split = SplitWeights(ctx, nc, "ff", sem, chunks)
        passed = sem("passed", 0)
        consts_done = sem("consts_done", 0)
        x_loaded = sem("x_loaded", 16)
        x_stored = sem("x_stored", 16, 2)
        biased = sem("biased", 1)
        ln_hi_done = sem("ln_hi_done", 1)
        ln_done = sem("ln_done", 1)
        hid_ps = sem("hid_ps", GROUPS, 1)
        pre_done = sem("pre_done", GROUPS, 1)
        sq_done = sem("sq_done", GROUPS)
        poly_done = sem("poly_done", GROUPS)
        cube_done = sem("cube_done", GROUPS)
        tanh_done = sem("tanh_done", GROUPS)
        gelu_done = sem("gelu_done", GROUPS, 1)
        hid_hi_done = sem("hid_hi_done", GROUPS)
        hid_done = sem("hid_done", GROUPS, 1)
        out_ps = sem("out_ps", GROUPS, 1)
        x_added = sem("x_added", 1, 1)

        ln = LayerNorm(ctx, nc, "ff", sem, x, x_loaded, ps_turn,
                       lambda eng, n, _: eng.wait_ge(ln_out().sem, ln_out().all(n - 1)),
                       lambda c: lnT[:, c, :],
                       lambda eng, n: eng.wait_ge(ln_done.sem, ln_done.all(n - 1)),
                       vecs[:, 0, :], vecs[:, 1, :], fixed[:, 0, :], half, passed)
        ln.out_done.ahead = 1
        ln_done.ahead = 1

        def ln_out():
            return ln.out_done

        block = ctx.enter_context(nc.Block())

        @block.sync
        def _(sp):
            grant(sp, [x_stored])

            def load(n, par):
                sp.wait_ge(ln.stats_done.sem, ln.stats_done.all(n - 1))
                sp.sem_inc(passed.sem, 1)
                sp.wait_ge(x_stored.sem, x_stored.all(n - 2))
                sp.sem_inc(passed.sem, 1)
                sp.dma_start(x[par][:, :, :], x_in[n, :, :].rearrange("(t p) c -> p t c", p=P))\
                  .then_inc(x_loaded.sem, 16)

            def store(n, par):
                sp.wait_ge(x_added.sem, x_added.all(n))
                sp.sem_inc(passed.sem, 1)
                sp.dma_start(x_out[n, :, :].rearrange("(t p) c -> p t c", p=P), x[par][:, :, :])\
                  .then_inc(x_stored.sem, 16)

            def first():
                sp.dma_start(x[0][:, :, :], x_in[0, :, :].rearrange("(t p) c -> p t c", p=P))\
                  .then_inc(x_loaded.sem, 16)
                for tile, w in [(fixed, "fixed"), (vecs, "vecs")]:
                    sp.dma_start(tile[:, :, :], weights[w]).then_inc(first_in.sem, 16)
                sp.dma_start(b1[:, :], weights["b1"]).then_inc(first_in.sem, 16)
                for i in range(2 * CHUNKS):
                    split.sync_load(sp, i)
                    if i == 1:
                        sp.dma_start(b2[:, :], weights["b2"].unsqueeze(0).broadcast_to([P, C])).then_inc(b2_in.sem, 16)

            def step(n, par):
                load(n + 1, 1 - par)
                store(n, par)

            def last(n, par):
                store(n, par)
                sp.wait_ge(x_stored.sem, x_stored.all(n))

            over_batches(sp, first, step, last)

        @block.vector
        def _(dve):
            dve.memset(half[:, :], -0.5).then_inc(consts_done.sem, 1)
            grant(dve, [ln.stats_done, ln_done, gelu_done, hid_done, x_added])
            dve.wait_ge(first_in.sem, 16 * 3)

            def norm(n, par):
                ln.vector_moments(dve, n, par)
                ln.vector_normalise(dve, n, par)

            def ln_lo(n):
                dve.wait_ge(ln_hi_done.sem, ln_hi_done.all(n))
                dve.wait_ge(hid_ps.sem, hid_ps.all(n - 1))
                dve.tensor_tensor(lnT_parts[1][:, :, :], lnT[:, :, :], lnT_parts[0][:, :, :], ALU.subtract)\
                   .then_inc(ln_done.sem, 1)

            def square(n, g):
                u, poly = pre[g % 2][:, :, :], gel[g % 2][:, :, :]
                dve.wait_ge(pre_done.sem, pre_done.at(n, g + 1))
                dve.wait_ge(hid_done.sem, hid_done.at(n, g - 1))
                dve.tensor_tensor(poly, u, u, ALU.mult).then_inc(sq_done.sem, 1)
                dve.wait_ge(sq_done.sem, sq_done.at(n, g + 1))
                dve.tensor_scalar(poly, poly, 0.044715, 1.0, ALU.mult, ALU.add).then_inc(poly_done.sem, 1)

            def gelu(n, g):
                tanh, u = gel[g % 2][:, :, :], pre[g % 2][:, :, :]
                dve.wait_ge(tanh_done.sem, tanh_done.at(n, g + 1))
                dve.wait_ge(out_ps.sem, out_ps.at(n, g - 1))
                dve.scalar_tensor_tensor(hid[0][g % 2][:, :, :], tanh, 1.0, u, ALU.add, ALU.mult)\
                   .then_inc(hid_hi_done.sem, 1)
                dve.wait_ge(hid_hi_done.sem, hid_hi_done.at(n, g + 1))
                dve.scalar_tensor_tensor(tanh, tanh, 1.0, u, ALU.add, ALU.mult).then_inc(gelu_done.sem, 1)
                dve.wait_ge(gelu_done.sem, gelu_done.at(n, g + 1))
                dve.tensor_tensor(hid[1][g % 2][:, :, :], gel[g % 2][:, :, :], hid[0][g % 2][:, :, :], ALU.subtract)\
                   .then_inc(hid_done.sem, 1)

            def back(n, par):
                dve.wait_ge(out_ps.sem, out_ps.all(n))
                dve.wait_ge(biased.sem, biased.all(n))
                dve.scalar_tensor_tensor(x[par][:, :, :], ps_out[:, :, :], 0.5, x[par][:, :, :], ALU.mult, ALU.add)\
                   .then_inc(x_added.sem, 1)

            def first():
                norm(0, 0)
                for i in range(2):
                    split.vector_lo(dve, i)
                ln_lo(0)
                for i in range(2, CHUNKS):
                    split.vector_lo(dve, i)
                square(0, 0)
                for i in range(CHUNKS, 2 * CHUNKS):
                    split.vector_lo(dve, i)

            def step(n, par):
                gelu(n, 0)
                square(n, 1)
                gelu(n, 1)
                square(n, 2)
                norm(n + 1, 1 - par)
                gelu(n, 2)
                square(n, 3)
                ln_lo(n + 1)
                gelu(n, 3)
                square(n + 1, 0)
                back(n, par)

            def last(n, par):
                for g in range(1, GROUPS):
                    gelu(n, g - 1)
                    square(n, g)
                gelu(n, GROUPS - 1)
                back(n, par)

            over_batches(dve, first, step, last)

        @block.gpsimd
        def _(pool):
            pool.wait_ge(consts_done.sem, 1)

            def cube(n, g):
                pool.wait_ge(poly_done.sem, poly_done.at(n, g + 1))
                pool.tensor_tensor(gel[g % 2][:, :, :], gel[g % 2][:, :, :], pre[g % 2][:, :, :], ALU.mult)\
                    .then_inc(cube_done.sem, 1)

            def front(n, par):
                ln.gpsimd_rstd(pool, n)
                pool.wait_ge(ln.normed_done.sem, ln.normed_done.all(n))
                pool.wait_ge(b2_in.sem, 16)
                pool.tensor_tensor(x[par][:, :, :], x[par][:, :, :],
                                   b2[:, :].unsqueeze(1).broadcast_to([P, TT, C]), ALU.add).then_inc(biased.sem, 1)

            def first():
                front(0, 0)
                cube(0, 0)

            def step(n, par):
                cube(n, 1)
                cube(n, 2)
                front(n + 1, 1 - par)
                cube(n, 3)
                cube(n + 1, 0)

            def last(n, par):
                for g in range(1, GROUPS):
                    cube(n, g)

            over_batches(pool, first, step, last)

        @block.scalar
        def _(act):
            grant(act, [ln.out_done, pre_done])
            act.wait_ge(first_in.sem, 16 * 3)

            def ln_hi(n):
                ln.scalar_out(act, n)
                act.wait_ge(ln.out_done.sem, ln.out_done.all(n))
                act.wait_ge(hid_ps.sem, hid_ps.all(n - 1))
                act.activation(lnT_parts[0][:, :, :], lnT[:, :, :], ACT.Copy).then_inc(ln_hi_done.sem, 1)

            def pre_copy(n, g):
                act.wait_ge(hid_ps.sem, hid_ps.at(n, g + 1))
                act.wait_ge(gelu_done.sem, gelu_done.at(n, g - 1))
                for c in range(CT):
                    r = act.activation(pre[g % 2][:, c, :], ps_hid[g % 2][:, c, :], ACT.Identity,
                                       bias=b1[:, g * CT + c:g * CT + c + 1])
                r.then_inc(pre_done.sem, 1)

            def tanhs(n, g):
                act.wait_ge(cube_done.sem, cube_done.at(n, g + 1))
                act.activation(gel[g % 2][:, :, :], gel[g % 2][:, :, :], ACT.Tanh, scale=0.7978845608028654)\
                   .then_inc(tanh_done.sem, 1)

            def first():
                for i in range(2):
                    split.scalar_hi(act, i)
                ln_hi(0)
                for i in range(2, CHUNKS):
                    split.scalar_hi(act, i)
                pre_copy(0, 0)
                for i in range(CHUNKS, 2 * CHUNKS):
                    split.scalar_hi(act, i)

            def step(n, par):
                for g in range(1, GROUPS):
                    tanhs(n, g - 1)
                    pre_copy(n, g)
                ln_hi(n + 1)
                tanhs(n, GROUPS - 1)
                pre_copy(n + 1, 0)

            def last(n, par):
                for g in range(1, GROUPS):
                    tanhs(n, g - 1)
                    pre_copy(n, g)
                tanhs(n, GROUPS - 1)

            over_batches(act, first, step, last)

        @block.tensor
        def _(pe):
            grant(pe, [ln.turned_done, hid_ps, out_ps])
            pe.wait_ge(first_in.sem, 16 * 3)

            def hidden(n, g):
                if g == 0:
                    pe.wait_ge(ln_done.sem, ln_done.all(n))
                pe.wait_ge(pre_done.sem, pre_done.at(n, g - 1))
                for m in range(CT):
                    cols = slice((g * CT + m) * P, (g * CT + m + 1) * P)
                    for c in range(CT):
                        r = split_product(pe, ps_hid[g % 2][:, m, :], [w[:, c, cols] for w in w1],
                                          [a[:, c, :] for a in lnT_parts], c == 0, c == CT - 1)
                r.then_inc(hid_ps.sem, 1)

            def output(n, g):
                if g == 0:
                    pe.wait_ge(x_added.sem, x_added.all(n - 1))
                pe.wait_ge(hid_done.sem, hid_done.at(n, g + 1))
                for k in range(CT):
                    for t in range(TT):
                        r = split_product(pe, ps_out[:, t, :], [a[g % 2][:, k, t * P:(t + 1) * P] for a in hid],
                                          [w[:, g * CT + k, :] for w in w2], g == 0 and k == 0,
                                          g == GROUPS - 1 and k == CT - 1)
                r.then_inc(out_ps.sem, 1)

            def middle(n):
                hidden(n, 1)
                hidden(n, 2)
                pe.wait_ge(split.done.sem, 2 * CHUNKS)
                output(n, 0)
                hidden(n, 3)
                output(n, 1)

            def first():
                ln.tensor_turn(pe, 0)
                pe.wait_ge(split.done.sem, 2)
                hidden(0, 0)
                pe.wait_ge(split.done.sem, CHUNKS)

            def step(n, par):
                middle(n)
                ln.tensor_turn(pe, n + 1)
                output(n, 2)
                hidden(n + 1, 0)
                output(n, 3)

            def last(n, par):
                middle(n)
                output(n, 2)
                output(n, 3)

            over_batches(pe, first, step, last)


def build(nc, ins, out, scratch):
    held = []
    xs, v_rows = scratch
    ctx_rows = ins["ctx"]
    first_state = ctx_rows[:, 2:2 + S, :].rearrange("b s c -> b (s c)").rearrange("b (p s) -> b p s", s=S)
    time_mix(nc, held, ins["x"], xs[0], first_state, v_rows, ins)
    end_phase(nc, held)
    channel_mix(nc, held, xs[0], xs[1], ins)
    end_phase(nc, held)
    attention(nc, held, "sa", xs[1], xs[2], None, ins["mask_1x1xSxS2_fc1"],
              {"vecs": ins["sa_vecs"], "fixed": ins["fixed"], "q": ins["sa_q"], "k": ins["sa_k"], "v": ins["sa_v"],
               "o": ins["sa_o"], "bo": ins["b_ao"]}, False)
    end_phase(nc, held)
    attention(nc, held, "ca", xs[2], xs[3], ins["ctxT"], ins["mask_Bx1xSxS2_ff1"],
              {"vecs": ins["ca_vecs"], "fixed": ins["fixed"], "q": ins["ca_q"], "k": ins["ca_k"], "v": ins["ca_v"],
               "o": ins["ca_o"], "bo": ins["b_co"]}, True)
    end_phase(nc, held)
    mlp(nc, held, xs[3], out, {"vecs": ins["ff_vecs"], "fixed": ins["fixed"], "w1": ins["w1"], "w2": ins["w2"],
                         "b1": ins["b1"], "b2": ins["b2"]})


def fixed_matrices():
    import numpy as np
    k = np.arange(P)
    same_head = (k[:, None] // S == k[None, :] // S).astype(np.float32)
    eye = np.eye(P, dtype=np.float32)
    centre = eye - same_head / S
    fixed = np.stack([eye, same_head, centre], axis=1)
    pick = np.stack([same_head * ((k[None, :] % S == s) - 1.0 / S) for s in range(S)], axis=1).astype(np.float32)
    head_sum = np.zeros((P, CT, C // S), np.float32)
    for c in range(CT):
        head_sum[k, c, c * HT + k // S] = 1.0 / S
    head_out = np.ascontiguousarray((head_sum > 0).astype(np.float32).transpose(2, 1, 0))
    return {"fixed": fixed, "pick": pick, "head_sum": head_sum, "head_out": head_out}


def layouts(inputs):
    import numpy as np
    a = {k: np.asarray(v) for k, v in inputs.items()}

    def rows(w):
        return np.ascontiguousarray(w.reshape(-1, P, w.shape[1]).transpose(1, 0, 2))

    def columns(*vs):
        return np.ascontiguousarray(np.stack([v.reshape(-1, P).T for v in vs], axis=1))

    t, u = "L0_xattn_", "L1_xattn_"
    out = {"x": a["x"], "ctx": a["ctx_2048"], "ctxT": np.ascontiguousarray(a["ctx_2048"].transpose(0, 2, 1)),
           "mask_1x1xSxS2_fc1": a["mask_1x1xSxS2_fc1"], "mask_Bx1xSxS2_ff1": a["mask_Bx1xSxS2_ff1"]}
    for w in ("Wr", "Wk", "Wv", "Wg", "Wo", "fWk", "fWr", "fWv"):
        out[w] = rows(a[t + w].T)
    for i in range(2):
        out[f"prev{i}"] = np.ascontiguousarray(a["ctx_2048"][:, i].reshape(B, CT, P).transpose(2, 0, 1))
    out["maa_w1"], out["decay_w1"] = rows(a[t + "maa_w1"]), rows(a[t + "decay_w1"])
    out["maa_w2"] = np.ascontiguousarray(a[t + "maa_w2"].reshape(5 * DM, C))
    out["decay_w2"] = a[t + "decay_w2"]
    out["time_vecs"] = columns(*[a[t + v].reshape(C) for v in TIME_VECS])
    out["chan_vecs"] = columns(*[a[t + v] for v in CHAN_VECS])
    for p, w, b, ln in (("sa", a[u + "w_qkv"], a[u + "b_qkv"], "ln1"),
                        ("ca", np.concatenate([a[u + "w_q"], a[u + "w_kv"]], axis=1),
                         np.concatenate([a[u + "b_q"], a[u + "b_kv"]]), "ln2")):
        for i, f in enumerate("qkv"):
            out[f"{p}_{f}"] = rows(w[:, i * C:(i + 1) * C])
        out[f"{p}_vecs"] = columns(a[f"{u}{ln}_s"], a[f"{u}{ln}_b"], *[b[i * C:(i + 1) * C] for i in range(3)])
    out["sa_o"], out["ca_o"] = rows(a[u + "w_ao"]), rows(a[u + "w_co"])
    out["b_ao"], out["b_co"] = a[u + "b_ao"], a[u + "b_co"]
    out["ff_vecs"] = columns(a[u + "ln3_s"], a[u + "ln3_b"])
    out["w1"], out["w2"] = rows(a[u + "w1"]), rows(a[u + "w2"])
    out["b1"] = np.ascontiguousarray(a[u + "b1"].reshape(-1, P).T)
    out["b2"] = a[u + "b2"]
    out.update(fixed_matrices())
    return out


def kernel(**inputs):
    import numpy as np
    import concourse.bacc as bacc
    from concourse.bass_utils import run_bass_kernel_spmd as run

    nc = bacc.Bacc("TRN2", target_bir_lowering=False, num_devices=1)
    arrays, ins = {}, {}
    for name, a in layouts(inputs).items():
        arrays[f"in_{name}"] = a
        ins[name] = nc.dram_tensor(f"in_{name}", a.shape, mybir.dt.from_np(a.dtype), kind="ExternalInput").ap()
    out = nc.dram_tensor("out_0", (B, L, C), F32, kind="ExternalOutput").ap()
    xs = [nc.dram_tensor(f"x_stage{i}", (B, L, C), F32, kind="Internal").ap() for i in range(4)]
    v_rows = [nc.dram_tensor(f"v_rows{i}", (C, L), F32, kind="Internal").ap() for i in range(2)]
    build(nc, ins, out, (xs, v_rows))
    r = run(nc, [arrays], core_ids=[0])
    return r.results[0]["out_0"]
```
